# Optimizing a Trainium2 kernel written in Bass

```python
import numpy as np
import jax
import jax.numpy as jnp

def _softmax(x, axis=-1):
    return jax.nn.softmax(x, axis=axis)

def _gelu(x):
    return jax.nn.gelu(x, approximate=True)

def _silu(x):
    return jax.nn.silu(x)

def _sigmoid(x):
    return jax.nn.sigmoid(x)

def _layernorm(x, axis=-1, eps=1e-05):
    m = jnp.mean(x, axis=axis, keepdims=True)
    v = jnp.var(x, axis=axis, keepdims=True)
    return (x - m) / jnp.sqrt(v + eps)

def _scatter_add(tgt, idx, src, axis=0):
    return tgt.at[idx].add(src)

def _segment_sum(src, seg, n):
    return jax.ops.segment_sum(src, seg, n)
kernel_name = 'mk_seq_postln_d2_jaxref_r8_c44c4c'

def setup_inputs(seed: int=0):
    np.random.seed(seed)
    _w = jnp.asarray

    def _L0_attn_setup():
        import jax, jax.numpy as jnp
        import numpy as np
        import math
        H = 8
        D = 32
        DEPTH = 1
        LAMBDA_INIT = 0.8 - 0.6 * math.exp(-0.3 * DEPTH)
        EPS = 1e-08
        key = jax.random.key(seed)
        ks = jax.random.split(key, 9)
        B, T, IN_DIM, OUT_DIM = (2, 256, 128, 128)
        E = 2 * H * D
        inp = {'x': jax.random.normal(ks[0], (B, T, IN_DIM), dtype=jnp.float32), 'Wq': jax.random.normal(ks[1], (IN_DIM, E), dtype=jnp.float32) * IN_DIM ** (-0.5), 'Wkv': jax.random.normal(ks[2], (IN_DIM, 2 * E), dtype=jnp.float32) * IN_DIM ** (-0.5), 'Wout': jax.random.normal(ks[3], (E, OUT_DIM), dtype=jnp.float32) * E ** (-0.5), 'lambda_q1': 0.1 * jax.random.normal(ks[4], (D,), dtype=jnp.float32), 'lambda_k1': 0.1 * jax.random.normal(ks[5], (D,), dtype=jnp.float32), 'lambda_q2': 0.1 * jax.random.normal(ks[6], (D,), dtype=jnp.float32), 'lambda_k2': 0.1 * jax.random.normal(ks[7], (D,), dtype=jnp.float32), 'gamma': jnp.ones((2 * D,), dtype=jnp.float32)}
        return inp
    _L0_attn_in = _L0_attn_setup()

    def _L0_ffn_setup():
        import jax, jax.numpy as jnp
        import numpy as np

        def gelu(x):
            return jax.nn.gelu(x, approximate=False)
        key = jax.random.key(seed)
        ks = jax.random.split(key, 6)
        B, S, d_model = (4, 256, 128)
        n_input, n_process, n_output, d_pv = (1024, 512, 1024, 64)
        s = 0.02
        return {'x': jax.random.normal(ks[0], (B, S, d_model), jnp.float32), 'input_patterns': jax.random.normal(ks[1], (n_input, d_model), jnp.float32) * s, 'process_input_weights': jax.random.normal(ks[2], (n_process, n_input), jnp.float32) * s, 'process_values': jax.random.normal(ks[3], (n_process, d_pv), jnp.float32) * s, 'output_input_weights': jax.random.normal(ks[4], (n_output, d_pv), jnp.float32) * s, 'output_patterns': jax.random.normal(ks[5], (n_output, d_model), jnp.float32) * s}
    _L0_ffn_in = _L0_ffn_setup()

    def _L1_attn_setup():
        import jax, jax.numpy as jnp
        import numpy as np
        B, S, D, H = (2, 256, 128, 16)
        DH = D // H
        RD = DH // 2
        EPS = 1e-05

        def _rope(x):
            seq = x.shape[-2]
            inv_freq = 1.0 / 10000.0 ** (jnp.arange(0, RD, 2, dtype=jnp.float32) / RD)
            t = jnp.arange(seq, dtype=jnp.float32)
            freqs = t[:, None] * inv_freq[None, :]
            freqs = jnp.repeat(freqs, 2, axis=-1)
            cosf, sinf = (jnp.cos(freqs), jnp.sin(freqs))
            xr, xp = (x[..., :RD], x[..., RD:])
            pairs = xr.reshape(*xr.shape[:-1], RD // 2, 2)
            rot = jnp.stack([-pairs[..., 1], pairs[..., 0]], axis=-1).reshape(xr.shape)
            return jnp.concatenate([xr * cosf + rot * sinf, xp], axis=-1)
        key = jax.random.key(seed)
        ks = jax.random.split(key, 4)
        s = 0.02
        return {'X': jax.random.normal(ks[0], (B, S, D), jnp.float32), 'W_in': jax.random.normal(ks[1], (D, 3 * D), jnp.float32) * s, 'b_in': jnp.zeros((3 * D,), jnp.float32), 'W_out': jax.random.normal(ks[2], (D, D), jnp.float32) * s, 'b_out': jnp.zeros((D,), jnp.float32), 'gamma': jnp.ones((D,), jnp.float32), 'beta': jnp.zeros((D,), jnp.float32)}
    _L1_attn_in = _L1_attn_setup()

    def _L1_ffn_setup():
        import jax, jax.numpy as jnp
        import numpy as np
        TOP_K = 2

        def _mlp(x, w_fc, w_proj):
            return jnp.square(jax.nn.relu(x @ w_fc.T)) @ w_proj.T
        key = jax.random.key(seed)
        ks = jax.random.split(key, 6)
        B, S, D, E = (4, 256, 128, 8)
        d_ff = 4 * D
        x = jax.random.normal(ks[0], (B, S, D), dtype=jnp.float32)
        router_w = jax.random.normal(ks[1], (E, D), dtype=jnp.float32) * 0.02
        w_fc = jax.random.normal(ks[2], (E, d_ff, D), dtype=jnp.float32) * 0.02
        w_proj = jax.random.normal(ks[3], (E, D, d_ff), dtype=jnp.float32) * 0.02
        shared_fc = jax.random.normal(ks[4], (d_ff, D), dtype=jnp.float32) * 0.02
        shared_proj = jax.random.normal(ks[5], (D, d_ff), dtype=jnp.float32) * 0.02
        return {'x': x, 'router_w': router_w, 'w_fc': w_fc, 'w_proj': w_proj, 'shared_fc': shared_fc, 'shared_proj': shared_proj}
    _L1_ffn_in = _L1_ffn_setup()
    _d = {'L0_attn_x': _L0_attn_in['x'], 'L0_attn_Wq': _L0_attn_in['Wq'], 'L0_attn_Wkv': _L0_attn_in['Wkv'], 'L0_attn_Wout': _L0_attn_in['Wout'], 'L0_attn_lambda_q1': _L0_attn_in['lambda_q1'], 'L0_attn_lambda_k1': _L0_attn_in['lambda_k1'], 'L0_attn_lambda_q2': _L0_attn_in['lambda_q2'], 'L0_attn_lambda_k2': _L0_attn_in['lambda_k2'], 'L0_attn_gamma': _L0_attn_in['gamma'], 'L0_ffn_input_patterns': _L0_ffn_in['input_patterns'], 'L0_ffn_process_input_weights': _L0_ffn_in['process_input_weights'], 'L0_ffn_process_values': _L0_ffn_in['process_values'], 'L0_ffn_output_input_weights': _L0_ffn_in['output_input_weights'], 'L0_ffn_output_patterns': _L0_ffn_in['output_patterns'], 'L1_attn_W_in': _L1_attn_in['W_in'], 'L1_attn_b_in': _L1_attn_in['b_in'], 'L1_attn_W_out': _L1_attn_in['W_out'], 'L1_attn_b_out': _L1_attn_in['b_out'], 'L1_attn_gamma': _L1_attn_in['gamma'], 'L1_attn_beta': _L1_attn_in['beta'], 'L1_ffn_router_w': _L1_ffn_in['router_w'], 'L1_ffn_w_fc': _L1_ffn_in['w_fc'], 'L1_ffn_w_proj': _L1_ffn_in['w_proj'], 'L1_ffn_shared_fc': _L1_ffn_in['shared_fc'], 'L1_ffn_shared_proj': _L1_ffn_in['shared_proj']}
    _x0 = _d['L0_attn_x']
    _d['L0_attn_x'] = jax.random.normal(jax.random.fold_in(jax.random.key(seed), 1), (4, 512, 128), dtype=_x0.dtype)
    del _x0
    return _d

def reference(L0_attn_x, L0_attn_Wq, L0_attn_Wkv, L0_attn_Wout, L0_attn_lambda_q1, L0_attn_lambda_k1, L0_attn_lambda_q2, L0_attn_lambda_k2, L0_attn_gamma, L0_ffn_input_patterns, L0_ffn_process_input_weights, L0_ffn_process_values, L0_ffn_output_input_weights, L0_ffn_output_patterns, L1_attn_W_in, L1_attn_b_in, L1_attn_W_out, L1_attn_b_out, L1_attn_gamma, L1_attn_beta, L1_ffn_router_w, L1_ffn_w_fc, L1_ffn_w_proj, L1_ffn_shared_fc, L1_ffn_shared_proj):

    def _L0_attn_ref(x, Wq, Wkv, Wout, lambda_q1, lambda_k1, lambda_q2, lambda_k2, gamma):
        import jax, jax.numpy as jnp
        import numpy as np
        import math
        H = 8
        D = 32
        DEPTH = 1
        LAMBDA_INIT = 0.8 - 0.6 * math.exp(-0.3 * DEPTH)
        EPS = 1e-08
        B, T, _ = x.shape
        scaling = D ** (-0.5)
        q = (x @ Wq).reshape(B, T, 2 * H, D).transpose(0, 2, 1, 3) * scaling
        kv = x @ Wkv
        k, v = jnp.split(kv, 2, axis=-1)
        k = k.reshape(B, T, 2 * H, D).transpose(0, 2, 1, 3)
        v = v.reshape(B, T, H, 2 * D).transpose(0, 2, 1, 3)
        dots = jnp.einsum('bhqd,bhkd->bhqk', q, k)
        attn_w = jax.nn.softmax(dots.astype(jnp.float32), axis=-1).astype(dots.dtype)
        lam1 = jnp.exp(jnp.sum(lambda_q1 * lambda_k1))
        lam2 = jnp.exp(jnp.sum(lambda_q2 * lambda_k2))
        lam = lam1 - lam2 + LAMBDA_INIT
        attn_w = attn_w.reshape(B, H, 2, T, T)
        attn_w = attn_w[:, :, 0] - lam * attn_w[:, :, 1]
        attn = jnp.einsum('bhqk,bhkd->bhqd', attn_w, v)
        rms = jnp.sqrt(jnp.mean(attn * attn, axis=-1, keepdims=True))
        attn = gamma * (attn / (rms + EPS))
        attn = attn * (1.0 - LAMBDA_INIT)
        attn = attn.transpose(0, 2, 1, 3).reshape(B, T, 2 * H * D)
        return attn @ Wout

    def _L0_ffn_ref(x, input_patterns, process_input_weights, process_values, output_input_weights, output_patterns):
        import jax, jax.numpy as jnp
        import numpy as np

        def gelu(x):
            return jax.nn.gelu(x, approximate=False)
        B, S, d_model = x.shape
        n_input = input_patterns.shape[0]
        n_process = process_input_weights.shape[0]
        n_output = output_input_weights.shape[0]
        k_input = max(n_input // 8, 64)
        k_process = max(n_process // 8, 32)
        k_output = max(n_output // 8, 64)
        input_acts = gelu(jnp.einsum('bsd,nd->bsn', x, input_patterns))
        input_acts_seq = input_acts.mean(axis=1)
        top_input_acts, top_input_idx = jax.lax.top_k(input_acts_seq, k_input)
        brow = jnp.arange(B)[:, None]
        input_repr = jnp.zeros((B, n_input), x.dtype).at[brow, top_input_idx].set(top_input_acts)
        process_acts = gelu(jnp.einsum('bn,pn->bp', input_repr, process_input_weights))
        top_process_acts, top_process_idx = jax.lax.top_k(process_acts, k_process)
        selected_process_values = process_values[top_process_idx]
        process_weights = jax.nn.softmax(top_process_acts, axis=-1)
        aggregated_value = jnp.einsum('bk,bkd->bd', process_weights, selected_process_values)
        output_acts_seq = gelu(jnp.einsum('bd,od->bo', aggregated_value, output_input_weights))
        top_output_acts, top_output_idx = jax.lax.top_k(output_acts_seq, k_output)
        selected_output_patterns = output_patterns[top_output_idx]
        out_per_seq = jnp.einsum('bk,bkm->bm', top_output_acts, selected_output_patterns)
        output = jnp.broadcast_to(out_per_seq[:, None, :], (B, S, d_model))
        return output

    def _L1_attn_ref(X, W_in, b_in, W_out, b_out, gamma, beta):
        import jax, jax.numpy as jnp
        import numpy as np
        B, S, D, H = (2, 256, 128, 16)
        DH = D // H
        RD = DH // 2
        EPS = 1e-05

        def _rope(x):
            seq = x.shape[-2]
            inv_freq = 1.0 / 10000.0 ** (jnp.arange(0, RD, 2, dtype=jnp.float32) / RD)
            t = jnp.arange(seq, dtype=jnp.float32)
            freqs = t[:, None] * inv_freq[None, :]
            freqs = jnp.repeat(freqs, 2, axis=-1)
            cosf, sinf = (jnp.cos(freqs), jnp.sin(freqs))
            xr, xp = (x[..., :RD], x[..., RD:])
            pairs = xr.reshape(*xr.shape[:-1], RD // 2, 2)
            rot = jnp.stack([-pairs[..., 1], pairs[..., 0]], axis=-1).reshape(xr.shape)
            return jnp.concatenate([xr * cosf + rot * sinf, xp], axis=-1)
        b, s, d = X.shape
        mu = jnp.mean(X, axis=-1, keepdims=True)
        var = jnp.var(X, axis=-1, keepdims=True)
        xn = (X - mu) * jax.lax.rsqrt(var + EPS) * gamma + beta
        qkv = xn @ W_in + b_in
        q, k, v = jnp.split(qkv, 3, axis=-1)

        def to_heads(t):
            return t.reshape(b, s, H, DH).transpose(0, 2, 1, 3)
        q, k, v = (to_heads(q), to_heads(k), to_heads(v))
        q, k = (_rope(q), _rope(k))
        scores = jnp.einsum('bhqd,bhkd->bhqk', q, k) / jnp.sqrt(jnp.float32(DH))
        attn = jax.nn.softmax(scores, axis=-1)
        ctx = jnp.einsum('bhqk,bhkd->bhqd', attn, v)
        ctx = ctx.transpose(0, 2, 1, 3).reshape(b, s, d)
        return ctx @ W_out + b_out + X

    def _L1_ffn_ref(x, router_w, w_fc, w_proj, shared_fc, shared_proj):
        import jax, jax.numpy as jnp
        import numpy as np
        TOP_K = 2

        def _mlp(x, w_fc, w_proj):
            return jnp.square(jax.nn.relu(x @ w_fc.T)) @ w_proj.T
        B, S, D = x.shape
        E = router_w.shape[0]
        T = B * S
        flat = x.reshape(T, D)
        logits = flat @ router_w.T
        probs = jax.nn.softmax(logits.astype(jnp.float32), axis=-1)
        topk_p, topk_i = jax.lax.top_k(probs, TOP_K)
        topk_w = (topk_p / jnp.maximum(topk_p.sum(-1, keepdims=True), 1e-09)).astype(flat.dtype)
        combine = jnp.zeros((T, E), dtype=flat.dtype)
        combine = combine.at[jnp.arange(T)[:, None], topk_i].add(topk_w)
        out = jnp.zeros_like(flat)
        for e in range(E):
            out = out + _mlp(flat, w_fc[e], w_proj[e]) * combine[:, e:e + 1]
        out = out + _mlp(flat, shared_fc, shared_proj)
        return out.reshape(B, S, D)
    x = L0_attn_x
    x = _layernorm(x + _L0_attn_ref(x, L0_attn_Wq, L0_attn_Wkv, L0_attn_Wout, L0_attn_lambda_q1, L0_attn_lambda_k1, L0_attn_lambda_q2, L0_attn_lambda_k2, L0_attn_gamma), axis=-1)
    x = _layernorm(x + _L0_ffn_ref(x, L0_ffn_input_patterns, L0_ffn_process_input_weights, L0_ffn_process_values, L0_ffn_output_input_weights, L0_ffn_output_patterns), axis=-1)
    x = _layernorm(x + _L1_attn_ref(x, L1_attn_W_in, L1_attn_b_in, L1_attn_W_out, L1_attn_b_out, L1_attn_gamma, L1_attn_beta), axis=-1)
    x = _layernorm(x + _L1_ffn_ref(x, L1_ffn_router_w, L1_ffn_w_fc, L1_ffn_w_proj, L1_ffn_shared_fc, L1_ffn_shared_proj), axis=-1)
    return x

_drawn_inputs = setup_inputs


def setup_inputs(seed=0):
    import zlib

    import numpy as np

    out = dict(_drawn_inputs(seed))
    spreads = {'L0_attn_gamma': (1.0, 0.2),
     'L1_attn_b_in': (0.0, 0.781),
     'L1_attn_b_out': (0.0, 0.1),
     'L1_attn_gamma': (1.0, 0.6),
     'L1_attn_beta': (0.0, 0.8)}
    factors = {'L0_attn_lambda_q2': 4.964,
     'L0_attn_lambda_k2': 4.755,
     'L0_ffn_input_patterns': 8.0,
     'L0_ffn_process_input_weights': 8.0,
     'L0_ffn_process_values': 8.0,
     'L0_ffn_output_input_weights': 8.0,
     'L0_ffn_output_patterns': 8.0,
     'L1_attn_W_in': 8.0,
     'L1_attn_W_out': 4.541,
     'L1_ffn_router_w': 3.192,
     'L1_ffn_w_fc': 3.107,
     'L1_ffn_w_proj': 2.835}
    for name, (base, spread) in spreads.items():
        noise = np.random.default_rng([zlib.crc32(name.encode()), seed]).standard_normal(out[name].shape)
        drawn = base * np.exp(spread * noise) if base else spread * noise
        out[name] = jnp.asarray(drawn.astype(out[name].dtype))
    for name, factor in factors.items():
        out[name] = (out[name] * factor).astype(out[name].dtype)
    return out
```

```python
from contextlib import ExitStack
import math

import numpy as np

import concourse.bass as bass
from concourse import mybir

F32 = mybir.dt.float32
F16 = mybir.dt.float16
ALU = mybir.AluOpType
ACT = mybir.ActivationFunctionType
AX = mybir.AxisListType

P = 128
D = 128
B = 4
S = 512
T = B * S
NT = T // P
TPB = S // P
BANK = 512
NQK = 16
H0, DH0, DV0 = 8, 32, 64
DH1 = 8
RD = DH1 // 2
LAMBDA_INIT = 0.8 - 0.6 * math.exp(-0.3)
SROWS = 96
PRING = 16
N_IN, N_PROC, N_OUT, D_PV = 1024, 512, 1024, 64
K_IN, K_PROC, K_OUT = N_IN // 8, N_PROC // 8, N_OUT // 8
NE, FF = 8, 512
NX = NE + 1
WSCALE = 64.0
MSHIFT = -3.0e38
EPS_LN, EPS_RMS = 1e-5, 1e-8


class Links:

    def __init__(self, eng, sem, base=0):
        self.eng, self.sem, self.base, self.n = eng, sem, base, 0

    def __call__(self, ins):
        self.n += 1
        ins.then_inc(self.sem, 1)
        self.eng.wait_ge(self.sem, self.base + self.n)


class AttnPlan:

    def __init__(self, layer):
        self.layer = layer
        self.J = 2 if layer == 0 else 4
        self.W = NQK // self.J
        self.dh = DH0 if layer == 0 else DH1
        self.scale = self.dh ** -0.5
        self.nd = 6 * self.J if layer == 0 else 6
        self.ecnt = 2 if layer == 0 else 1
        self.ring_steps = PRING // self.J
        self.credit = self.ring_steps - 1 if layer == 0 else self.ring_steps
        if layer == 0:
            self.pieces = {(0, 2): "q0", (1, 2): "k0", (2, 2): "v0", (3, 2): "v1", (4, 2): "q1", (5, 2): "k1"}
            self.vcopies = {1: (3, 0), 6: (0, 16), 7: (2, 24)}
            self.vregions = {1: [3], 6: [0, 1], 7: [2]}
            self.loads = {1: [0, 1], 2: [2], 3: [3], 5: [4, 5], 6: [6], 7: [7]}
            self.last_v = 6
        else:
            self.pieces = {(0, 2): "q", (1, 2): "k", (2, 1): "v0", (2, 2): "v1"}
            self.vcopies = {1: (3, 0), 3: (0, 12)}
            self.vregions = {1: [3], 3: [0, 1, 2]}
            self.loads = {1: [0, 1], 2: [2], 3: [3]}
            self.last_v = 3
        self.NP = len(self.pieces)
        self.per_window = 2 * self.J + 1
        self.U0 = self.NP + 2 * self.per_window
        self.UB = self.W * self.per_window + self.NP
        assert self.UB % 2 == 0 and self.U0 % 2 == 0

    def before(self, w, last):
        return w * self.per_window + (0 if last else sum(1 for p in self.pieces if p[0] < w))

    def use(self, w, s, kind, i=0, last=False):
        n = self.before(w, last)
        for step in range(4):
            for pair in range(self.J // 2):
                if kind == "sm" and (step, pair) == (s, i):
                    return n
                n += 1
            if not last and (w, step) in self.pieces:
                if kind == "piece" and step == s:
                    return n
                n += 1
        assert kind == "tr"
        return n


def attention(nc, M, plan):
    A, L, J, W = plan, plan.layer, plan.J, plan.W
    PS = M.PS
    ctx = ExitStack()

    def sem(name):
        return ctx.enter_context(nc.semaphore(f"l{L}_{name}"))

    with ctx:
        weights_in = sem("weights_in")
        xb_in = sem("xb_in")
        stack_in = [sem(f"stack_in{g}") for g in range(W)]
        bounce_out = sem("bounce_out")
        max_in = [sem(f"max_in{p}") for p in range(2)]
        sums_out = [sem(f"sums_out{p}") for p in range(2)]
        sm_ready = sem("sm_ready")
        sm_free = sem("sm_free")
        st_ready = sem("st_ready")
        exp_done = sem("exp_done")
        pv_done = sem("pv_done")
        o_evac = sem("o_evac")
        hi_done = sem("hi_done")
        v_copied = sem("v_copied")
        own = sem("own")
        pool_own = sem("pool_own")
        carried = sem("carried")
        ready = sem("ready")
        block = ctx.enter_context(nc.Block())

        piece_order = list(A.pieces.values())

        @block.sync
        def _(sp):
            M.load_weights(sp, L, weights_in)
            for par in range(2):
                sp.sem_inc(sums_out[par], 1)

            def wait(s, value):
                sp.wait_ge(s, value)
                if not isinstance(value, int):
                    sp.sem_inc(carried, 1)

            def load_xb(b):
                if L == 0:
                    sp.dma_start(M.xb[:], M.xT_dram[:, bass.ds(b * S, S)]).then_inc(xb_in, 16)
                else:
                    sp.dma_start(M.xb[:], M.xT[:, bass.ds(b * S, S)]).then_inc(xb_in, 16)

            def load_stack(g):
                blocks = [(M.Qs, 0, 0), (M.Qs, 1, 0), (M.Qs, 2, 1), (M.Ks, 0, 2), (M.Ks, 1, 3), (M.Ks, 2, 2)]
                for stack, blk, part in blocks:
                    if L == 0:
                        hp, half = g // 2, g % 2
                        for j in range(J):
                            row = DH0 * (2 * j + half)
                            sp.dma_start(stack[DH0 * blk:DH0 * (blk + 1), g * J + j, :],
                                         M.qk[row:row + DH0, part, hp, :]).then_inc(stack_in[g], 16)
                    else:
                        src = M.qk_dram[part, g * J * DH1:(g + 1) * J * DH1, :]
                        sp.dma_start(stack[DH1 * blk:DH1 * (blk + 1), g * J:(g + 1) * J, :],
                                     src.rearrange("(h p) t -> p h t", p=DH1)).then_inc(stack_in[g], 16)

            def bounce(n):
                sp.dma_start(M.qk_dram.rearrange("k p t -> p k t"), M.qk[:, :, 0, :]).then_inc(bounce_out, 16)
                wait(bounce_out, 16 * (n + 1))

            def max_row(u, g, par):
                wait(sm_free, u + 1)
                sp.dma_start(M.Qs[SROWS:SROWS + 1, g * J:(g + 1) * J, :], M.mrow[par][0:4 * J, :])\
                  .then_inc(max_in[par], 16)

            load_xb(0)
            sp.wait_ge(ready, 1)
            sp.wait_ge(sm_free, A.NP)
            if L == 1:
                bounce(0)
            for g in range(W):
                load_stack(g)
            for g in range(2):
                max_row(A.NP + (g + 1) * A.per_window - 1, g, g % 2)

            def batch(b, last):
                base, stb = A.U0 + b * A.UB, 4 * J * W * b
                if not last:
                    wait(sm_free, base - 1)
                    load_xb(b + 1)
                for w in range(W):
                    if not last and w in A.loads:
                        if L == 1 and w == 1:
                            wait(sm_free, base + A.use(1, 2, "piece") + 1)
                            for g in range(W):
                                wait(stack_in[g], 16 * A.nd * (b + 1))
                            bounce(b + 1)
                        for g in A.loads[w]:
                            if L == 0:
                                wait(sm_free, base + A.use(1 if g < 4 else 5, 2, "piece") + 1)
                            wait(st_ready, stb + 4 * J * (g + 1))
                            load_stack(g)
                    if not (last and w >= W - 2):
                        max_row(base + A.use(w, 0, "tr", last=last), (w + 2) % W, w % 2)
                    if L == 0:
                        wait(o_evac, 1 + A.ecnt * (W * b + w + 1))
                        sp.dma_start(M.sums_dram[bass.ds(b, 1), w].rearrange("a t q -> (a t) q"),
                                     M.sums[w % 2][0:P:32, :]).then_inc(sums_out[w % 2], 16)

            with sp.Fori(0, B - 1) as b:
                batch(b, False)
            batch(B - 1, True)
            if L == 0:
                for par in range(2):
                    sp.wait_ge(sums_out[par], 1 + 16 * B * W // 2)

        @block.gpsimd
        def _(pool):
            if L == 0:
                nc.gpsimd.memset(M.ones[:], 1.0).then_inc(pool_own, 1)
                pool.wait_ge(pool_own, 1)
                nc.gpsimd.memset(M.Ks[SROWS:SROWS + 1], 1.0).then_inc(ready, 1)
            else:
                nc.gpsimd.memset(M.Qs[0:SROWS], 0.0).then_inc(pool_own, 1)
                pool.wait_ge(pool_own, 1)
                nc.gpsimd.memset(M.Ks[0:SROWS], 0.0).then_inc(ready, 1)
                pool.wait_ge(weights_in, 16 * M.n_weights[L])
                nc.gpsimd.tensor_tensor(M.x[:], M.x[:], M.x[:], ALU.add).then_inc(pool_own, 1)
                pool.wait_ge(pool_own, 2)
                nc.gpsimd.tensor_tensor(M.x[:], M.x[:], M.bo[:].rearrange("p (o d) -> p o d", o=1).broadcast_to([P, NT, D]),
                                        ALU.add)

        @block.tensor
        def _(pe):
            pe.sem_inc(pv_done, A.credit)
            pe.wait_ge(weights_in, M.n_weights[L] * 16)
            pe.wait_ge(ready, 1)

            def free(base, local):
                u = base + local
                if not (isinstance(u, int) and u < 2):
                    pe.wait_ge(sm_free, u - 1)
                return 2 * (local % 2)

            def score_max(base, local, g, qt, pair):
                bank = free(base, local)
                for i in range(2):
                    slot = g * J + 2 * pair + i
                    mm = pe.matmul(PS[:, bank + i, :], M.Qs[0:SROWS, slot, qt * P:(qt + 1) * P],
                                   M.Ks[0:SROWS, slot, :], start=True, stop=True)
                mm.then_inc(sm_ready, 1)

            def turn_max(base, local):
                pe.wait_ge(sm_free, base + local)
                bank = 2 * (local % 2)
                pe.transpose(PS[0:4 * J, bank, 0:P], M.negm[:, 0:4 * J], M.ident[:]).then_inc(sm_ready, 1)

            def piece(base, local, name, nb):
                pe.wait_ge(xb_in, 16 * (nb + 1))
                bank = free(base, local)
                if L == 0:
                    for i in range(2):
                        c = 2 * int(name[1]) + i
                        if name[0] == "v":
                            mm = pe.matmul(PS[:, bank + i, :], M.xb[:, c * P:(c + 1) * P], M.Wkv[:, 512:1024],
                                           start=True, stop=True)
                        else:
                            w_ = (M.Wq if name[0] == "q" else M.Wkv)[:, c * P:(c + 1) * P]
                            mm = pe.matmul(PS[:, bank + i, :], w_, M.xb[:], start=True, stop=True)
                elif name in ("q", "k"):
                    c = 0 if name == "q" else 1
                    pe.matmul(PS[:, bank, :], M.Win[:, c * D:(c + 1) * D], M.xb[:], start=True, stop=True)
                    mm = pe.matmul(PS[:, bank + 1, :], M.WinR[:, c * D:(c + 1) * D], M.xb[:], start=True, stop=True)
                else:
                    for i in range(2):
                        c = 2 * int(name[1]) + i
                        mm = pe.matmul(PS[:, bank + i, 0:D], M.xb[:, c * P:(c + 1) * P], M.Win[:, 2 * D:3 * D],
                                       start=True, stop=True)
                mm.then_inc(sm_ready, 1)

            def score_t(k, b):
                w, kt = k // 4, k % 4
                for j in range(J):
                    n, slot = k * J + j, w * J + j
                    nb = 4 * W * J * b + n
                    if not (isinstance(nb, int) and nb < 2):
                        pe.wait_ge(exp_done, nb - 1)
                    if j == 0 and kt == 0:
                        pe.wait_ge(max_in[w % 2], 16 * (W // 2 * b + w // 2 + 1))
                    pe.matmul(PS[:, 4 + n % 2, :], M.Ks[0:SROWS + 1, slot, kt * P:(kt + 1) * P],
                              M.Qs[0:SROWS + 1, slot, :], start=True, stop=True).then_inc(st_ready, 1)

            def product(k, b):
                w, kt = k // 4, k % 4
                if kt == 0:
                    pe.wait_ge(o_evac, 1 + A.ecnt * (W * b + w))
                    if w in (0, A.last_v):
                        pe.wait_ge(v_copied, 3 + 4 * b + (1 if w else 0))
                pe.wait_ge(exp_done, 4 * W * J * b + J * (k + 1))
                for j in range(J):
                    slot = (k * J + j) % PRING
                    if L == 0:
                        hp = w // 2
                        mm = pe.matmul(PS[64 * j:64 * j + 64, 6, :],
                                       M.V[:, kt, hp * P + DV0 * j:hp * P + DV0 * (j + 1)], M.Pr[:, slot, :],
                                       start=(kt == 0), stop=(kt == 3), skip_group_check=True)
                    else:
                        h = w * J + j
                        mm = pe.matmul(PS[32 * j:32 * j + 32, 6, :], M.V[:, kt, 32 * h:32 * h + 32], M.Pr[:, slot, :],
                                       start=(kt == 0), stop=(kt == 3), skip_group_check=True)
                if L == 0 and kt % 2 == 1:
                    for kk in (k - 1, k):
                        for j in range(J):
                            strip = 32 * (2 * (kk % 2) + j)
                            mm = pe.matmul(PS[strip:strip + 32, 7, :], M.ones[:, 0:32], M.Pr[:, (kk * J + j) % PRING, :],
                                           start=(kt == 1), stop=(kt == 3), skip_group_check=True)
                mm.then_inc(pv_done, 1)

            for i, name in enumerate(piece_order):
                piece(0, i, name, 0)
            for g in range(2):
                pe.wait_ge(stack_in[g], 16 * A.nd)
                for qt in range(4):
                    for pair in range(J // 2):
                        score_max(0, A.NP + g * A.per_window + qt * (J // 2) + pair, g, qt, pair)
                turn_max(0, A.NP + (g + 1) * A.per_window - 1)
            score_t(0, 0)

            def batch(b, last):
                base = A.U0 + b * A.UB
                for k in range(4 * W):
                    w, s = k // 4, k % 4
                    if not (last and w >= W - 2):
                        g = (w + 2) % W
                        if s == 0:
                            pe.wait_ge(stack_in[g], 16 * A.nd * (b + (2 if w + 2 >= W else 1)))
                        for pair in range(J // 2):
                            score_max(base, A.use(w, s, "sm", pair, last), g, s, pair)
                    if not (last and k == 4 * W - 1):
                        score_t((k + 1) % (4 * W), b if k < 4 * W - 1 else b + 1)
                    if not last and (w, s) in A.pieces:
                        piece(base, A.use(w, s, "piece"), A.pieces[(w, s)], b + 1)
                    product(k, b)
                    if s == 3 and not (last and w >= W - 2):
                        turn_max(base, A.use(w, 0, "tr", last=last))

            with pe.Fori(0, B - 1) as b:
                batch(b, False)
            batch(B - 1, True)

        @block.scalar
        def _(act):
            def exps(k, b):
                for j in range(J):
                    n = k * J + j
                    nb = 4 * W * J * b + n
                    act.wait_ge(st_ready, nb + 1)
                    if j == 0:
                        act.wait_ge(pv_done, 4 * W * b + k + 1)
                    nc.scalar.activation(M.Pr[:, n % PRING, :], PS[:, 4 + n % 2, :], ACT.Exp, scale=A.scale)\
                      .then_inc(exp_done, 1)

            def high_parts(base, local, name):
                u = base + local
                bank = 2 * (local % 2)
                act.wait_ge(sm_ready, u + 1)
                c = 2 * int(name[1])
                part = 0 if name[0] == "q" else 2
                nc.scalar.activation(M.qk[:, part, c:c + 2, :], PS[:, bank:bank + 2, :], ACT.Copy).then_inc(hi_done, 1)

            if L == 0:
                for i, name in enumerate(piece_order):
                    if name[0] in "qk":
                        high_parts(0, i, name)
            exps(0, 0)
            act.sem_inc(o_evac, 1)

            def batch(b, last):
                base = A.U0 + b * A.UB
                for k in range(4 * W):
                    w, s = k // 4, k % 4
                    if k < 4 * W - 1:
                        exps(k + 1, b)
                    elif not last:
                        exps(0, b + 1)
                    if L == 0 and not last and (w, s) in A.pieces and A.pieces[(w, s)][0] in "qk":
                        name = A.pieces[(w, s)]
                        for g in range(4 * int(name[1]), 4 * int(name[1]) + 4):
                            act.wait_ge(stack_in[g], 16 * A.nd * (b + 1))
                        high_parts(base, A.use(w, s, "piece"), name)
                    if s == 3:
                        act.wait_ge(pv_done, A.credit + 4 * W * b + k + 1)
                        if L == 0:
                            nc.scalar.activation(M.o[:, w % 2, w // 2, bass.ds(b * S, S)], PS[:, 6, :], ACT.Copy)\
                              .then_inc(o_evac, 1)
                            act.wait_ge(sums_out[w % 2], 1 + 16 * (W // 2 * b + w // 2))
                            nc.scalar.activation(M.sums[w % 2][:], PS[:, 7, :], ACT.Copy).then_inc(o_evac, 1)
                        else:
                            nc.scalar.activation(M.o[:, w, bass.ds(b * S, S)], PS[:, 6, :], ACT.Copy)\
                              .then_inc(o_evac, 1)

            with act.Fori(0, B - 1) as b:
                batch(b, False)
            batch(B - 1, True)

        @block.vector
        def _(dve):
            def reduce(base, local, qt, pair):
                bank = 2 * (local % 2)
                dve.wait_ge(sm_ready, base + local + 1)
                cols = M.negm[:, 8 * pair:8 * pair + 8].rearrange("p (j q) -> p j q", q=4)[:, :, qt]
                nc.vector.tensor_reduce(cols, PS[:, bank:bank + 2, :], AX.X, ALU.max, negate=True).then_inc(sm_free, 1)

            def take_row(base, local, par, count):
                bank = 2 * (local % 2)
                dve.wait_ge(sm_ready, base + local + 1)
                dve.wait_ge(max_in[par], 16 * count)
                nc.vector.tensor_copy(M.mrow[par][0:4 * J, :], PS[0:4 * J, bank, 0:P]).then_inc(sm_free, 1)

            def piece(base, local, name, hi_count, own_base, b1):
                bank = 2 * (local % 2)
                u = base + local
                dve.wait_ge(sm_ready, u + 1)
                if L == 0 and name[0] == "v":
                    c = 2 * int(name[1])
                    nc.vector.tensor_copy(M.Vn[:, c:c + 2, :], PS[:, bank:bank + 2, :]).then_inc(sm_free, 1)
                elif L == 0:
                    c, part = 2 * int(name[1]), 0 if name[0] == "q" else 2
                    dve.wait_ge(hi_done, hi_count)
                    nc.vector.tensor_tensor(M.qk[:, part + 1, c:c + 2, :], PS[:, bank:bank + 2, :],
                                            M.qk[:, part, c:c + 2, :], ALU.subtract).then_inc(sm_free, 1)
                elif name[0] == "v":
                    for i in range(2):
                        c = 2 * int(name[1]) + i
                        dst = M.Vn[:, c, :].rearrange("p (h e) -> p h e", e=32)[:, :, 0:DH1]
                        last = nc.vector.tensor_tensor(dst, PS[:, bank + i, 0:D].rearrange("p (h e) -> p h e", e=DH1),
                                                       M.bv[:].rearrange("p (h e) -> p h e", e=DH1), ALU.add)
                    last.then_inc(sm_free, 1)
                else:
                    c, part = (0, 0) if name == "q" else (1, 2)
                    link = Links(dve, own, own_base)
                    dve.wait_ge(sm_free, u)
                    link(nc.vector.scalar_tensor_tensor(out=M.rot[:, 0, :], in0=PS[:, bank, :], scalar=M.bqk[:, c:c + 1],
                                                        in1=M.cos[:], op0=ALU.add, op1=ALU.mult))
                    link(nc.vector.scalar_tensor_tensor(out=M.rot[:, 1, :], in0=PS[:, bank + 1, :],
                                                        scalar=M.bqk[:, 2 + c:3 + c], in1=M.sin[:],
                                                        op0=ALU.add, op1=ALU.mult))
                    link(nc.vector.tensor_tensor(M.rot[:, 0, :], M.rot[:, 0, :], M.rot[:, 1, :], ALU.add))
                    dve.wait_ge(bounce_out, 16 * b1)
                    link(nc.vector.tensor_copy(M.qk[:, part, 0, :], M.rot[:, 0, :]))
                    nc.vector.tensor_tensor(M.qk[:, part + 1, 0, :], M.rot[:, 0, :], M.qk[:, part, 0, :],
                                            ALU.subtract).then_inc(sm_free, 1)

            def copy_v(region):
                cols = slice(region * P, (region + 1) * P)
                nc.vector.tensor_copy(M.V[:, :, cols], M.Vn[:, :, cols]).then_inc(v_copied, 1)

            dve.wait_ge(weights_in, 16 * M.n_weights[L])
            if L == 1:
                nc.vector.memset(M.Vn[:], 0.0).then_inc(own, 1)
                dve.wait_ge(own, 1)
                nc.vector.memset(M.Vn[:].rearrange("p k (h e) -> p k h e", e=32)[:, :, :, DH1], 1.0).then_inc(own, 1)
                dve.wait_ge(own, 2)
            own0, hi0 = 2, 0
            for i, name in enumerate(piece_order):
                if name[0] in "qk":
                    hi0 += 1
                piece(0, i, name, hi0, own0 + 4 * i, 0)
            dve.wait_ge(sm_free, A.NP)
            for region in range(3):
                copy_v(region)
            for g in range(2):
                for qt in range(4):
                    for pair in range(J // 2):
                        reduce(0, A.NP + g * A.per_window + qt * (J // 2) + pair, qt, pair)
                take_row(0, A.NP + (g + 1) * A.per_window - 1, g % 2, 0)

            def batch(b, last):
                base = A.U0 + b * A.UB
                hi, ni = 0, 0
                for w in range(W):
                    for s in range(4):
                        if not (last and w >= W - 2):
                            for pair in range(J // 2):
                                reduce(base, A.use(w, s, "sm", pair, last), s, pair)
                        if s == 2 and w in A.vcopies and not (last and w > 1):
                            dve.wait_ge(pv_done, A.credit + 4 * W * b + A.vcopies[w][1])
                            if w > 1:
                                vl = max(p for p in A.pieces if A.pieces[p][0] == "v")
                                dve.wait_ge(sm_free, base + A.use(*vl, "piece") + 1)
                            for region in A.vregions[w]:
                                copy_v(region)
                        if not last and (w, s) in A.pieces:
                            name = A.pieces[(w, s)]
                            if name[0] in "qk":
                                hi += 1
                            piece(base, A.use(w, s, "piece"), name, hi0 + b * hi0 + hi, own0 + 8 * (b + 1) + 4 * ni, b + 1)
                            ni += 1
                    if not (last and w >= W - 2):
                        take_row(base, A.use(w, 0, "tr", last=last), w % 2, W // 2 * b + w // 2 + 1)

            with dve.Fori(0, B - 1) as b:
                batch(b, False)
            batch(B - 1, True)


def spread(ap, n):
    p, a = ap.shape
    return ap.rearrange("p (a o) -> p a o", o=1).broadcast_to([p, a, n])


def l0_output(nc, M):
    PS = M.PS
    HP = H0 // 2
    ctx = ExitStack()

    def sem(name):
        return ctx.enter_context(nc.semaphore(f"out0_{name}"))

    ring = M.Pr[:].rearrange("p a b -> p (a b)")
    rsum = [ring[:, 4096 * i:4096 * (i + 1)].rearrange("p (h s q) -> p h s q", h=HP, s=2) for i in range(2)]
    sqb = [M.Vn[:].rearrange("p k c -> p (k c)").rearrange("p (h q) -> p h q", h=HP),
           M.V[:].rearrange("p k c -> p (k c)").rearrange("p (h q) -> p h q", h=HP)]
    with ctx:
        w_in = sem("w_in")
        sums_in = sem("sums_in")
        r_ready = sem("r_ready")
        r_out = sem("r_out")
        r_in = [sem(f"r_in{i}") for i in range(2)]
        own = sem("own")
        lam_e = sem("lam_e")
        diff = sem("diff")
        sq = sem("sq")
        ms = sem("ms")
        ms_c = sem("ms_c")
        ms_out = sem("ms_out")
        ms_in = sem("ms_in")
        rms = sem("rms")
        r2_ready = sem("r2_ready")
        r2_out = sem("r2_out")
        r2_in = [sem(f"r2_in{i}") for i in range(2)]
        normed = sem("normed")
        yT = sem("yT")
        yT_c = sem("yT_c")
        y = sem("y")
        var = sem("var")
        std = sem("std")
        x1 = sem("x1")
        x1T = sem("x1T")
        x1T_c = sem("x1T_c")
        block = ctx.enter_context(nc.Block())

        @block.sync
        def _(sp):
            sp.dma_start(M.lam[:], M.lam_dram.rearrange("(o k) d -> o k d", o=1).broadcast_to([P, 4, DH0])).then_inc(w_in, 16)
            sp.dma_start(M.gam0[:], M.gamma0_dram).then_inc(w_in, 16)
            sp.dma_start(M.Wout[:], M.Wout_dram.rearrange("(h p) n -> p h n", p=P)).then_inc(w_in, 16)
            sp.dma_start(M.x[:], M.x_dram.rearrange("(t p) d -> p t d", p=P)).then_inc(w_in, 16)
            sp.dma_start(M.blk[:], M.blk_dram).then_inc(w_in, 16)
            for b in range(B):
                for par in range(2):
                    sp.dma_start(M.csum[:, par, b, :],
                                 M.sums_dram[b, :, 2 * par:2 * par + 2, :].rearrange("g j (a c) -> g (j a) c", c=64))\
                      .then_inc(sums_in, 16)
            M.load_ffn(sp)
            sp.wait_ge(r_ready, 1)
            sp.dma_start(M.r_dram.rearrange("b (p c) -> p b c", c=64), M.crec[:]).then_inc(r_out, 16)
            sp.wait_ge(r_out, 16)

            def load_r(b):
                for j in range(2):
                    src = M.r_dram[b].rearrange("(o g j q) -> j o g q", o=1, g=16 // 2, j=2)[j]
                    sp.dma_start(rsum[b % 2][64 * j:64 * j + 64].rearrange("p h s q -> p (h s) q"),
                                 src.broadcast_to([64, 8, S])).then_inc(r_in[b % 2], 16)

            for b in range(B):
                if b >= 2:
                    sp.wait_ge(diff, b - 1)
                load_r(b)
            for b in range(B):
                sp.wait_ge(ms_c, b + 1)
                for j in range(2):
                    sp.dma_start(M.ms_dram[b].rearrange("(h j q) -> j h q", h=HP, j=2)[j], M.msb[b % 2][j:P:32, :])\
                      .then_inc(ms_out, 16)
            sp.wait_ge(ms_out, 16 * 2 * B)
            sp.dma_start(M.cms[:], M.ms_dram.rearrange("b (p c) -> p b c", c=32)).then_inc(ms_in, 16)
            sp.wait_ge(r2_ready, 1)
            sp.dma_start(M.r2_dram.rearrange("b (p c) -> p b c", c=32), M.crms[:]).then_inc(r2_out, 16)
            sp.wait_ge(r2_out, 16)
            for b in range(B):
                if b >= 2:
                    sp.wait_ge(normed, b - 1)
                for j in range(2):
                    src = M.r2_dram[b].rearrange("(o h j q) -> j o h q", o=1, h=HP, j=2)[j]
                    sp.dma_start(sqb[b % 2][64 * j:64 * j + 64], src.broadcast_to([64, HP, S])).then_inc(r2_in[b % 2], 16)

        @block.vector
        def _(dve):
            link = Links(dve, own)
            dve.wait_ge(w_in, 16 * 5)
            link(nc.vector.tensor_tensor(M.lamp[:], M.lam[:].rearrange("p (a b) d -> p a b d", b=2)[:, :, 0, :],
                                         M.lam[:].rearrange("p (a b) d -> p a b d", b=2)[:, :, 1, :], ALU.mult))
            link(nc.vector.tensor_reduce(M.lams[:, 0:2], M.lamp[:], AX.X, ALU.add))
            dve.wait_ge(lam_e, 1)
            link(nc.vector.tensor_tensor(M.lams[:, 4:5], M.lams[:, 3:4], M.lams[:, 2:3], ALU.subtract))
            link(nc.vector.tensor_scalar(M.nlam[:], M.lams[:, 4:5], -LAMBDA_INIT, None, ALU.add))
            for h in range(HP):
                link(nc.vector.tensor_scalar(M.Wout[:, h, :], M.Wout[:, h, :], M.gam0[:, 0:1], 1.0 - LAMBDA_INIT,
                                             ALU.mult, ALU.mult))
            dve.wait_ge(sums_in, 16 * 2 * B)
            link(nc.vector.tensor_tensor(M.csum[:, 0], M.csum[:, 0], M.csum[:, 1], ALU.add))
            nc.vector.reciprocal(M.crec[:], M.csum[:, 0]).then_inc(r_ready, 1)
            for b in range(B):
                o = M.o[:, :, :, b * S:(b + 1) * S]
                dve.wait_ge(r_in[b % 2], 32 * (b // 2 + 1))
                nc.vector.tensor_tensor(o[:, 0], o[:, 0], rsum[b % 2][:, :, 0, :], ALU.mult)
                link(nc.vector.scalar_tensor_tensor(out=o[:, 1], in0=o[:, 1], scalar=M.nlam[:, 0:1],
                                                    in1=rsum[b % 2][:, :, 1, :], op0=ALU.mult, op1=ALU.mult))
                nc.vector.tensor_tensor(o[:, 0], o[:, 0], o[:, 1], ALU.add).then_inc(diff, 1)
            dve.wait_ge(rms, 1)
            link(nc.vector.tensor_scalar(M.crms[:], M.crms[:], EPS_RMS, None, ALU.add))
            nc.vector.reciprocal(M.crms[:], M.crms[:]).then_inc(r2_ready, 1)

            def norm(b):
                dve.wait_ge(r2_in[b % 2], 32 * (b // 2 + 1))
                o = M.o[:, 0, :, b * S:(b + 1) * S]
                nc.vector.tensor_tensor(o, o, sqb[b % 2], ALU.mult).then_inc(normed, 1)

            norm(0)
            for b in range(B):
                if b + 1 < B:
                    norm(b + 1)
                x = M.x[:, TPB * b:TPB * (b + 1), :]
                dve.wait_ge(y, b + 1)
                link(nc.vector.tensor_tensor(x, x, PS[:, 2 + b % 2, :].rearrange("p (t d) -> p t d", d=D), ALU.add))
                layernorm(nc, dve, link, M, TPB * b, TPB, var, std, b + 1, done=x1)

        @block.scalar
        def _(act):
            act.wait_ge(own, 2)
            nc.scalar.activation(M.lams[:, 2:4], M.lams[:, 0:2], ACT.Exp).then_inc(lam_e, 1)
            for b in range(B):
                act.wait_ge(diff, b + 1)
                if b >= 2:
                    act.wait_ge(ms, b - 1)
                nc.scalar.activation(sqb[b % 2], M.o[:, 0, :, b * S:(b + 1) * S], ACT.Square).then_inc(sq, 1)
                act.wait_ge(ms, b + 1)
                if b >= 2:
                    act.wait_ge(ms_out, 32 * b)
                nc.scalar.activation(M.msb[b % 2][:], PS[:, b % 2, :], ACT.Copy).then_inc(ms_c, 1)
            act.wait_ge(ms_in, 16)
            nc.scalar.activation(M.crms[:], M.cms[:], ACT.Sqrt).then_inc(rms, 1)

            def take_yT(b):
                act.wait_ge(yT, b + 1)
                if b >= 2:
                    act.wait_ge(y, b - 1)
                nc.scalar.activation(M.yT[b % 2][:], PS[:, b % 2, :], ACT.Copy).then_inc(yT_c, 1)

            take_yT(0)
            for b in range(B):
                if b + 1 < B:
                    take_yT(b + 1)
                act.wait_ge(var, b + 1)
                nc.scalar.activation(M.std[:, 0:TPB], M.mv[:, 0:TPB, 1], ACT.Sqrt, bias=M.eps[:, 0:1]).then_inc(std, 1)
                act.wait_ge(x1T, b + 1)
                nc.scalar.activation(M.xT[:, b * S:(b + 1) * S], PS[:, 4 + b % 2, :], ACT.Copy).then_inc(x1T_c, 1)

        @block.tensor
        def _(pe):
            pe.wait_ge(w_in, 16 * 5)
            for b in range(B):
                pe.wait_ge(sq, b + 1)
                if b >= 2:
                    pe.wait_ge(ms_c, b - 1)
                for h in range(HP):
                    mm = pe.matmul(PS[32 * h:32 * h + 32, b % 2, :], M.blk[:], sqb[b % 2][:, h, :], start=True, stop=True,
                                   skip_group_check=True)
                mm.then_inc(ms, 1)
            pe.wait_ge(own, 8)
            pe.wait_ge(ms_c, B)

            def project(b):
                pe.wait_ge(normed, b + 1)
                if b >= 2:
                    pe.wait_ge(yT_c, b - 1)
                for h in range(HP):
                    mm = pe.matmul(PS[:, b % 2, :], M.Wout[:, h, :], M.o[:, 0, h, b * S:(b + 1) * S],
                                   start=(h == 0), stop=(h == HP - 1))
                mm.then_inc(yT, 1)

            project(0)
            for b in range(B):
                if b + 1 < B:
                    project(b + 1)
                pe.wait_ge(yT_c, b + 1)
                if b >= 2:
                    pe.wait_ge(x1, b - 1)
                for t in range(TPB):
                    mm = pe.transpose(PS[:, 2 + b % 2, t * P:(t + 1) * P], M.yT[b % 2][:, t * P:(t + 1) * P], M.ident[:])
                mm.then_inc(y, 1)
                pe.wait_ge(x1, b + 1)
                if b >= 2:
                    pe.wait_ge(x1T_c, b - 1)
                for t in range(TPB):
                    mm = pe.transpose(PS[:, 4 + b % 2, t * P:(t + 1) * P], M.x[:, TPB * b + t, :], M.ident[:])
                mm.then_inc(x1T, 1)


def layernorm(nc, dve, link, M, first, n, var, std, count, out=None, done=None):
    def src(t):
        return M.x[:, first + t, :]
    out = src if out is None else out
    for t in range(n):
        ins = nc.vector.bn_stats(M.stats[:, t, :], src(t))
    link(ins)
    for t in range(n):
        ins = nc.vector.bn_aggr(M.mv[:, t, :], M.stats[:, t, :])
    ins.then_inc(var, 1)
    dve.wait_ge(std, count)
    link(nc.vector.reciprocal(M.rstd[:, 0:n], M.std[:, 0:n]))
    for t in range(n):
        ins = nc.vector.tensor_scalar(out(t), src(t), M.mv[:, t, 0:1], M.rstd[:, t:t + 1], ALU.subtract, ALU.mult)
    if done is None:
        link(ins)
    else:
        ins.then_inc(done, 1)


def ffn(nc, M):
    PS = M.PS
    NTI, NTP, NTO = N_IN // P, N_PROC // P, N_OUT // P
    ctx = ExitStack()

    def sem(name):
        return ctx.enter_context(nc.semaphore(f"ffn_{name}"))

    with ctx:
        acts = sem("acts")
        gelu = sem("gelu")
        sT = sem("sT")
        own = sem("own")
        rep = sem("rep")
        repT = sem("repT")
        repT_c = sem("repT_c")
        lin = sem("lin")
        lin_g = sem("lin_g")
        pmax = sem("pmax")
        pexp = sem("pexp")
        agg = sem("agg")
        agg_c = sem("agg_c")
        res = sem("res")
        res_c = sem("res_c")
        spreadb = sem("spread")
        var = sem("var")
        std = sem("std")
        xn = sem("xn")
        xnT = sem("xnT")
        xnT_c = sem("xnT_c")
        block = ctx.enter_context(nc.Block())
        w_in = M.ffn_in

        @block.tensor
        def _(pe):
            pe.wait_ge(w_in, 16 * M.n_ffn)
            for b in range(B):
                for n in range(NTI):
                    i = b * NTI + n
                    if i >= 4:
                        pe.wait_ge(gelu, i - 3)
                    pe.matmul(PS[:, i % 4, :], M.patT[:, n * P:(n + 1) * P], M.xT[:, b * S:(b + 1) * S],
                              start=True, stop=True).then_inc(acts, 1)
            pe.wait_ge(gelu, B * NTI)
            for n in range(NTI):
                mm = pe.transpose(PS[0:B, 4 + n // 4, (n % 4) * P:(n % 4 + 1) * P], M.actsum[:, n, :], M.ident[:])
            mm.then_inc(sT, 1)

            def turn(nt, count):
                pe.wait_ge(rep, count)
                for n in range(nt):
                    mm = pe.transpose(PS[:, 6, n * B:(n + 1) * B], M.rowb[:, n * P:(n + 1) * P], M.ident[0:B, 0:B])
                mm.then_inc(repT, 1)
                pe.wait_ge(repT_c, count)

            turn(NTI, 1)
            for n in range(NTI):
                mm = pe.matmul(PS[0:B, 0, :], M.colb[:, n * B:(n + 1) * B], M.piwT[:, n, :],
                               start=(n == 0), stop=(n == NTI - 1))
            mm.then_inc(lin, 1)
            turn(NTP, 2)
            for n in range(NTP):
                mm = pe.matmul(PS[0:D_PV, 7, 0:B], M.pv[:, n, :], M.colb[:, n * B:(n + 1) * B],
                               start=(n == 0), stop=(n == NTP - 1))
            mm.then_inc(agg, 1)
            pe.wait_ge(agg_c, 1)
            for n in range(2):
                mm = pe.matmul(PS[0:B, 1 + n, :], M.aggT[:], M.oiwT[0:D_PV, n * 512:(n + 1) * 512], start=True, stop=True)
            mm.then_inc(lin, 1)
            turn(NTO, 3)
            for n in range(NTO):
                mm = pe.matmul(PS[0:B, 3, 0:D], M.colb[:, n * B:(n + 1) * B], M.opat[:, n, :],
                               start=(n == 0), stop=(n == NTO - 1))
            mm.then_inc(res, 1)
            pe.wait_ge(res_c, 1)
            for b in range(B):
                mm = pe.matmul(PS[:, 7, b * D:(b + 1) * D], M.sel[:, b * P:(b + 1) * P], M.res[:], start=True, stop=True)
            mm.then_inc(spreadb, 1)
            for b in range(B):
                pe.wait_ge(xn, b + 1)
                if b >= 2:
                    pe.wait_ge(xnT_c, b - 1)
                for t in range(TPB):
                    mm = pe.transpose(PS[:, 4 + b % 2, t * P:(t + 1) * P], M.xn[b % 2][:, t, :], M.ident[:])
                mm.then_inc(xnT, 1)

        @block.scalar
        def _(act):
            for b in range(B):
                for n in range(NTI):
                    i = b * NTI + n
                    act.wait_ge(acts, i + 1)
                    if i >= 2:
                        act.wait_ge(gelu, i - 1)
                    nc.scalar.activation(M.junk[i % 2][:], PS[:, i % 4, :], ACT.Gelu, accum_out=M.actsum[:, n, b:b + 1])\
                      .then_inc(gelu, 1)

            def take_cols(nt, count):
                act.wait_ge(repT, count)
                nc.scalar.activation(M.colb[:, 0:nt * B], PS[:, 6, 0:nt * B], ACT.Copy).then_inc(repT_c, 1)

            take_cols(NTI, 1)
            act.wait_ge(lin, 1)
            nc.scalar.activation(M.rowa[:, 0:N_PROC], PS[0:B, 0, :], ACT.Gelu).then_inc(lin_g, 1)
            act.wait_ge(pmax, 1)
            nc.scalar.activation(M.rowb[:, 0:N_PROC], M.rowa[:, 0:N_PROC], ACT.Exp, bias=M.tops[:, 8:9]).then_inc(pexp, 1)
            take_cols(NTP, 2)
            act.wait_ge(agg, 1)
            nc.scalar.activation(M.aggT[:], PS[0:D_PV, 7, 0:B], ACT.Copy).then_inc(agg_c, 1)
            act.wait_ge(lin, 2)
            nc.scalar.activation(M.rowa[:], PS[0:B, 1:3, :].rearrange("p a b -> p (a b)"), ACT.Gelu).then_inc(lin_g, 1)
            take_cols(NTO, 3)
            act.wait_ge(res, 1)
            nc.scalar.activation(M.res[:], PS[0:B, 3, 0:D], ACT.Copy).then_inc(res_c, 1)
            for i in range(2 * B):
                act.wait_ge(var, i + 1)
                nc.scalar.activation(M.std[:, 0:TPB], M.mv[:, 0:TPB, 1], ACT.Sqrt, bias=M.eps[:, 0:1]).then_inc(std, 1)

        @block.vector
        def _(dve):
            link = Links(dve, own)

            def take_top(n, k, first=None):
                for r in range(k // 8):
                    m8 = M.tops[:, 0:8]
                    link(nc.vector.max(m8, M.rowc[:, 0:n]))
                    if r == 0 and first is not None:
                        first()
                    link(nc.vector.match_replace(out=M.rowc[:, 0:n], in_to_replace=m8, in_values=M.rowc[:, 0:n],
                                                 imm_value=MSHIFT))

            dve.wait_ge(sT, 1)
            link(nc.vector.tensor_scalar(M.rowa[:], PS[0:B, 4:6, :].rearrange("p a b -> p (a b)"), 1.0 / S, None, ALU.mult))
            link(nc.vector.tensor_copy(M.rowc[:], M.rowa[:]))
            take_top(N_IN, K_IN)
            nc.vector.scalar_tensor_tensor(out=M.rowb[:], in0=M.rowc[:], scalar=MSHIFT, in1=M.rowa[:],
                                           op0=ALU.is_equal, op1=ALU.mult).then_inc(rep, 1)
            dve.wait_ge(lin_g, 1)
            link(nc.vector.tensor_copy(M.rowc[:, 0:N_PROC], M.rowa[:, 0:N_PROC]))

            def negate_max():
                nc.vector.tensor_scalar(M.tops[:, 8:9], M.tops[:, 0:1], -1.0, None, ALU.mult).then_inc(pmax, 1)

            take_top(N_PROC, K_PROC, negate_max)
            dve.wait_ge(pexp, 1)
            link(nc.vector.scalar_tensor_tensor(out=M.rowb[:, 0:N_PROC], in0=M.rowc[:, 0:N_PROC], scalar=MSHIFT,
                                                in1=M.rowb[:, 0:N_PROC], op0=ALU.is_equal, op1=ALU.mult))
            link(nc.vector.tensor_reduce(M.tops[:, 9:10], M.rowb[:, 0:N_PROC], AX.X, ALU.add))
            link(nc.vector.reciprocal(M.tops[:, 10:11], M.tops[:, 9:10]))
            nc.vector.tensor_scalar(M.rowb[:, 0:N_PROC], M.rowb[:, 0:N_PROC], M.tops[:, 10:11], None,
                                    ALU.mult).then_inc(rep, 1)
            dve.wait_ge(lin_g, 2)
            link(nc.vector.tensor_copy(M.rowc[:], M.rowa[:]))
            take_top(N_OUT, K_OUT)
            nc.vector.scalar_tensor_tensor(out=M.rowb[:], in0=M.rowc[:], scalar=MSHIFT, in1=M.rowa[:],
                                           op0=ALU.is_equal, op1=ALU.mult).then_inc(rep, 1)
            dve.wait_ge(spreadb, 1)

            def take_xnT(b):
                dve.wait_ge(xnT, b + 1)
                nc.vector.tensor_scalar(M.xT[:, b * S:(b + 1) * S], PS[:, 4 + b % 2, :], M.gb1[:, 0:1], M.gb1[:, 1:2],
                                        ALU.mult, ALU.add).then_inc(xnT_c, 1)

            for b in range(B):
                x = M.x[:, TPB * b:TPB * (b + 1), :]
                row = PS[:, 7, b * D:(b + 1) * D].rearrange("p (o d) -> p o d", o=1).broadcast_to([P, TPB, D])
                link(nc.vector.tensor_tensor(x, x, row, ALU.add))
                layernorm(nc, dve, link, M, TPB * b, TPB, var, std, 2 * b + 1)
                if b >= 2:
                    dve.wait_ge(xnT, b - 1)
                layernorm(nc, dve, link, M, TPB * b, TPB, var, std, 2 * b + 2, out=lambda t: M.xn[b % 2][:, t, :], done=xn)
                if b:
                    take_xnT(b - 1)
            take_xnT(B - 1)


def l1_output(nc, M):
    PS = M.PS
    ctx = ExitStack()

    def sem(name):
        return ctx.enter_context(nc.semaphore(f"out1_{name}"))

    with ctx:
        oT = sem("oT")
        cx = sem("cx")
        cxT = sem("cxT")
        cxT_c = sem("cxT_c")
        y = sem("y")
        y_added = sem("y_added")
        own = sem("own")
        var = sem("var")
        std = sem("std")
        x3 = sem("x3")
        x3T = sem("x3T")
        x3T_c = sem("x3T_c")
        x3T_h = sem("x3T_h")
        lo = sem("lo")
        logit = sem("logit")
        lexp = sem("lexp")
        lsub = sem("lsub")
        wh = sem("wh")
        block = ctx.enter_context(nc.Block())

        @block.tensor
        def _(pe):
            def turn_o(t):
                if t >= 2:
                    pe.wait_ge(cx, t - 1)
                for g in range(4):
                    mm = pe.transpose(PS[:, t % 2, g * P:(g + 1) * P], M.o[:, g, t * P:(t + 1) * P], M.ident[:])
                mm.then_inc(oT, 1)

            def turn_cx(t):
                pe.wait_ge(cx, t + 1)
                if t >= 2:
                    pe.wait_ge(cxT_c, t - 1)
                pe.transpose(PS[:, 2 + t % 2, 0:P], M.cx[t % 2][:], M.ident[:]).then_inc(cxT, 1)

            def project(t):
                pe.wait_ge(cxT_c, t + 1)
                if t >= 2:
                    pe.wait_ge(y_added, t - 1)
                pe.matmul(PS[:, 4 + t % 2, 0:D], M.cxT[t % 2][:], M.Wo1[:], start=True, stop=True).then_inc(y, 1)

            def turn_x3(b):
                pe.wait_ge(x3, b + 1)
                if b >= 1:
                    pe.wait_ge(lo, b)
                for t in range(TPB):
                    mm = pe.transpose(PS[:, 6, t * P:(t + 1) * P], M.x[:, TPB * b + t, :], M.ident[:])
                mm.then_inc(x3T, 1)
                pe.wait_ge(x3T_c, b + 1)
                for t in range(TPB * b, TPB * (b + 1)):
                    mm = pe.matmul(PS[:, 7, t * NE:(t + 1) * NE], M.xT[:, t * P:(t + 1) * P], M.rT[:], start=True, stop=True)
                mm.then_inc(logit, 1)

            turn_o(0)
            for t in range(NT):
                if t + 1 < NT:
                    turn_o(t + 1)
                turn_cx(t)
                project(t)
                if t % TPB == TPB - 1 and t > TPB:
                    turn_x3(t // TPB - 1)
            turn_x3(B - 1)

        @block.scalar
        def _(act):
            def take_x3T(b):
                act.wait_ge(x3T, b + 1)
                nc.scalar.activation(M.xT[:, b * S:(b + 1) * S], PS[:, 6, :], ACT.Copy).then_inc(x3T_c, 1)
                nc.scalar.activation(M.xTh[:, b * S:(b + 1) * S], PS[:, 6, :], ACT.Copy).then_inc(x3T_h, 1)

            nc.scalar.activation(M.fch[:], M.fc[:], ACT.Copy, scale=WSCALE).then_inc(wh, 1)
            nc.scalar.activation(M.prh[:], M.pr[:], ACT.Copy, scale=WSCALE).then_inc(wh, 1)
            for t in range(NT):
                act.wait_ge(cxT, t + 1)
                if t >= 2:
                    act.wait_ge(y, t - 1)
                nc.scalar.activation(M.cxT[t % 2][:], PS[:, 2 + t % 2, 0:P], ACT.Copy).then_inc(cxT_c, 1)
                if t % TPB == TPB - 1:
                    act.wait_ge(var, t // TPB + 1)
                    nc.scalar.activation(M.std[:, 0:TPB], M.mv[:, 0:TPB, 1], ACT.Sqrt, bias=M.eps[:, 0:1]).then_inc(std, 1)
                    if t > TPB:
                        take_x3T(t // TPB - 1)
            take_x3T(B - 1)
            act.wait_ge(lsub, 1)
            nc.scalar.activation(M.rt[:, 0], M.rt[:, 0], ACT.Exp).then_inc(lexp, 1)

        @block.vector
        def _(dve):
            link = Links(dve, own)

            def take_lo(b):
                dve.wait_ge(x3T_h, b + 1)
                nc.vector.tensor_tensor(M.xTl[:, b * S:(b + 1) * S], PS[:, 6, :], M.xTh[:, b * S:(b + 1) * S],
                                        ALU.subtract).then_inc(lo, 1)

            for t in range(NT):
                dve.wait_ge(oT, t + 1)
                heads = PS[:, t % 2, :].rearrange("p (h e) -> p h e", e=32)
                link(nc.vector.reciprocal(M.rden[:], heads[:, :, DH1]))
                nc.vector.tensor_tensor(M.cx[t % 2][:].rearrange("p (h e) -> p h e", e=DH1), heads[:, :, 0:DH1],
                                        spread(M.rden[:], DH1), ALU.mult).then_inc(cx, 1)
                dve.wait_ge(y, t + 1)
                nc.vector.tensor_tensor(M.x[:, t, :], M.x[:, t, :], PS[:, 4 + t % 2, 0:D], ALU.add).then_inc(y_added, 1)
                if t % TPB == TPB - 1:
                    b = t // TPB
                    dve.wait_ge(y_added, t + 1)
                    layernorm(nc, dve, link, M, TPB * b, TPB, var, std, b + 1, done=x3)
                    if b:
                        take_lo(b - 1)
            dve.wait_ge(wh, 2)
            nc.vector.scalar_tensor_tensor(out=M.fcl[:], in0=M.fc[:], scalar=WSCALE, in1=M.fch[:],
                                           op0=ALU.mult, op1=ALU.subtract)
            nc.vector.scalar_tensor_tensor(out=M.prl[:], in0=M.pr[:], scalar=WSCALE, in1=M.prh[:],
                                           op0=ALU.mult, op1=ALU.subtract)
            take_lo(B - 1)
            dve.wait_ge(logit, B)
            lg = PS[:, 7, 0:NT * NE].rearrange("p (t e) -> p t e", e=NE)
            prob, one, two, three = M.rt[:, 0], M.rt1[:, 0], M.rt1[:, 1], M.rt1[:, 2]
            link(nc.vector.tensor_reduce(one, lg, AX.X, ALU.max))
            nc.vector.tensor_tensor(prob, lg, spread(one, NE), ALU.subtract).then_inc(lsub, 1)
            dve.wait_ge(lexp, 1)
            link(nc.vector.tensor_reduce(two, prob, AX.X, ALU.add))
            link(nc.vector.reciprocal(three, two))
            link(nc.vector.tensor_tensor(prob, prob, spread(three, NE), ALU.mult))
            other = prob.rearrange("p t (o e) -> p t o e", o=1).broadcast_to([P, NT, NE, NE])
            mine = prob.rearrange("p t (e o) -> p t e o", o=1).broadcast_to([P, NT, NE, NE])
            tri = M.tri[:].rearrange("p (o e j) -> p o e j", o=1, e=NE).broadcast_to([P, NT, NE, NE])
            nc.vector.tensor_tensor(M.gt[:], other, mine, ALU.is_gt)
            link(nc.vector.tensor_tensor(M.eq[:], other, mine, ALU.is_equal))
            link(nc.vector.tensor_tensor(M.eq[:], M.eq[:], tri, ALU.mult))
            link(nc.vector.tensor_tensor(M.gt[:], M.gt[:], M.eq[:], ALU.add))
            link(nc.vector.tensor_reduce(M.rt[:, 1], M.gt[:], AX.X, ALU.add))
            link(nc.vector.scalar_tensor_tensor(out=M.rt[:, 1], in0=M.rt[:, 1], scalar=1.5, in1=prob,
                                                op0=ALU.is_lt, op1=ALU.mult))
            link(nc.vector.tensor_reduce(one, M.rt[:, 1], AX.X, ALU.add))
            link(nc.vector.tensor_scalar(one, one, 1e-9, None, ALU.max))
            link(nc.vector.reciprocal(two, one))
            link(nc.vector.tensor_scalar(two, two, 1.0 / WSCALE, None, ALU.mult))
            link(nc.vector.memset(M.comb[:], 1.0 / WSCALE))
            link(nc.vector.tensor_tensor(M.comb[:, :, 0:NE], M.rt[:, 1], spread(two, NE), ALU.mult))


def moe(nc, M):
    PS = M.PS
    NF = FF // P
    U = NX * NF
    HB, OB = 3, 3
    ctx = ExitStack()

    def sem(name):
        return ctx.enter_context(nc.semaphore(f"moe_{name}"))

    with ctx:
        h_ready = sem("h_ready")
        h_free = sem("h_free")
        sq_done = sem("sq_done")
        hi_done = sem("hi_done")
        lo_done = sem("lo_done")
        p_done = sem("p_done")
        o_free = sem("o_free")
        own = sem("own")
        var = sem("var")
        std = sem("std")
        carried = sem("carried")
        y_ready = sem("y_ready")
        y_out = sem("y_out")
        block = ctx.enter_context(nc.Block())
        NL = 1 + 1 + 1

        @block.tensor
        def _(pe):
            pe.sem_inc(p_done, 2)

            def hidden(u, g):
                e, f = u // NF, u % NF
                pe.wait_ge(h_free, U * g + u + 1)
                cols = slice(e * FF + f * P, e * FF + (f + 1) * P)
                xh, xl = M.xTh[:, bass.ds(g * S, S)], M.xTl[:, bass.ds(g * S, S)]
                out = PS[:, u % HB, :]
                pe.matmul(out, M.fch[:, cols], xh, start=True, stop=False)
                pe.matmul(out, M.fch[:, cols], xl, start=False, stop=False)
                pe.matmul(out, M.fcl[:, cols], xh, start=False, stop=True).then_inc(h_ready, 1)

            def project(u, g):
                e, f = u // NF, u % NF
                if f == 0:
                    pe.wait_ge(o_free, NX * g + e + 1)
                pe.wait_ge(lo_done, 2 + U * g + u + 1)
                hh, hl = M.hh[u % 2], M.hl[u % 2]
                for t in range(TPB):
                    out = PS[:, 4 + e % OB, t * D:(t + 1) * D]
                    cols = slice(t * P, (t + 1) * P)
                    w = (e * NF + f) * D
                    pe.matmul(out, hh[:, cols], M.prh[:, w:w + D], start=(f == 0 and t == 0), stop=False,
                              skip_group_check=True)
                    pe.matmul(out, hh[:, cols], M.prl[:, w:w + D], start=False, stop=False, skip_group_check=True)
                    mm = pe.matmul(out, hl[:, cols], M.prh[:, w:w + D], start=False, stop=(f == NF - 1 and t == TPB - 1),
                                   skip_group_check=True)
                mm.then_inc(p_done, 1)

            with pe.Fori(0, B) as g:
                hidden(0, g)
                hidden(1, g)
                for u in range(U):
                    if u + 2 < U:
                        hidden(u + 2, g)
                    project(u, g)

        @block.scalar
        def _(act):
            act.sem_inc(h_free, HB)
            with act.Fori(0, B) as g:
                for u in range(U):
                    n = U * g + u
                    act.wait_ge(h_ready, n + 1)
                    act.wait_ge(sq_done, n + 1)
                    nc.scalar.activation(M.r[u % 2][:], PS[:, u % HB, :], ACT.Relu, scale=1.0 / WSCALE).then_inc(h_free, 1)
                    act.wait_ge(h_free, HB + n + 1)
                    act.wait_ge(p_done, n + 1)
                    nc.scalar.activation(M.hh[u % 2][:], M.r[u % 2][:], ACT.Square).then_inc(hi_done, 1)
                act.wait_ge(var, g + 1)
                nc.scalar.activation(M.std[:, 0:TPB], M.mv[:, 0:TPB, 1], ACT.Sqrt, bias=M.eps[:, 0:1]).then_inc(std, 1)

        @block.gpsimd
        def _(pool):
            pool.sem_inc(sq_done, 2)
            with pool.Fori(0, B) as g:
                for u in range(U):
                    n = U * g + u
                    pool.wait_ge(h_free, HB + n + 1)
                    pool.wait_ge(lo_done, n + 1)
                    nc.gpsimd.tensor_tensor(M.sq[u % 2][:], M.r[u % 2][:], M.r[u % 2][:], ALU.mult).then_inc(sq_done, 1)

        @block.vector
        def _(dve):
            dve.sem_inc(lo_done, 2)
            dve.sem_inc(o_free, OB)

            def combine(e, g):
                dve.wait_ge(p_done, 2 + U * g + NF * (e + 1))
                dve.wait_ge(o_free, OB + NX * g + e)
                for t in range(TPB):
                    prev = M.xg[:, t, :] if e == 0 else M.acc[:, t, :]
                    ins = nc.vector.scalar_tensor_tensor(out=M.acc[:, t, :], in0=PS[:, 4 + e % OB, t * D:(t + 1) * D],
                                                         scalar=M.cg[:, t, e:e + 1], in1=prev, op0=ALU.mult, op1=ALU.add)
                ins.then_inc(o_free, 1)

            with dve.Fori(0, B) as g:
                link = Links(dve, own, g * NL)
                nc.vector.tensor_copy(M.cg[:], M.comb[:, bass.ds(TPB * g, TPB), :])
                link(nc.vector.tensor_copy(M.xg[:], M.x[:, bass.ds(TPB * g, TPB), :]))
                for u in range(U):
                    n = U * g + u
                    dve.wait_ge(sq_done, 2 + n + 1)
                    dve.wait_ge(hi_done, n + 1)
                    dve.wait_ge(p_done, n + 1)
                    nc.vector.tensor_tensor(M.hl[u % 2][:], M.sq[u % 2][:], M.hh[u % 2][:], ALU.subtract).then_inc(lo_done, 1)
                    if u % NF == 1 and u > NF:
                        combine(u // NF - 1, g)
                combine(NX - 1, g)
                dve.wait_ge(o_free, OB + NX * (g + 1))
                for t in range(TPB):
                    ins = nc.vector.bn_stats(M.stats[:, t, :], M.acc[:, t, :])
                link(ins)
                dve.sem_inc(carried, 1)
                for t in range(TPB):
                    ins = nc.vector.bn_aggr(M.mv[:, t, :], M.stats[:, t, :])
                ins.then_inc(var, 1)
                dve.wait_ge(std, g + 1)
                link(nc.vector.reciprocal(M.rstd[:, 0:TPB], M.std[:, 0:TPB]))
                dve.wait_ge(y_out, 1 + 16 * g)
                for t in range(TPB):
                    ins = nc.vector.tensor_scalar(M.y[:, t, :], M.acc[:, t, :], M.mv[:, t, 0:1], M.rstd[:, t:t + 1],
                                                  ALU.subtract, ALU.mult)
                ins.then_inc(y_ready, 1)
                assert link.n == NL

        @block.sync
        def _(sp):
            sp.sem_inc(y_out, 1)
            with sp.Fori(0, B) as g:
                sp.wait_ge(y_ready, g + 1)
                sp.dma_start(M.out_dram[bass.ds(g, 1)].rearrange("b (t p) d -> p (b t) d", p=P), M.y[:]).then_inc(y_out, 16)
            sp.wait_ge(y_out, 1 + 16 * B)


class Memory:
    pass


def build(nc, I, out, debug=None):
    M = Memory()
    M.out_dram = out
    with ExitStack() as ctx:
        def sb(name, shape, dt=F32):
            return ctx.enter_context(nc.sbuf_tensor(name, shape, dt))

        def dram(name, shape, dt=F32):
            return nc.dram_tensor(name, shape, dt, kind="Internal").ap()

        M.PS = ctx.enter_context(nc.psum_tensor("PS", [P, 8, BANK], F32))
        M.sums_dram = dram("sums_scratch", [B, 8, 4, S])
        M.r_dram = dram("r_scratch", [B, 16 * S])
        M.ms_dram = dram("ms_scratch", [B, H0 * S])
        M.r2_dram = dram("r2_scratch", [B, H0 * S])
        M.qk_dram = dram("qk_scratch", [4, P, S], F16)
        M.x_dram, M.xT_dram = I["x"], I["xT"]
        M.lam_dram, M.gamma0_dram, M.Wout_dram, M.blk_dram = I["lam"], I["gamma0"], I["Wout"], I["blk"]

        M.x = sb("x_tokens", [P, NT, D])
        M.xT = sb("x_transposed", [P, T])
        M.ident = sb("ident", [P, P])
        M.eps = sb("eps", [P, 1])
        M.stats = sb("stats", [P, TPB, 6])
        M.mv = sb("mv", [P, TPB, 2])
        M.std = sb("std", [P, TPB])
        M.rstd = sb("rstd", [P, TPB])
        M.xb = sb("xb", [P, S])
        M.Qs = sb("q_stack", [SROWS + 1, NQK, S], F16)
        M.Ks = sb("k_stack", [SROWS + 1, NQK, S], F16)
        M.Pr = sb("exp_ring", [P, PRING, S])
        M.qk = sb("qk_parts", [P, 4, 4, S], F16)
        M.V = sb("V", [P, 4, 512])
        M.Vn = sb("V_next", [P, 4, 512])
        M.negm = sb("neg_max", [P, 16])
        M.mrow = [sb(f"max_row{i}", [16, P], F16) for i in range(2)]
        M.ones = sb("ones", [P, 32])

        M.ffn_in = ctx.enter_context(nc.semaphore("ffn_in"))
        M.n_weights = {}
        M.piwT = M.qk[:].rearrange("p a b c -> p (a b c)").bitcast(F32).rearrange("p (n c) -> p n c", c=N_PROC)

        with ExitStack() as l0:
            def sb0(name, shape, dt=F32):
                return l0.enter_context(nc.sbuf_tensor(name, shape, dt))

            M.o = sb0("o0", [P, 2, H0 // 2, T])
            M.Wq = sb0("Wq", [P, 512])
            M.Wkv = sb0("Wkv", [P, 1024])
            M.sums = [sb0(f"sums{i}", [P, S]) for i in range(2)]

            def load_l0(sp, layer, sem):
                pairs = [(M.Wq, I["Wq"]), (M.Wkv, I["Wkv"]), (M.ident, I["ident"]), (M.eps, I["eps"])]
                for dst, src in pairs:
                    sp.dma_start(dst[:], src).then_inc(sem, 16)
            M.n_weights[0] = 4
            M.load_weights = load_l0
            attention(nc, M, AttnPlan(0))

            with ExitStack() as o0:
                M.Wout = M.Wq[:].rearrange("p (h n) -> p h n", n=D)
                kv = M.Wkv
                small = o0.enter_context(nc.sbuf_tensor("small0", [P, 64], F32))
                M.lams, M.nlam, M.gam0 = small[:, 0:8], small[:, 8:9], small[:, 9:10]
                M.lamp = kv[:, 0:64].rearrange("p (a d) -> p a d", d=DH0)
                M.lam = kv[:, 64:192].rearrange("p (k d) -> p k d", d=DH0)
                M.blk = kv[:, 192:224]
                M.yT = [M.xb, o0.enter_context(nc.sbuf_tensor("yT1", [P, S], F32))]
                M.msb = M.sums
                M.csum = M.xT[:, 0:512].rearrange("p (k b c) -> p k b c", k=2, b=B)
                M.crec = M.xT[:, 512:768].rearrange("p (b c) -> p b c", b=B)
                M.cms = M.xT[:, 768:896].rearrange("p (b c) -> p b c", b=B)
                M.crms = kv[:, 512:640].rearrange("p (b c) -> p b c", b=B)
                M.n_ffn = 0

                def load_ffn(sp):
                    sp.dma_start(M.piwT, I["piwT"].rearrange("(n p) c -> p n c", p=P)).then_inc(M.ffn_in, 16)
                M.load_ffn = load_ffn
                l0_output(nc, M)

        if debug == "x1":
            return M
        with ExitStack() as fc:
            def sbf(name, shape, dt=F32):
                return fc.enter_context(nc.sbuf_tensor(name, shape, dt))
            M.patT = sbf("patT", [P, N_IN])
            M.oiwT = sbf("oiwT", [P, N_OUT])
            M.opat = sbf("opat", [P, N_OUT // P, D])
            M.pv = sbf("pv", [P, N_PROC // P, D_PV])
            M.sel = sbf("sel", [B, B * P])
            M.gb1 = sbf("gb1", [P, 2])
            M.actsum = sbf("actsum", [P, N_IN // P, B])
            M.junk = [sbf(f"junk{i}", [P, S]) for i in range(2)]
            M.rowa, M.rowb, M.rowc = (sbf(f"row{c}", [B, 1024]) for c in "abc")
            M.colb = sbf("colb", [P, 8 * B])
            M.tops = sbf("tops", [B, 16])
            M.aggT = sbf("aggT", [D_PV, B])
            M.res = sbf("res", [B, D])
            M.xn = [sbf(f"xn{i}", [P, TPB, D]) for i in range(2)]
            M.n_ffn = 1 + 6
            with nc.Block() as block:
                @block.sync
                def _(sp):
                    sp.dma_start(M.patT[:], I["patT"]).then_inc(M.ffn_in, 16)
                    sp.dma_start(M.oiwT[0:D_PV, :], I["oiwT"]).then_inc(M.ffn_in, 16)
                    sp.dma_start(M.opat[:], I["opat"].rearrange("(n p) c -> p n c", p=P)).then_inc(M.ffn_in, 16)
                    sp.dma_start(M.pv[:], I["pv"].rearrange("(n p) c -> p n c", p=P)).then_inc(M.ffn_in, 16)
                    sp.dma_start(M.sel[:], I["sel"]).then_inc(M.ffn_in, 16)
                    sp.dma_start(M.gb1[:], I["gb1"]).then_inc(M.ffn_in, 16)
            ffn(nc, M)
        if debug == "x2":
            return M
        with ExitStack() as l1:
            def sb1(name, shape, dt=F32):
                return l1.enter_context(nc.sbuf_tensor(name, shape, dt))
            M.fc = sb1("w_fc", [P, NX * FF])
            M.pr = sb1("w_proj", [P, NX * FF])
            M.Wo1 = sb1("Wo1", [P, D])
            M.rT = sb1("routerT", [P, NE])
            M.tri = sb1("tri", [P, NE * NE])
            M.comb = sb1("comb", [P, NT, NX])
            with ExitStack() as l1a:
                def sba(name, shape, dt=F32):
                    return l1a.enter_context(nc.sbuf_tensor(name, shape, dt))
                M.o = sba("o1", [P, 4, T])
                with ExitStack() as at:
                    def sbt(name, shape, dt=F32):
                        return at.enter_context(nc.sbuf_tensor(name, shape, dt))
                    M.Win = sbt("Win", [P, 3 * D])
                    M.WinR = sbt("WinR", [P, 2 * D])
                    M.cos, M.sin = sbt("cos", [P, S]), sbt("sin", [P, S])
                    M.bqk, M.bv, M.bo = sbt("bqk", [P, 4]), sbt("bv", [P, D]), sbt("bo", [P, D])
                    M.rot = sbt("rot", [P, 2, S])

                    def load_l1(sp, layer, sem):
                        pairs = [(M.Win, I["Win"]), (M.WinR, I["WinR"]), (M.cos, I["cos"]), (M.sin, I["sin"]),
                                 (M.bqk, I["bqk"])]
                        for dst, src in pairs:
                            sp.dma_start(dst[:], src).then_inc(sem, 16)
                        for dst, src in [(M.bv, I["bv"]), (M.bo, I["bo"])]:
                            sp.dma_start(dst[:], src.broadcast_to([P, D])).then_inc(sem, 16)
                        for e in range(NX):
                            w = I["fcT"][e] if e < NE else I["sfcT"]
                            sp.dma_start(M.fc[:, e * FF:(e + 1) * FF], w).then_inc(sem, 16)
                            w = I["prT"][e] if e < NE else I["sprT"]
                            sp.dma_start(M.pr[:, e * FF:(e + 1) * FF].rearrange("p (f d) -> p f d", d=D),
                                         w.rearrange("(f p) d -> p f d", p=P)).then_inc(sem, 16)
                        for dst, src in [(M.Wo1, I["Wo1"]), (M.rT, I["rT"]), (M.tri, I["tri"])]:
                            sp.dma_start(dst[:], src).then_inc(sem, 16)
                    M.n_weights[1] = 7 + 2 * NX + 3
                    M.load_weights = load_l1
                    attention(nc, M, AttnPlan(1))
                    if debug == "o1":
                        return M
                ringf = M.Pr[:].rearrange("p a b -> p (a b)")
                ring = ringf.bitcast(F16)
                NW = NX * FF
                M.fch, M.fcl = ring[:, 0:NW], ring[:, NW:2 * NW]
                M.prh = ring[:, 2 * NW:3 * NW]
                with ExitStack() as po:
                    def sbp(name, shape, dt=F32):
                        return po.enter_context(nc.sbuf_tensor(name, shape, dt))
                    M.rden = sbp("rden", [P, 16])
                    M.cx = [sbp(f"cx{i}", [P, D]) for i in range(2)]
                    M.cxT = [sbp(f"cxT{i}", [P, P]) for i in range(2)]
                    M.rt, M.rt1 = sbp("rt", [P, 2, NT, NE]), sbp("rt1", [P, 3, NT])
                    vv = M.V[:].rearrange("p a b -> p (a b)")
                    M.gt = vv[:, 0:1024].rearrange("p (t e j) -> p t e j", e=NE, j=NE)
                    M.eq = vv[:, 1024:2048].rearrange("p (t e j) -> p t e j", e=NE, j=NE)
                    qkf = M.qk[:].rearrange("p a b c -> p (a b c)")
                    M.xTh, M.xTl = qkf[:, 0:T], qkf[:, T:2 * T]
                    M.prl = sbp("prl", [P, NW], F16)
                    l1_output(nc, M)
                    of = M.o[:].rearrange("p g t -> p (g t)")
                    oh = of.bitcast(F16)
                    M.r = [of[:, i * S:(i + 1) * S] for i in range(2)]
                    M.sq = [of[:, (2 + i) * S:(3 + i) * S] for i in range(2)]
                    M.hh = [oh[:, (8 + i) * S:(9 + i) * S] for i in range(2)]
                    M.hl = [oh[:, (10 + i) * S:(11 + i) * S] for i in range(2)]
                    vn = M.Vn[:].rearrange("p a b -> p (a b)")
                    M.acc, M.xg, M.y = (vn[:, 512 * i:512 * (i + 1)].rearrange("p (t d) -> p t d", d=D) for i in range(3))
                    M.cg = vn[:, 1536:1536 + TPB * NX].rearrange("p (t e) -> p t e", e=NX)
                    if debug == "x3":
                        return M
                    moe(nc, M)
    return M


def kernel(**inputs):
    import concourse.bacc as bacc
    from concourse.bass_utils import run_bass_kernel_spmd

    def row(name):
        return np.asarray(inputs[name])

    def laid(a):
        return np.ascontiguousarray(a)

    x = row("L0_attn_x").reshape(T, D)
    Win = row("L1_attn_W_in")
    within = np.arange(DH1)
    within[:RD] = within[:RD].reshape(-1, 2)[:, ::-1].reshape(-1)
    swap = (np.arange(D).reshape(-1, DH1)[:, within]).reshape(-1)
    b_in = row("L1_attn_b_in")
    t = np.arange(S, dtype=np.float32)
    inv_freq = (np.float32(1.0) / np.power(np.float32(10000.0), np.arange(0, RD, 2, dtype=np.float32) / np.float32(RD)))
    freqs = np.repeat(t[:, None] * inv_freq[None, :].astype(np.float32), 2, axis=-1)
    cos = np.ones((DH1, S), np.float32)
    sin = np.zeros((DH1, S), np.float32)
    cos[:RD] = np.cos(freqs).T
    sin[:RD] = np.sin(freqs).T * np.where(np.arange(RD) % 2 == 0, -1.0, 1.0)[:, None]
    blk = np.zeros((P, 32), np.float32)
    blk[:DV0, 0] = 1.0 / DV0
    blk[DV0:, 1] = 1.0 / DV0
    sel = np.zeros((B, B * P), np.float32)
    for b in range(B):
        sel[b, b * P:(b + 1) * P] = 1.0
    arrays = {
        "x": laid(x), "xT": laid(x.T),
        "Wq": row("L0_attn_Wq"), "Wkv": row("L0_attn_Wkv"), "Wout": row("L0_attn_Wout"),
        "lam": laid(np.stack([row(f"L0_attn_lambda_{n}") for n in ("q1", "k1", "q2", "k2")])),
        "gamma0": laid(np.tile(row("L0_attn_gamma"), 2)[:, None]),
        "patT": laid(row("L0_ffn_input_patterns").T), "piwT": laid(row("L0_ffn_process_input_weights").T),
        "pv": row("L0_ffn_process_values"), "oiwT": laid(row("L0_ffn_output_input_weights").T),
        "opat": row("L0_ffn_output_patterns"),
        "Win": Win, "WinR": laid(np.concatenate([Win[:, :D][:, swap], Win[:, D:2 * D][:, swap]], axis=1)),
        "bqk": laid(np.stack([b_in[:D], b_in[D:2 * D], b_in[:D][swap], b_in[D:2 * D][swap]], axis=1)),
        "bv": laid(b_in[None, 2 * D:]), "bo": laid(row("L1_attn_b_out")[None]),
        "Wo1": row("L1_attn_W_out"),
        "gb1": laid(np.stack([row("L1_attn_gamma"), row("L1_attn_beta")], axis=1)),
        "rT": laid(row("L1_ffn_router_w").T),
        "fcT": laid(row("L1_ffn_w_fc").transpose(0, 2, 1)), "prT": laid(row("L1_ffn_w_proj").transpose(0, 2, 1)),
        "sfcT": laid(row("L1_ffn_shared_fc").T), "sprT": laid(row("L1_ffn_shared_proj").T),
        "ident": np.eye(P, dtype=np.float32), "eps": np.full((P, 1), EPS_LN, np.float32), "blk": blk, "sel": sel,
        "cos": laid(np.tile(cos, (D // DH1, 1))), "sin": laid(np.tile(sin, (D // DH1, 1))),
        "tri": laid(np.tile(np.tril(np.ones((NE, NE), np.float32), -1).reshape(1, -1), (P, 1))),
    }
    nc = bacc.Bacc("TRN2", target_bir_lowering=False, num_devices=1)
    maps, I = {}, {}
    for name, a in arrays.items():
        a = np.ascontiguousarray(a)
        maps[f"in_{name}"] = a
        I[name] = nc.dram_tensor(f"in_{name}", a.shape, mybir.dt.from_np(a.dtype), kind="ExternalInput").ap()
    out = nc.dram_tensor("out_0", (B, S, D), F32, kind="ExternalOutput").ap()
    build(nc, I, out)
    result = run_bass_kernel_spmd(nc, [maps], core_ids=[0])
    return result.results[0]["out_0"]
```

```python
from contextlib import ExitStack
import math

import numpy as np

import concourse.bass as bass
from concourse import mybir

F32 = mybir.dt.float32
F16 = mybir.dt.float16
ALU = mybir.AluOpType
ACT = mybir.ActivationFunctionType
AX = mybir.AxisListType

P = 128
D = 128
B = 4
S = 512
T = B * S
NT = T // P
TPB = S // P
BANK = 512
NQK = 16
H0, DH0, DV0 = 8, 32, 64
DH1 = 8
RD = DH1 // 2
LAMBDA_INIT = 0.8 - 0.6 * math.exp(-0.3)
SROWS = 96
PRING = 16
N_IN, N_PROC, N_OUT, D_PV = 1024, 512, 1024, 64
K_IN, K_PROC, K_OUT = N_IN // 8, N_PROC // 8, N_OUT // 8
NE, FF = 8, 512
NX = NE + 1
WSCALE = 64.0
MSHIFT = -3.0e38
EPS_LN, EPS_RMS = 1e-5, 1e-8


class Links:

    def __init__(self, eng, sem, base=0):
        self.eng, self.sem, self.base, self.n = eng, sem, base, 0

    def __call__(self, ins):
        self.n += 1
        ins.then_inc(self.sem, 1)
        self.eng.wait_ge(self.sem, self.base + self.n)


class AttnPlan:

    def __init__(self, layer):
        self.layer = layer
        self.J = 2 if layer == 0 else 4
        self.W = NQK // self.J
        self.dh = DH0 if layer == 0 else DH1
        self.scale = self.dh ** -0.5
        self.nd = 6
        self.ring_steps = PRING // self.J
        self.credit = self.ring_steps - 3 if layer == 0 else self.ring_steps
        if layer == 0:
            self.pieces = {(0, 2): "q0", (1, 2): "k0", (2, 2): "v0", (3, 2): "v1", (4, 2): "q1", (5, 2): "k1"}
            self.vcopies = {1: (3, 0), 6: (0, 16), 7: (2, 24)}
            self.vregions = {1: [3], 6: [0, 1], 7: [2]}
            self.bounces = {2: 0, 6: 1}
            self.last_v = 6
            self.banks = (6, 6)
        else:
            self.pieces = {}
            self.proj = {(0, 0, 0): 0, (0, 0, 1): 1, (0, 1, 0): 2, (0, 1, 1): 3, (0, 2, 1): 4}
            self.last_v = 3
            self.banks = (6, 7)
        self.NP = len(self.pieces)
        self.per_window = 2 * self.J + 1
        self.U0 = self.NP + 2 * self.per_window - 1
        self.UB = self.W * self.per_window + self.NP
        assert self.UB % 2 == 0

    @staticmethod
    def stack_rows(M):
        return [(M.Qs, 0, 0), (M.Qs, 1, 0), (M.Qs, 2, 1), (M.Ks, 0, 2), (M.Ks, 1, 3), (M.Ks, 2, 2)]

    def before(self, w, last):
        return w * self.per_window + (0 if last else sum(1 for p in self.pieces if p[0] < w))

    def use(self, w, s, kind, i=0, last=False):
        n = self.before(w, last)
        ahead = not (last and w >= self.W - 2)
        for step in range(4):
            for pair in range(self.J // 2 if ahead else 0):
                if kind == "sm" and (step, pair) == (s, i):
                    return n
                n += 1
            if step == 0:
                if kind == "tr":
                    return n
                n += 1
            if not last and (w, step) in self.pieces:
                if kind == "piece" and step == s:
                    return n
                n += 1

    def bank(self, base, local):
        return 2 * (((base if isinstance(base, int) else self.U0) + local) % 2)


def attention(nc, M, plan):
    A, L, J, W = plan, plan.layer, plan.J, plan.W
    PS = M.PS
    ctx = ExitStack()

    def sem(name, layer=plan.layer):
        return ctx.enter_context(nc.semaphore(f"l{L}_{name}")) if layer == L else None

    with ctx:
        weights_in = sem("weights_in", 0)
        xb_in = sem("xb_in")
        stack_in = [sem(f"stack_in{g}") for g in range(2 if L == 0 else W)]
        bounce_out = [sem(f"bounce_out{h}") for h in range(2 - L)]
        all_in = sem("all_in", 1)
        max_in = [sem(f"max_in{p}") for p in range(2)]
        sums_out = [sem(f"sums_out{p}", 0) for p in range(2)]
        sm_ready = sem("sm_ready")
        sm_free = sem("sm_free")
        st_ready = sem("st_ready")
        exp_done = sem("exp_done")
        added = sem("added", 0)
        pv_done = sem("pv_done")
        o_evac = sem("o_evac")
        sums_evac = sem("sums_evac", 0)
        hi_done = sem("hi_done", 0)
        v_copied = sem("v_copied")
        own = sem("own")
        pool_own = sem("pool_own")
        carried = sem("carried")
        pool_carried = sem("pool_carried")
        ready = sem("ready", 0)
        csum_in = sem("csum_in", 0)
        factors = sem("factors", 0)
        r_out = sem("r_out", 0)
        r_in = sem("r_in", 0)
        divided = sem("divided", 0)
        proj_ready = sem("proj_ready", 1)
        proj_out = sem("proj_out", 1)
        q_split = sem("q_split", 1)
        k_split = sem("k_split", 1)
        v_next = sem("v_next", 1)
        doubled = sem("doubled", 1)
        lam_e = sem("lam_e", 0)
        block = ctx.enter_context(nc.Block())

        piece_order = list(A.pieces.values())

        @block.sync
        def _(sp):
            def load_xb(b):
                if L == 0:
                    sp.dma_start(M.xb[:], M.xT_dram[:, bass.ds(b * S, S)]).then_inc(xb_in, 16)
                else:
                    sp.dma_start(M.xb[:], M.xT[:, bass.ds(b * S, S)]).then_inc(xb_in, 16)

            def wait(s, value):
                sp.wait_ge(s, value)
                if not isinstance(value, int):
                    sp.sem_inc(carried, 1)

            def bounce(h, n):
                if L == 0:
                    sp.dma_start(M.qk0_dram[h].rearrange("k (c p) t -> p (k c) t", p=P), M.qk[:, h].rearrange("p k c t -> p (k c) t"))\
                      .then_inc(bounce_out[h], 16)
                else:
                    sp.dma_start(M.qk_dram.rearrange("k p t -> p k t"), M.qk[:, 0, :, 0, :]).then_inc(bounce_out[h], 16)
                wait(bounce_out[h], 16 * (n + 1))

            def load_stack(g):
                for stack, blk, part in A.stack_rows(M):
                    if L == 0:
                        n, src = NQK // 2, M.qk0_dram[g, part]
                    else:
                        n, src = J, M.qk_dram[part, g * J * DH1:(g + 1) * J * DH1, :]
                    sp.dma_start(stack[A.dh * blk:A.dh * (blk + 1), g * n:(g + 1) * n, :],
                                 src.rearrange("(h p) t -> p h t", p=A.dh)).then_inc(stack_in[g], 16)

            def max_row(u, g, par):
                wait(sm_free, u + 1)
                sp.dma_start(M.Qs[SROWS:SROWS + 1, g * J:(g + 1) * J, :], M.mrow[par][0:4 * J, :])\
                  .then_inc(max_in[par], 16)

            load_xb(0)
            if L == 0:
                M.load_weights(sp, weights_in)
                for par in range(2):
                    sp.sem_inc(sums_out[par], 1)
            if L == 0:
                for h in range(2):
                    sp.wait_ge(sm_free, (2, 6)[h])
                    bounce(h, 0)
                    load_stack(h)
            else:
                sp.wait_ge(q_split, 1)
                sp.wait_ge(k_split, 1)
                bounce(0, 0)
                for stack, blk, part in A.stack_rows(M):
                    sp.dma_start(stack[A.dh * blk:A.dh * (blk + 1), :, :],
                                 M.qk_dram[part].rearrange("(h p) t -> p h t", p=A.dh)).then_inc(all_in, 16)
                sp.wait_ge(all_in, 16 * A.nd)
                for g in range(W):
                    sp.sem_inc(stack_in[g], 16 * A.nd)
            max_row(A.NP + A.per_window - 1, 0, 0)

            def batch(b, first, last):
                base, stb = A.U0 + b * A.UB, 4 * J * W * b
                if not last:
                    if L == 0:
                        wait(sm_free, base - 1)
                    else:
                        wait(proj_out, 5 * (b + 1))
                    load_xb(b + 1)
                for w in range(W):
                    if not (last and w == W - 1):
                        max_row(base + A.use(w, 0, "tr", last=last), (w + 1) % W, (w + 1) % 2)
                    if L == 0 and w == 0 and not first:
                        wait(st_ready, stb)
                        load_stack(1)
                    if L == 0 and w == 4 and not last:
                        wait(st_ready, stb + 4 * J * 4)
                        load_stack(0)
                    if L == 0 and not first and w == 1:
                        for par in range(2):
                            wait(sums_out[par], 1 + 16 * (W // 2 * b))
                        sp.dma_start(M.csum[:], M.sums_dram[bass.ds(b - 1, 1)].rearrange("o g j (a c) -> (o g j a) c", c=64))\
                          .then_inc(csum_in, 16)
                    if L == 0 and not first and w == 2:
                        wait(factors, b)
                        sp.dma_start(M.r_dram[bass.ds(b - 1, 1)].rearrange("o (p c) -> (o p) c", c=64), M.crec[:])\
                          .then_inc(r_out, 16)
                        wait(r_out, 16 * b)
                        wait(divided, 1 + 12 * (b - 1))
                        for half in range(2):
                            for j in range(2):
                                src = M.r_dram[bass.ds(b - 1, 1)].rearrange("o (h s j q) -> o j s h q", h=4, s=2, j=2)
                                sp.dma_start(M.rsum[half][64 * j:64 * j + 64], src[:, j, half].broadcast_to([64, 4, S]))\
                                  .then_inc(r_in, 16)
                    if L == 0 and not last and w in A.bounces:
                        h = A.bounces[w]
                        wait(sm_free, base + A.use(1 + 4 * h, 2, "piece") + 1)
                        wait(stack_in[h], 16 * A.nd * (b + 1))
                        bounce(h, b + 1)
                    if L == 1 and not last:
                        if w == 0:
                            wait(q_split, b + 2)
                            wait(k_split, b + 2)
                            for g in range(W):
                                wait(stack_in[g], 16 * A.nd * (b + 1))
                            bounce(0, b + 1)
                        wait(st_ready, stb + 4 * J * (w + 1))
                        load_stack(w)
                    if L == 0:
                        wait(sums_evac, 1 + W * b + w + 1)
                        sp.dma_start(M.sums_dram[bass.ds(b, 1), w].rearrange("a t q -> (a t) q"),
                                     M.sums[w % 2][0:2 * 32:32, :]).then_inc(sums_out[w % 2], 16)

            batch(0, True, False)
            with sp.Fori(1, B - 1) as b:
                batch(b, False, False)
            batch(B - 1, False, True)
            if L == 0:
                for par in range(2):
                    sp.wait_ge(sums_out[par], 1 + 16 * B * W // 2)

        @block.gpsimd
        def _(pool):
            def wait(s, value):
                pool.wait_ge(s, value)
                if not isinstance(value, int):
                    pool.sem_inc(pool_carried, 1)

            if L == 0:
                nc.gpsimd.memset(M.ones[:], 1.0).then_inc(pool_own, 1)
                wait(pool_own, 1)
                nc.gpsimd.memset(M.Ks[SROWS:SROWS + 1], 1.0).then_inc(ready, 1)
                pool.sem_inc(divided, 1)

                def batch(b, first, last):
                    n = 0
                    steps = 4 * W * b
                    own0 = 1 + W * b
                    for w in range(W):
                        wait(pv_done, A.credit + steps + 4 * (w - 1))
                        wait(exp_done, J * (steps + 4 * w + 2))
                        for j in range(J):
                            a, c = ((4 * w + i) * J + j for i in range(2))
                            ins = nc.gpsimd.tensor_tensor(M.esum[w % 2][:, j, :], M.Pr[:, a % PRING, :],
                                                          M.Pr[:, c % PRING, :], ALU.add)
                        ins.then_inc(pool_own, 1)
                        n += 1
                        wait(pool_own, own0 + n)
                        wait(exp_done, J * (steps + 4 * w + 3))
                        for j in range(J):
                            c = (4 * w + 2) * J + j
                            ins = nc.gpsimd.tensor_tensor(M.esum[w % 2][:, j, :], M.esum[w % 2][:, j, :],
                                                          M.Pr[:, c % PRING, :], ALU.add)
                        ins.then_inc(added, 1)
                        if first or w < 2:
                            continue
                        for i in (2 * (w - 2), 2 * (w - 2) + 1):
                            hp, kind = i // 3, i % 3
                            o = [M.o[:, half, hp, bass.ds((b - 1) * S, S)] for half in range(2)]
                            if i == 0:
                                wait(o_evac, 1 + W * b)
                                wait(r_in, 64 * b)
                            if kind < 2:
                                ins = nc.gpsimd.tensor_tensor(o[kind], o[kind], M.rsum[kind][:, hp, :], ALU.mult)
                            else:
                                wait(divided, 1 + 12 * (b - 1) + i)
                                ins = nc.gpsimd.tensor_tensor(o[0], o[0], o[1], ALU.add)
                            ins.then_inc(divided, 1)

                batch(0, True, False)
                with pool.Fori(1, B - 1) as b:
                    batch(b, False, False)
                batch(B - 1, False, True)
            else:
                def turn_q(n):
                    raw = M.raw
                    wait(proj_out, 5 * n + 2)
                    nc.gpsimd.tensor_tensor(M.raw[:, 0, :], M.raw[:, 0, :], M.cos[:], ALU.mult)
                    nc.gpsimd.tensor_tensor(M.raw[:, 1, :], M.raw[:, 1, :], M.sin[:], ALU.mult).then_inc(pool_own, 1)
                    wait(pool_own, 3 * n + 1)
                    nc.gpsimd.tensor_tensor(M.raw[:, 0, :], M.raw[:, 0, :], M.raw[:, 1, :], ALU.add).then_inc(pool_own, 1)
                    wait(pool_own, 3 * n + 2)
                    if not (isinstance(n, int) and n == 0):
                        wait(bounce_out[0], 16 * n)
                    nc.gpsimd.tensor_copy(M.qk[:, 0, 0, 0, :], M.raw[:, 0, :]).then_inc(pool_own, 1)
                    wait(pool_own, 3 * n + 3)
                    nc.gpsimd.tensor_tensor(M.qk[:, 0, 1, 0, :], M.raw[:, 0, :], M.qk[:, 0, 0, 0, :], ALU.subtract)\
                      .then_inc(q_split, 1)

                def take_v(n):
                    wait(proj_out, 5 * n + 5)
                    if not (isinstance(n, int) and n == 0):
                        wait(v_copied, 4 * n)
                    nc.gpsimd.tensor_tensor(
                        M.Vn[:].rearrange("p k (h e) -> p k h e", e=32)[:, :, :, 0:DH1],
                        M.raw[:, 4, :].rearrange("p (k h e) -> p k h e", k=4, e=DH1),
                        M.bv[:].rearrange("p (k h e) -> p k h e", k=1, e=DH1).broadcast_to([P, 4, NQK, DH1]),
                        ALU.add).then_inc(v_next, 1)

                def copy_v(region):
                    cols = (slice(None), slice(None), slice(4 * region, 4 * region + 4), slice(0, DH1))
                    nc.gpsimd.tensor_copy(M.V[:].rearrange("p k (h e) -> p k h e", e=32)[cols],
                                          M.Vn[:].rearrange("p k (h e) -> p k h e", e=32)[cols]).then_inc(v_copied, 1)

                turn_q(0)
                wait(own, 3)
                take_v(0)
                wait(v_next, 1)
                for region in range(3):
                    copy_v(region)
                def batch(b, first, last):
                    wait(pv_done, A.credit + 4 * W * b)
                    copy_v(3)
                    if last:
                        return
                    turn_q(b + 1)
                    take_v(b + 1)
                    wait(v_next, b + 2)
                    wait(pv_done, A.credit + 4 * W * b + 12)
                    for region in range(3):
                        copy_v(region)

                with pool.Fori(0, B - 1) as b:
                    batch(b, False, False)
                batch(B - 1, False, True)
                nc.gpsimd.tensor_tensor(M.x[:], M.x[:], M.x[:], ALU.add).then_inc(doubled, 1)
                wait(doubled, 1)
                nc.gpsimd.tensor_tensor(M.x[:], M.x[:], M.bo[:].rearrange("p (o d) -> p o d", o=1).broadcast_to([P, NT, D]),
                                        ALU.add)

        @block.tensor
        def _(pe):
            pe.sem_inc(pv_done, A.credit)
            if L == 0:
                pe.wait_ge(weights_in, 16 * M.n_l0)

            def free(base, local):
                u = base + local
                if not (isinstance(u, int) and u < 2):
                    pe.wait_ge(sm_free, u - 1)
                return A.bank(base, local)

            def score_max(base, local, g, qt, pair):
                bank = free(base, local)
                for i in range(2):
                    slot = g * J + 2 * pair + i
                    mm = pe.matmul(PS[:, bank + i, :], M.Qs[0:SROWS, slot, qt * P:(qt + 1) * P],
                                   M.Ks[0:SROWS, slot, :], start=True, stop=True)
                mm.then_inc(sm_ready, 1)

            def turn_max(base, local, par, written):
                pe.wait_ge(sm_free, base + written)
                bank = free(base, local)
                pe.transpose(PS[0:4 * J, bank, 0:P], M.negm[:, par, 0:4 * J], M.ident[:]).then_inc(sm_ready, 1)

            def piece(base, local, name, nb):
                pe.wait_ge(xb_in, 16 * (nb + 1))
                bank = free(base, local)
                for i in range(2):
                    c = 2 * int(name[1]) + i
                    if name[0] == "v":
                        mm = pe.matmul(PS[:, bank + i, :], M.xb[:, c * P:(c + 1) * P], M.Wkv[:, 512:1024],
                                       start=True, stop=True)
                    else:
                        w_ = (M.Wq if name[0] == "q" else M.Wkv)[:, c * P:(c + 1) * P]
                        mm = pe.matmul(PS[:, bank + i, :], w_, M.xb[:], start=True, stop=True)
                mm.then_inc(sm_ready, 1)

            def project(i, nb):
                pe.wait_ge(xb_in, 16 * (nb + 1))
                if i == 0 and not (isinstance(nb, int) and nb == 0):
                    pe.wait_ge(o_evac, 1 + W * (nb - 1))
                if not (isinstance(nb, int) and nb == 0 and i == 0):
                    pe.wait_ge(proj_out, 5 * nb + i)
                if i < 4:
                    w_ = (M.WinR if i % 2 else M.Win)[:, (i // 2) * D:(i // 2 + 1) * D]
                    mm = pe.matmul(PS[:, 7, :], w_, M.xb[:], start=True, stop=True)
                else:
                    for c in range(4):
                        mm = pe.matmul(PS[:, 7, c * D:(c + 1) * D], M.xb[:, c * P:(c + 1) * P], M.Win[:, 2 * D:3 * D],
                                       start=True, stop=True)
                mm.then_inc(proj_ready, 1)

            def score_t(k, b, j):
                w, kt = k // 4, k % 4
                n, slot = k * J + j, w * J + j
                nb = 4 * W * J * b + n
                if not (isinstance(nb, int) and nb < 2):
                    pe.wait_ge(exp_done, nb - 1)
                if j == 0 and kt == 0:
                    pe.wait_ge(max_in[w % 2], 16 * (W // 2 * b + w // 2 + 1))
                pe.matmul(PS[:, 4 + n % 2, :], M.Ks[0:SROWS + 1, slot, kt * P:(kt + 1) * P],
                          M.Qs[0:SROWS + 1, slot, :], start=True, stop=True).then_inc(st_ready, 1)

            def product(k, b, heads, last):
                w, kt = k // 4, k % 4
                bank = A.banks[w % 2]
                if kt == 0 and heads[0] == 0:
                    pe.wait_ge(o_evac, (1 if L == 0 else 2) + W * b + w - (0 if L == 0 else 1))
                    if L == 1 and w == 1:
                        pe.wait_ge(proj_out, 5 * (b + (1 if last else 2)))
                    if w in (0, A.last_v):
                        pe.wait_ge(v_copied, 3 + 4 * b + (1 if w else 0))
                for j in heads:
                    slot = (k * J + j) % PRING
                    pe.wait_ge(exp_done, 4 * W * J * b + J * k + j + 1)
                    if L == 0:
                        hp = w // 2
                        mm = pe.matmul(PS[64 * j:64 * j + 64, bank, :],
                                       M.V[:, kt, hp * P + DV0 * j:hp * P + DV0 * (j + 1)], M.Pr[:, slot, :],
                                       start=(kt == 0), stop=(kt == 3), skip_group_check=True)
                    else:
                        h = w * J + j
                        mm = pe.matmul(PS[32 * j:32 * j + 32, bank, :], M.V[:, kt, 32 * h:32 * h + 32], M.Pr[:, slot, :],
                                       start=(kt == 0), stop=(kt == 3), skip_group_check=True)
                if L == 0 and kt == 3:
                    pe.wait_ge(sums_evac, 1 + W * b + w)
                    for j in range(J):
                        pe.matmul(PS[32 * j:32 * j + 32, 7, :], M.ones[:, 0:32], M.Pr[:, (k * J + j) % PRING, :],
                                  start=True, stop=False, skip_group_check=True)
                    pe.wait_ge(added, W * b + w + 1)
                    for j in range(J):
                        mm = pe.matmul(PS[32 * j:32 * j + 32, 7, :], M.ones[:, 0:32], M.esum[w % 2][:, j, :],
                                       start=False, stop=True, skip_group_check=True)
                if heads[-1] == J - 1:
                    mm.then_inc(pv_done, 1)

            if L == 0:
                pe.wait_ge(ready, 1)
                for i, name in enumerate(piece_order):
                    piece(0, i, name, 0)
            else:
                for i in range(5):
                    project(i, 0)
            for g in range(2):
                pe.wait_ge(stack_in[0 if L == 0 else g], 16 * A.nd)
                for qt in range(4):
                    for pair in range(J // 2):
                        score_max(0, A.NP + g * A.per_window + qt * (J // 2) + pair, g, qt, pair)
                if g == 0:
                    turn_max(0, A.NP + A.per_window - 1, 0, A.NP + A.per_window - 1)
            for j in range(J):
                score_t(0, 0, j)

            def batch(b, last):
                base = A.U0 + b * A.UB
                for k in range(4 * W):
                    w, s = k // 4, k % 4
                    ahead = not (last and w >= W - 2)
                    g = (w + 2) % W
                    nk, nb = (k + 1) % (4 * W), b if k < 4 * W - 1 else b + 1
                    if ahead and s == 0 and (L == 1 or g % 4 == 0):
                        pe.wait_ge(stack_in[g // 4 if L == 0 else g], 16 * A.nd * (b + (2 if w + 2 >= W else 1)))
                    scores_left = not (last and k == 4 * W - 1)
                    turn_due = s == 0 and not (last and w == W - 1)
                    turn = A.use(w, 0, "tr", last=last) if turn_due else None
                    written = turn - (J // 2 if ahead else 0) if turn_due else None
                    if L == 0:
                        if scores_left:
                            score_t(nk, nb, 0)
                        if ahead:
                            score_max(base, A.use(w, s, "sm", 0, last), g, s, 0)
                        if scores_left:
                            score_t(nk, nb, 1)
                        if not last and (w, s) in A.pieces:
                            piece(base, A.use(w, s, "piece"), A.pieces[(w, s)], b + 1)
                        product(k, b, (0, 1), last)
                    else:
                        for place in range(2):
                            if scores_left:
                                score_t(nk, nb, 2 * place)
                            if ahead:
                                score_max(base, A.use(w, s, "sm", place, last), g, s, place)
                            if scores_left:
                                score_t(nk, nb, 2 * place + 1)
                            product(k, b, (2 * place, 2 * place + 1), last)
                            if not last and (w, s, place) in A.proj:
                                project(A.proj[(w, s, place)], b + 1)
                    if turn_due:
                        turn_max(base, turn, (w + 1) % 2, written)

            with pe.Fori(0, B - 1) as b:
                batch(b, False)
            batch(B - 1, True)

        @block.scalar
        def _(act):
            def exp(k, b, j):
                n = k * J + j
                act.wait_ge(st_ready, 4 * W * J * b + n + 1)
                if j == 0:
                    act.wait_ge(pv_done, 4 * W * b + k + 1)
                nc.scalar.activation(M.Pr[:, n % PRING, :], PS[:, 4 + n % 2, :], ACT.Exp, scale=A.scale)\
                  .then_inc(exp_done, 1)

            def high_parts(base, local, name):
                u = base + local
                bank = A.bank(base, local)
                act.wait_ge(sm_ready, u + 1)
                part = 0 if name[0] == "q" else 2
                nc.scalar.activation(M.qk[:, int(name[1]), part], PS[:, bank:bank + 2, :], ACT.Copy).then_inc(hi_done, 1)

            def take_projection(i, nb):
                act.wait_ge(proj_ready, 5 * nb + i + 1)
                if not (isinstance(nb, int) and nb == 0):
                    if i == 0:
                        act.wait_ge(q_split, nb)
                    elif i == 2:
                        act.wait_ge(k_split, nb)
                    elif i == 4:
                        act.wait_ge(v_next, nb)
                if i < 4:
                    bias = M.bqk[:, (0, 2, 1, 3)[i]:(0, 2, 1, 3)[i] + 1]
                    nc.scalar.activation(M.raw[:, i, :], PS[:, 7, :], ACT.Identity, bias=bias).then_inc(proj_out, 1)
                else:
                    nc.scalar.activation(M.raw[:, i, :], PS[:, 7, :], ACT.Copy).then_inc(proj_out, 1)

            if L == 0:
                act.wait_ge(weights_in, 16 * M.n_l0)
                act.wait_ge(own, 2)
                nc.scalar.activation(M.lams[:, 2:4], M.lams[:, 0:2], ACT.Exp).then_inc(lam_e, 1)
                for i, name in enumerate(piece_order):
                    if name[0] in "qk":
                        high_parts(0, i, name)
            else:
                for i in range(5):
                    take_projection(i, 0)
            for j in range(J):
                exp(0, 0, j)
            act.sem_inc(o_evac, 1)
            if L == 0:
                act.sem_inc(sums_evac, 1)

            def batch(b, last):
                base = A.U0 + b * A.UB
                for k in range(4 * W):
                    w, s = k // 4, k % 4
                    for j in range(J):
                        if k < 4 * W - 1:
                            exp(k + 1, b, j)
                        elif not last:
                            exp(0, b + 1, j)
                        if L == 1 and not last and j % 2 == 1 and (w, s, j // 2) in A.proj:
                            take_projection(A.proj[(w, s, j // 2)], b + 1)
                    if L == 0 and not last and (w, s) in A.pieces and A.pieces[(w, s)][0] in "qk":
                        name = A.pieces[(w, s)]
                        act.wait_ge(bounce_out[int(name[1])], 16 * (b + 1))
                        high_parts(base, A.use(w, s, "piece"), name)
                    if s == 3:
                        act.wait_ge(pv_done, A.credit + 4 * W * b + k + 1)
                        if L == 0:
                            nc.scalar.activation(M.o[:, w % 2, w // 2, bass.ds(b * S, S)], PS[:, 6, :], ACT.Copy)\
                              .then_inc(o_evac, 1)
                            act.wait_ge(sums_out[w % 2], 1 + 16 * (W // 2 * b + w // 2))
                            nc.scalar.activation(M.sums[w % 2][0:64, :], PS[0:64, 7, :], ACT.Copy).then_inc(sums_evac, 1)
                        else:
                            nc.scalar.activation(M.o[:, w, bass.ds(b * S, S)], PS[:, A.banks[w % 2], :], ACT.Copy)\
                              .then_inc(o_evac, 1)

            with act.Fori(0, B - 1) as b:
                batch(b, False)
            batch(B - 1, True)

        @block.vector
        def _(dve):
            def reduce(base, local, par, qt, pair):
                bank = A.bank(base, local)
                dve.wait_ge(sm_ready, base + local + 1)
                cols = M.negm[:, par, 8 * pair:8 * pair + 8].rearrange("p (j q) -> p j q", q=4)[:, :, qt]
                nc.vector.tensor_reduce(cols, PS[:, bank:bank + 2, :], AX.X, ALU.max, negate=True).then_inc(sm_free, 1)

            def take_row(base, local, par, count):
                bank = A.bank(base, local)
                dve.wait_ge(sm_ready, base + local + 1)
                if not (isinstance(count, int) and count == 0):
                    dve.wait_ge(max_in[par], 16 * count)
                nc.vector.tensor_copy(M.mrow[par][0:4 * J, :], PS[0:4 * J, bank, 0:P]).then_inc(sm_free, 1)

            def piece(base, local, name, hi_count):
                bank = A.bank(base, local)
                dve.wait_ge(sm_ready, base + local + 1)
                c = 2 * int(name[1])
                if name[0] == "v":
                    nc.vector.tensor_copy(M.Vn[:, c:c + 2, :], PS[:, bank:bank + 2, :]).then_inc(sm_free, 1)
                else:
                    part = 0 if name[0] == "q" else 2
                    dve.wait_ge(hi_done, hi_count)
                    nc.vector.tensor_tensor(M.qk[:, int(name[1]), part + 1], PS[:, bank:bank + 2, :],
                                            M.qk[:, int(name[1]), part], ALU.subtract).then_inc(sm_free, 1)

            def turn_k(i, n, own0):
                raw = M.raw
                if i == 0:
                    dve.wait_ge(proj_out, 5 * n + 3)
                    nc.vector.tensor_tensor(raw[:, 2, :], raw[:, 2, :], M.cos[:], ALU.mult).then_inc(own, 1)
                elif i == 1:
                    dve.wait_ge(proj_out, 5 * n + 4)
                    nc.vector.tensor_tensor(raw[:, 3, :], raw[:, 3, :], M.sin[:], ALU.mult).then_inc(own, 1)
                elif i == 2:
                    dve.wait_ge(own, own0 + 2)
                    nc.vector.tensor_tensor(raw[:, 2, :], raw[:, 2, :], raw[:, 3, :], ALU.add).then_inc(own, 1)
                elif i == 3:
                    dve.wait_ge(own, own0 + 3)
                    if not (isinstance(n, int) and n == 0):
                        dve.wait_ge(bounce_out[0], 16 * n)
                    nc.vector.tensor_copy(M.qk[:, 0, 2, 0, :], raw[:, 2, :]).then_inc(own, 1)
                else:
                    dve.wait_ge(own, own0 + 4)
                    nc.vector.tensor_tensor(M.qk[:, 0, 3, 0, :], raw[:, 2, :], M.qk[:, 0, 2, 0, :], ALU.subtract)\
                      .then_inc(k_split, 1)

            def copy_v(region):
                cols = slice(region * P, (region + 1) * P)
                nc.vector.tensor_copy(M.V[:, :, cols], M.Vn[:, :, cols]).then_inc(v_copied, 1)

            hi0 = 4
            if L == 0:
                link = Links(dve, own)
                dve.wait_ge(weights_in, 16 * M.n_l0)
                link(nc.vector.tensor_tensor(M.lamp[:], M.lam[:].rearrange("p (a b) d -> p a b d", b=2)[:, :, 0, :],
                                             M.lam[:].rearrange("p (a b) d -> p a b d", b=2)[:, :, 1, :], ALU.mult))
                link(nc.vector.tensor_reduce(M.lams[:, 0:2], M.lamp[:], AX.X, ALU.add))
                dve.wait_ge(lam_e, 1)
                link(nc.vector.tensor_tensor(M.lams[:, 4:5], M.lams[:, 3:4], M.lams[:, 2:3], ALU.subtract))
                link(nc.vector.tensor_scalar(M.nlam[:], M.lams[:, 4:5], -LAMBDA_INIT, None, ALU.add))
                link(nc.vector.scalar_tensor_tensor(out=M.sign[:, 0:1], in0=M.sign[:, 2:3], scalar=M.nlam[:, 0:1],
                                                    in1=M.sign[:, 1:2], op0=ALU.mult, op1=ALU.add))
                hi = 0
                for i, name in enumerate(piece_order):
                    if name[0] in "qk":
                        hi += 1
                    piece(0, i, name, hi)
                dve.wait_ge(sm_free, 6)
                for region in range(3):
                    copy_v(region)
            else:
                nc.vector.memset(M.Vn[:], 0.0).then_inc(own, 1)
                dve.wait_ge(own, 1)
                nc.vector.memset(M.Vn[:].rearrange("p k (h e) -> p k h e", e=32)[:, :, :, DH1], 1.0).then_inc(own, 1)
                dve.wait_ge(own, 2)
                nc.vector.tensor_copy(M.V[:], M.Vn[:]).then_inc(own, 1)
                for i in range(5):
                    turn_k(i, 0, 3)
            for g in range(2):
                for qt in range(4):
                    for pair in range(J // 2):
                        reduce(0, A.NP + g * A.per_window + qt * (J // 2) + pair, g, qt, pair)
                if g == 0:
                    take_row(0, A.NP + A.per_window - 1, 0, 0)

            def batch(b, first, last):
                base = A.U0 + b * A.UB
                hi, ni = 0, 0
                for w in range(W):
                    for s in range(4):
                        for pair in range(J // 2):
                            if not (last and w >= W - 2):
                                reduce(base, A.use(w, s, "sm", pair, last), w % 2, s, pair)
                            if L == 1 and not last:
                                place = 8 * w + 2 * s + pair
                                if 3 <= place < 8:
                                    turn_k(place - 3, b + 1, 3 + 4 * (b + 1))
                        if s == 0 and not (last and w == W - 1):
                            take_row(base, A.use(w, 0, "tr", last=last), (w + 1) % 2, W // 2 * b + (w + 1) // 2)
                        if L == 1:
                            continue
                        if s == 0 and w == 2 and not first:
                            dve.wait_ge(csum_in, 16 * b)
                            nc.vector.reciprocal(M.crec[:], M.csum[:]).then_inc(own, 1)
                            dve.wait_ge(own, 5 + b)
                            nc.vector.tensor_scalar(M.crec[:], M.crec[:], M.sign[:, 0:1], None, ALU.mult).then_inc(factors, 1)
                        if s == 2 and w in A.vcopies and not (last and w > 1):
                            dve.wait_ge(pv_done, A.credit + 4 * W * b + A.vcopies[w][1])
                            if w > 1:
                                vl = max(p for p in A.pieces if A.pieces[p][0] == "v")
                                dve.wait_ge(sm_free, base + A.use(*vl, "piece") + 1)
                            for region in A.vregions[w]:
                                copy_v(region)
                        if not last and (w, s) in A.pieces:
                            name = A.pieces[(w, s)]
                            if name[0] in "qk":
                                hi += 1
                            piece(base, A.use(w, s, "piece"), name, hi0 + b * hi0 + hi)
                            ni += 1

            batch(0, True, False)
            with dve.Fori(1, B - 1) as b:
                batch(b, False, False)
            batch(B - 1, False, True)


def spread(ap, n):
    p, a = ap.shape
    return ap.rearrange("p (a o) -> p a o", o=1).broadcast_to([p, a, n])


def l0_output(nc, M):
    PS = M.PS
    HP = H0 // 2
    NTI = N_IN // P
    ctx = ExitStack()

    def sem(name):
        return ctx.enter_context(nc.semaphore(f"out0_{name}"))

    with ctx:
        w_in = sem("w_in")
        x_in = sem("x_in")
        csum_in = sem("csum_in")
        factors = sem("factors")
        r_out = sem("r_out")
        r_in = sem("r_in")
        own = sem("own")
        diff = sem("diff")
        sq = sem("sq")
        ms = sem("ms")
        rms = sem("rms")
        inv = sem("inv")
        spr = sem("spr")
        normed = sem("normed")
        yT = sem("yT")
        yT_c = sem("yT_c")
        y = sem("y")
        var = sem("var")
        std = sem("std")
        x1 = sem("x1")
        x1T = sem("x1T")
        x1T_c = sem("x1T_c")
        acts = sem("acts")
        gelu = sem("gelu")
        block = ctx.enter_context(nc.Block())

        @block.sync
        def _(sp):
            sp.dma_start(M.csum[:], M.sums_dram[B - 1].rearrange("g j (a c) -> (g j a) c", c=64)).then_inc(csum_in, 16)
            sp.dma_start(M.gam0[:], M.gamma0_dram).then_inc(w_in, 16)
            sp.dma_start(M.Wout[:], M.Wout_dram.rearrange("(h p) n -> p h n", p=P)).then_inc(w_in, 16)
            sp.dma_start(M.blk[:], M.blk_dram).then_inc(w_in, 16)
            sp.dma_start(M.spread[:], M.spread_dram).then_inc(w_in, 16)
            sp.wait_ge(factors, 1)
            sp.dma_start(M.r_dram[B - 1].rearrange("(p c) -> p c", c=64), M.crec[:]).then_inc(r_out, 16)
            sp.wait_ge(r_out, 16)
            for half in range(2):
                for j in range(2):
                    src = M.r_dram[B - 1:B].rearrange("o (h s j q) -> o j s h q", h=4, s=2, j=2)
                    sp.dma_start(M.rsum[half][64 * j:64 * j + 64], src[:, j, half].broadcast_to([64, 4, S])).then_inc(r_in, 16)
            M.load_ffn(sp)
            sp.wait_ge(diff, 1)
            sp.dma_start(M.x[:], M.x_dram.rearrange("(t p) d -> p t d", p=P)).then_inc(x_in, 16)

        @block.vector
        def _(dve):
            link = Links(dve, own)
            dve.wait_ge(csum_in, 16)
            link(nc.vector.reciprocal(M.crec[:], M.csum[:]))
            nc.vector.tensor_scalar(M.crec[:], M.crec[:], M.sign[:, 0:1], None, ALU.mult).then_inc(factors, 1)
            dve.wait_ge(w_in, 16 * 4)
            for h in range(HP):
                ins = nc.vector.tensor_scalar(M.Wout[:, h, :], M.Wout[:, h, :], M.gam0[:, 0:1], 1.0 - LAMBDA_INIT,
                                              ALU.mult, ALU.mult)
            link(ins)

            def invert(b):
                dve.wait_ge(rms, b + 1)
                link(nc.vector.tensor_scalar(M.rmsb[b % 2], M.rmsb[b % 2], EPS_RMS, None, ALU.add))
                nc.vector.reciprocal(M.rmsb[b % 2], M.rmsb[b % 2]).then_inc(inv, 1)

            def norm(b):
                for h in range(HP):
                    o = M.o[:, 0, h, b * S:(b + 1) * S]
                    dve.wait_ge(spr, HP * b + h + 1)
                    nc.vector.tensor_tensor(o, o, PS[:, 2 + h % 2, :], ALU.mult).then_inc(normed, 1)

            def finish(b):
                x = M.x[:, TPB * b:TPB * (b + 1), :]
                dve.wait_ge(y, b + 1)
                link(nc.vector.tensor_tensor(x, x, PS[:, 5, :].rearrange("p (t d) -> p t d", d=D), ALU.add))
                layernorm(nc, dve, link, M, TPB * b, TPB, var, std, b + 1, done=x1)

            invert(0)
            o = M.o[:, :, :, (B - 1) * S:B * S]
            dve.wait_ge(r_in, 64)
            nc.vector.tensor_tensor(o[:, 0], o[:, 0], M.rsum[0][:], ALU.mult)
            link(nc.vector.tensor_tensor(o[:, 1], o[:, 1], M.rsum[1][:], ALU.mult))
            nc.vector.tensor_tensor(o[:, 0], o[:, 0], o[:, 1], ALU.add).then_inc(diff, 1)
            norm(0)
            dve.wait_ge(x_in, 16)
            for b in range(B):
                if b + 1 < B:
                    invert(b + 1)
                finish(b)
                if b + 1 < B:
                    norm(b + 1)

        @block.scalar
        def _(act):
            def square(b):
                if b == B - 1:
                    act.wait_ge(diff, 1)
                if b >= 2:
                    act.wait_ge(ms, b - 1)
                nc.scalar.activation(M.sqb[b % 2], M.o[:, 0, :, b * S:(b + 1) * S], ACT.Square).then_inc(sq, 1)

            def root(b):
                act.wait_ge(ms, b + 1)
                if b >= 2:
                    act.wait_ge(spr, HP * (b - 1))
                nc.scalar.activation(M.rmsb[b % 2], PS[:, 4, :], ACT.Sqrt).then_inc(rms, 1)

            square(0)
            root(0)
            square(1)
            for b in range(B):
                if b + 1 < B:
                    root(b + 1)
                act.wait_ge(yT, b + 1)
                nc.scalar.activation(M.yT[b % 2][:], PS[:, 6, :], ACT.Copy).then_inc(yT_c, 1)
                if b + 2 < B:
                    square(b + 2)
                act.wait_ge(var, b + 1)
                nc.scalar.activation(M.std[:, 0:TPB], M.mv[:, 0:TPB, 1], ACT.Sqrt, bias=M.eps[:, 0:1]).then_inc(std, 1)
                act.wait_ge(x1T, b + 1)
                nc.scalar.activation(M.xT[:, b * S:(b + 1) * S], PS[:, 7, :], ACT.Copy).then_inc(x1T_c, 1)
                for n in range(NTI):
                    i = b * NTI + n
                    act.wait_ge(acts, i + 1)
                    if i >= 2:
                        act.wait_ge(gelu, i - 1)
                    nc.scalar.activation(M.junk[i % 2], PS[:, i % 2, :], ACT.Gelu, accum_out=M.actsum[:, n, b:b + 1])\
                      .then_inc(gelu, 1)

        @block.tensor
        def _(pe):
            pe.wait_ge(w_in, 16 * 4)

            def mean_squares(b):
                pe.wait_ge(sq, b + 1)
                if b >= 1:
                    pe.wait_ge(rms, b)
                for h in range(HP):
                    mm = pe.matmul(PS[32 * h:32 * h + 32, 4, :], M.blk[:], M.sqb[b % 2][:, h, :], start=True, stop=True,
                                   skip_group_check=True)
                mm.then_inc(ms, 1)

            def spread_factors(b):
                pe.wait_ge(inv, b + 1)
                for h in range(HP):
                    if HP * b + h >= 2:
                        pe.wait_ge(normed, HP * b + h - 1)
                    pe.matmul(PS[:, 2 + h % 2, :], M.spread[:, h * P:(h + 1) * P], M.rmsb[b % 2], start=True, stop=True)\
                      .then_inc(spr, 1)

            def project(b):
                pe.wait_ge(own, 2)
                if b >= 1:
                    pe.wait_ge(yT_c, b)
                for h in range(HP):
                    pe.wait_ge(normed, HP * b + h + 1)
                    mm = pe.matmul(PS[:, 6, :], M.Wout[:, h, :], M.o[:, 0, h, b * S:(b + 1) * S],
                                   start=(h == 0), stop=(h == HP - 1))
                mm.then_inc(yT, 1)

            def turn_y(b):
                pe.wait_ge(yT_c, b + 1)
                if b >= 1:
                    pe.wait_ge(x1, b)
                for t in range(TPB):
                    mm = pe.transpose(PS[:, 5, t * P:(t + 1) * P], M.yT[b % 2][:, t * P:(t + 1) * P], M.ident[:])
                mm.then_inc(y, 1)

            mean_squares(0)
            spread_factors(0)
            mean_squares(1)
            project(0)
            turn_y(0)
            for b in range(B):
                if b + 1 < B:
                    spread_factors(b + 1)
                pe.wait_ge(x1, b + 1)
                if b >= 1:
                    pe.wait_ge(x1T_c, b)
                for t in range(TPB):
                    mm = pe.transpose(PS[:, 7, t * P:(t + 1) * P], M.x[:, TPB * b + t, :], M.ident[:])
                mm.then_inc(x1T, 1)
                if b + 2 < B:
                    mean_squares(b + 2)
                if b + 1 < B:
                    project(b + 1)
                if b == 0:
                    pe.wait_ge(M.ffn_in, 16 * M.n_ffn)
                pe.wait_ge(x1T_c, b + 1)
                for n in range(NTI):
                    i = b * NTI + n
                    if i >= 2:
                        pe.wait_ge(gelu, i - 1)
                    pe.matmul(PS[:, i % 2, :], M.patT[:, n * P:(n + 1) * P], M.xT[:, b * S:(b + 1) * S],
                              start=True, stop=True).then_inc(acts, 1)
                if b + 1 < B:
                    turn_y(b + 1)


def layernorm(nc, dve, link, M, first, n, var, std, count, out=None, done=None):
    def src(t):
        return M.x[:, first + t, :]
    out = src if out is None else out
    for t in range(n):
        ins = nc.vector.bn_stats(M.stats[:, t, :], src(t))
    link(ins)
    for t in range(n):
        ins = nc.vector.bn_aggr(M.mv[:, t, :], M.stats[:, t, :])
    ins.then_inc(var, 1)
    dve.wait_ge(std, count)
    link(nc.vector.reciprocal(M.rstd[:, 0:n], M.std[:, 0:n]))
    for t in range(n):
        ins = nc.vector.tensor_scalar(out(t), src(t), M.mv[:, t, 0:1], M.rstd[:, t:t + 1], ALU.subtract, ALU.mult)
    if done is None:
        link(ins)
    else:
        ins.then_inc(done, 1)


def ffn(nc, M):
    PS = M.PS
    NTI, NTP, NTO = N_IN // P, N_PROC // P, N_OUT // P
    ctx = ExitStack()

    def sem(name):
        return ctx.enter_context(nc.semaphore(f"ffn_{name}"))

    with ctx:
        sT = sem("sT")
        own = sem("own")
        rep = sem("rep")
        repT = sem("repT")
        repT_c = sem("repT_c")
        lin = sem("lin")
        lin_g = sem("lin_g")
        pmax = sem("pmax")
        pexp = sem("pexp")
        agg = sem("agg")
        agg_c = sem("agg_c")
        res = sem("res")
        res_c = sem("res_c")
        spreadb = sem("spread")
        var = sem("var")
        std = sem("std")
        xn = sem("xn")
        xnT = sem("xnT")
        xnT_c = sem("xnT_c")
        w_in = [sem(f"w_in{i}") for i in range(M.NSTAGE)]
        w_hi = sem("w_hi")
        w_sc = sem("w_sc")
        w_lo = sem("w_lo")
        l1_in = sem("l1_in")
        block = ctx.enter_context(nc.Block())

        NC = 2 * NX

        @block.sync
        def _(sp):
            M.load_l1(sp, l1_in)
            for c in range(NC):
                if c >= M.NSTAGE:
                    sp.wait_ge(w_lo, c - M.NSTAGE + 1)
                M.load_chunk(sp, c).then_inc(w_in[c % M.NSTAGE], 16)
            sp.wait_ge(l1_in, 16 * M.n_l1)

        @block.gpsimd
        def _(pool):
            nc.gpsimd.memset(M.wscale[:], WSCALE).then_inc(w_sc, 1)
            pool.wait_ge(w_sc, 1)
            for c in range(NC):
                pool.wait_ge(w_in[c % M.NSTAGE], 16 * (c // M.NSTAGE + 1))
                if c >= 2:
                    pool.wait_ge(w_lo, c - 1)
                nc.gpsimd.tensor_tensor(M.wtmp[:, c % 2, :], M.wst[:, c % M.NSTAGE, :],
                                        M.wscale[:].broadcast_to([P, 512]), ALU.mult).then_inc(w_sc, 1)
                pool.wait_ge(w_sc, c + 2)
                pool.wait_ge(w_hi, c + 1)
                hi, lo = (M.wh[:, c, :], M.wl[:, c, :])
                nc.gpsimd.tensor_tensor(lo, M.wtmp[:, c % 2, :], hi, ALU.subtract).then_inc(w_lo, 1)
            nc.gpsimd.memset(M.Ks[0:SROWS], 0.0)

        @block.tensor
        def _(pe):
            for n in range(NTI):
                mm = pe.transpose(PS[0:B, 4 + n // 4, (n % 4) * P:(n % 4 + 1) * P], M.actsum[:, n, :], M.ident[:])
            mm.then_inc(sT, 1)

            def turn(nt, count):
                pe.wait_ge(rep, count)
                for n in range(nt):
                    mm = pe.transpose(PS[:, 6, n * B:(n + 1) * B], M.rowb[:, n * P:(n + 1) * P], M.ident[0:B, 0:B])
                mm.then_inc(repT, 1)
                pe.wait_ge(repT_c, count)

            turn(NTI, 1)
            for n in range(NTI):
                mm = pe.matmul(PS[0:B, 0, :], M.colb[:, n * B:(n + 1) * B], M.piwT[:, n, :],
                               start=(n == 0), stop=(n == NTI - 1))
            mm.then_inc(lin, 1)
            turn(NTP, 2)
            for n in range(NTP):
                mm = pe.matmul(PS[0:D_PV, 7, 0:B], M.pv[:, n, :], M.colb[:, n * B:(n + 1) * B],
                               start=(n == 0), stop=(n == NTP - 1))
            mm.then_inc(agg, 1)
            pe.wait_ge(agg_c, 1)
            for n in range(2):
                mm = pe.matmul(PS[0:B, 1 + n, :], M.aggT[:], M.oiwT[0:D_PV, n * 512:(n + 1) * 512], start=True, stop=True)
            mm.then_inc(lin, 1)
            turn(NTO, 3)
            for n in range(NTO):
                mm = pe.matmul(PS[0:B, 3, 0:D], M.colb[:, n * B:(n + 1) * B], M.opat[:, n, :],
                               start=(n == 0), stop=(n == NTO - 1))
            mm.then_inc(res, 1)
            pe.wait_ge(res_c, 1)
            for b in range(B):
                mm = pe.matmul(PS[:, 7, b * D:(b + 1) * D], M.sel[:, b * P:(b + 1) * P], M.res[:], start=True, stop=True)
            mm.then_inc(spreadb, 1)
            for b in range(B):
                pe.wait_ge(xn, b + 1)
                if b >= 2:
                    pe.wait_ge(xnT_c, b - 1)
                for t in range(TPB):
                    mm = pe.transpose(PS[:, 4 + b % 2, t * P:(t + 1) * P], M.xn[b % 2][:, t, :], M.ident[:])
                mm.then_inc(xnT, 1)

        @block.scalar
        def _(act):
            def take_cols(nt, count):
                act.wait_ge(repT, count)
                nc.scalar.activation(M.colb[:, 0:nt * B], PS[:, 6, 0:nt * B], ACT.Copy).then_inc(repT_c, 1)

            for c in range(NC):
                act.wait_ge(w_in[c % M.NSTAGE], 16 * (c // M.NSTAGE + 1))
                nc.scalar.activation(M.wh[:, c, :], M.wst[:, c % M.NSTAGE, :], ACT.Copy, scale=WSCALE).then_inc(w_hi, 1)
            take_cols(NTI, 1)
            act.wait_ge(lin, 1)
            nc.scalar.activation(M.rowa[:, 0:N_PROC], PS[0:B, 0, :], ACT.Gelu).then_inc(lin_g, 1)
            act.wait_ge(pmax, 1)
            nc.scalar.activation(M.rowb[:, 0:N_PROC], M.rowa[:, 0:N_PROC], ACT.Exp, bias=M.tops[:, 8:9]).then_inc(pexp, 1)
            take_cols(NTP, 2)
            act.wait_ge(agg, 1)
            nc.scalar.activation(M.aggT[:], PS[0:D_PV, 7, 0:B], ACT.Copy).then_inc(agg_c, 1)
            act.wait_ge(lin, 2)
            nc.scalar.activation(M.rowa[:], PS[0:B, 1:3, :].rearrange("p a b -> p (a b)"), ACT.Gelu).then_inc(lin_g, 1)
            take_cols(NTO, 3)
            act.wait_ge(res, 1)
            nc.scalar.activation(M.res[:], PS[0:B, 3, 0:D], ACT.Copy).then_inc(res_c, 1)
            for i in range(2 * B):
                act.wait_ge(var, i + 1)
                nc.scalar.activation(M.std[:, 0:TPB], M.mv[:, 0:TPB, 1], ACT.Sqrt, bias=M.eps[:, 0:1]).then_inc(std, 1)

        @block.vector
        def _(dve):
            link = Links(dve, own)

            def take_top(n, k, first=None):
                for r in range(k // 8):
                    m8 = M.tops[:, 0:8]
                    link(nc.vector.max(m8, M.rowc[:, 0:n]))
                    if r == 0 and first is not None:
                        first()
                    link(nc.vector.match_replace(out=M.rowc[:, 0:n], in_to_replace=m8, in_values=M.rowc[:, 0:n],
                                                 imm_value=MSHIFT))

            dve.wait_ge(sT, 1)
            link(nc.vector.tensor_scalar(M.rowa[:], PS[0:B, 4:6, :].rearrange("p a b -> p (a b)"), 1.0 / S, None, ALU.mult))
            link(nc.vector.tensor_copy(M.rowc[:], M.rowa[:]))
            take_top(N_IN, K_IN)
            nc.vector.scalar_tensor_tensor(out=M.rowb[:], in0=M.rowc[:], scalar=MSHIFT, in1=M.rowa[:],
                                           op0=ALU.is_equal, op1=ALU.mult).then_inc(rep, 1)
            dve.wait_ge(lin_g, 1)
            link(nc.vector.tensor_copy(M.rowc[:, 0:N_PROC], M.rowa[:, 0:N_PROC]))

            def negate_max():
                nc.vector.tensor_scalar(M.tops[:, 8:9], M.tops[:, 0:1], -1.0, None, ALU.mult).then_inc(pmax, 1)

            take_top(N_PROC, K_PROC, negate_max)
            dve.wait_ge(pexp, 1)
            link(nc.vector.scalar_tensor_tensor(out=M.rowb[:, 0:N_PROC], in0=M.rowc[:, 0:N_PROC], scalar=MSHIFT,
                                                in1=M.rowb[:, 0:N_PROC], op0=ALU.is_equal, op1=ALU.mult))
            link(nc.vector.tensor_reduce(M.tops[:, 9:10], M.rowb[:, 0:N_PROC], AX.X, ALU.add))
            link(nc.vector.reciprocal(M.tops[:, 10:11], M.tops[:, 9:10]))
            nc.vector.tensor_scalar(M.rowb[:, 0:N_PROC], M.rowb[:, 0:N_PROC], M.tops[:, 10:11], None,
                                    ALU.mult).then_inc(rep, 1)
            dve.wait_ge(lin_g, 2)
            link(nc.vector.tensor_copy(M.rowc[:], M.rowa[:]))
            take_top(N_OUT, K_OUT)
            nc.vector.scalar_tensor_tensor(out=M.rowb[:], in0=M.rowc[:], scalar=MSHIFT, in1=M.rowa[:],
                                           op0=ALU.is_equal, op1=ALU.mult).then_inc(rep, 1)
            dve.wait_ge(spreadb, 1)

            def take_xnT(b):
                dve.wait_ge(xnT, b + 1)
                nc.vector.tensor_scalar(M.xT[:, b * S:(b + 1) * S], PS[:, 4 + b % 2, :], M.gb1[:, 0:1], M.gb1[:, 1:2],
                                        ALU.mult, ALU.add).then_inc(xnT_c, 1)

            for b in range(B):
                x = M.x[:, TPB * b:TPB * (b + 1), :]
                row = PS[:, 7, b * D:(b + 1) * D].rearrange("p (o d) -> p o d", o=1).broadcast_to([P, TPB, D])
                link(nc.vector.tensor_tensor(x, x, row, ALU.add))
                layernorm(nc, dve, link, M, TPB * b, TPB, var, std, 2 * b + 1)
                if b >= 2:
                    dve.wait_ge(xnT, b - 1)
                layernorm(nc, dve, link, M, TPB * b, TPB, var, std, 2 * b + 2, out=lambda t: M.xn[b % 2][:, t, :], done=xn)
                if b:
                    take_xnT(b - 1)
            take_xnT(B - 1)


def l1_output(nc, M):
    PS = M.PS
    ctx = ExitStack()

    def sem(name):
        return ctx.enter_context(nc.semaphore(f"out1_{name}"))

    with ctx:
        oT = sem("oT")
        cx = sem("cx")
        cxT = sem("cxT")
        cxT_c = sem("cxT_c")
        y = sem("y")
        y_added = sem("y_added")
        own = sem("own")
        var = sem("var")
        std = sem("std")
        x3 = sem("x3")
        x3T = sem("x3T")
        x3T_c = sem("x3T_c")
        x3T_h = sem("x3T_h")
        lo = sem("lo")
        logit = sem("logit")
        lexp = sem("lexp")
        lsub = sem("lsub")
        block = ctx.enter_context(nc.Block())

        @block.tensor
        def _(pe):
            def turn_o(t):
                if t >= 2:
                    pe.wait_ge(cx, t - 1)
                for g in range(4):
                    mm = pe.transpose(PS[:, t % 2, g * P:(g + 1) * P], M.o[:, g, t * P:(t + 1) * P], M.ident[:])
                mm.then_inc(oT, 1)

            def turn_cx(t):
                pe.wait_ge(cx, t + 1)
                if t >= 2:
                    pe.wait_ge(cxT_c, t - 1)
                pe.transpose(PS[:, 2 + t % 2, 0:P], M.cx[t % 2][:], M.ident[:]).then_inc(cxT, 1)

            def project(t):
                pe.wait_ge(cxT_c, t + 1)
                if t >= 2:
                    pe.wait_ge(y_added, t - 1)
                pe.matmul(PS[:, 4 + t % 2, 0:D], M.cxT[t % 2][:], M.Wo1[:], start=True, stop=True).then_inc(y, 1)

            def turn_x3(b):
                pe.wait_ge(x3, b + 1)
                if b >= 1:
                    pe.wait_ge(lo, b)
                for t in range(TPB):
                    mm = pe.transpose(PS[:, 6, t * P:(t + 1) * P], M.x[:, TPB * b + t, :], M.ident[:])
                mm.then_inc(x3T, 1)
                pe.wait_ge(x3T_c, b + 1)
                for t in range(TPB * b, TPB * (b + 1)):
                    mm = pe.matmul(PS[:, 7, t * NE:(t + 1) * NE], M.xT[:, t * P:(t + 1) * P], M.rT[:], start=True, stop=True)
                mm.then_inc(logit, 1)

            turn_o(0)
            for t in range(NT):
                if t + 1 < NT:
                    turn_o(t + 1)
                turn_cx(t)
                project(t)
                if t % TPB == TPB - 1 and t > TPB:
                    turn_x3(t // TPB - 1)
            turn_x3(B - 1)

        @block.scalar
        def _(act):
            def take_x3T(b):
                act.wait_ge(x3T, b + 1)
                nc.scalar.activation(M.xT[:, b * S:(b + 1) * S], PS[:, 6, :], ACT.Copy).then_inc(x3T_c, 1)
                nc.scalar.activation(M.xTh[:, b * S:(b + 1) * S], PS[:, 6, :], ACT.Copy).then_inc(x3T_h, 1)

            for t in range(NT):
                act.wait_ge(cxT, t + 1)
                if t >= 2:
                    act.wait_ge(y, t - 1)
                nc.scalar.activation(M.cxT[t % 2][:], PS[:, 2 + t % 2, 0:P], ACT.Copy).then_inc(cxT_c, 1)
                if t % TPB == TPB - 1:
                    act.wait_ge(var, t // TPB + 1)
                    nc.scalar.activation(M.std[:, 0:TPB], M.mv[:, 0:TPB, 1], ACT.Sqrt, bias=M.eps[:, 0:1]).then_inc(std, 1)
                    if t > TPB:
                        take_x3T(t // TPB - 1)
            take_x3T(B - 1)
            act.wait_ge(lsub, 1)
            nc.scalar.activation(M.rt[:, 0], M.rt[:, 0], ACT.Exp).then_inc(lexp, 1)

        @block.vector
        def _(dve):
            link = Links(dve, own)

            def take_lo(b):
                dve.wait_ge(x3T_h, b + 1)
                nc.vector.tensor_tensor(M.xTl[:, b * S:(b + 1) * S], PS[:, 6, :], M.xTh[:, b * S:(b + 1) * S],
                                        ALU.subtract).then_inc(lo, 1)

            for t in range(NT):
                dve.wait_ge(oT, t + 1)
                heads = PS[:, t % 2, :].rearrange("p (h e) -> p h e", e=32)
                link(nc.vector.reciprocal(M.rden[:], heads[:, :, DH1]))
                nc.vector.tensor_tensor(M.cx[t % 2][:].rearrange("p (h e) -> p h e", e=DH1), heads[:, :, 0:DH1],
                                        spread(M.rden[:], DH1), ALU.mult).then_inc(cx, 1)
                dve.wait_ge(y, t + 1)
                nc.vector.tensor_tensor(M.x[:, t, :], M.x[:, t, :], PS[:, 4 + t % 2, 0:D], ALU.add).then_inc(y_added, 1)
                if t % TPB == TPB - 1:
                    b = t // TPB
                    dve.wait_ge(y_added, t + 1)
                    layernorm(nc, dve, link, M, TPB * b, TPB, var, std, b + 1, done=x3)
                    if b:
                        take_lo(b - 1)
            take_lo(B - 1)
            dve.wait_ge(logit, B)
            lg = PS[:, 7, 0:NT * NE].rearrange("p (t e) -> p t e", e=NE)
            prob, one, two, three = M.rt[:, 0], M.rt1[:, 0], M.rt1[:, 1], M.rt1[:, 2]
            link(nc.vector.tensor_reduce(one, lg, AX.X, ALU.max))
            nc.vector.tensor_tensor(prob, lg, spread(one, NE), ALU.subtract).then_inc(lsub, 1)
            dve.wait_ge(lexp, 1)
            link(nc.vector.tensor_reduce(two, prob, AX.X, ALU.add))
            link(nc.vector.reciprocal(three, two))
            link(nc.vector.tensor_tensor(prob, prob, spread(three, NE), ALU.mult))
            other = prob.rearrange("p t (o e) -> p t o e", o=1).broadcast_to([P, NT, NE, NE])
            mine = prob.rearrange("p t (e o) -> p t e o", o=1).broadcast_to([P, NT, NE, NE])
            tri = M.tri[:].rearrange("p (o e j) -> p o e j", o=1, e=NE).broadcast_to([P, NT, NE, NE])
            nc.vector.tensor_tensor(M.gt[:], other, mine, ALU.is_gt)
            link(nc.vector.tensor_tensor(M.eq[:], other, mine, ALU.is_equal))
            link(nc.vector.tensor_tensor(M.eq[:], M.eq[:], tri, ALU.mult))
            link(nc.vector.tensor_tensor(M.gt[:], M.gt[:], M.eq[:], ALU.add))
            link(nc.vector.tensor_reduce(M.rt[:, 1], M.gt[:], AX.X, ALU.add))
            link(nc.vector.scalar_tensor_tensor(out=M.rt[:, 1], in0=M.rt[:, 1], scalar=1.5, in1=prob,
                                                op0=ALU.is_lt, op1=ALU.mult))
            link(nc.vector.tensor_reduce(one, M.rt[:, 1], AX.X, ALU.add))
            link(nc.vector.tensor_scalar(one, one, 1e-9, None, ALU.max))
            link(nc.vector.reciprocal(two, one))
            link(nc.vector.tensor_scalar(two, two, 1.0 / WSCALE, None, ALU.mult))
            link(nc.vector.memset(M.comb[:], 1.0 / WSCALE))
            link(nc.vector.tensor_tensor(M.comb[:, :, 0:NE], M.rt[:, 1], spread(two, NE), ALU.mult))


def moe(nc, M):
    PS = M.PS
    NF = FF // P
    U = NX * NF
    HB, OB = 3, 3
    ctx = ExitStack()

    def sem(name):
        return ctx.enter_context(nc.semaphore(f"moe_{name}"))

    with ctx:
        h_ready = sem("h_ready")
        h_free = sem("h_free")
        sq_done = sem("sq_done")
        hi_done = sem("hi_done")
        lo_done = sem("lo_done")
        p_done = sem("p_done")
        o_free = sem("o_free")
        own = sem("own")
        var = sem("var")
        std = sem("std")
        carried = sem("carried")
        y_ready = sem("y_ready")
        y_out = sem("y_out")
        block = ctx.enter_context(nc.Block())
        NL = 1 + 1 + 1

        @block.tensor
        def _(pe):
            pe.sem_inc(p_done, 2)

            def hidden(u, g):
                e, f = u // NF, u % NF
                pe.wait_ge(h_free, U * g + u + 1)
                cols = slice(e * FF + f * P, e * FF + (f + 1) * P)
                xh, xl = M.xTh[:, bass.ds(g * S, S)], M.xTl[:, bass.ds(g * S, S)]
                out = PS[:, u % HB, :]
                pe.matmul(out, M.fch[:, cols], xh, start=True, stop=False)
                pe.matmul(out, M.fch[:, cols], xl, start=False, stop=False)
                pe.matmul(out, M.fcl[:, cols], xh, start=False, stop=True).then_inc(h_ready, 1)

            def project(u, g):
                e, f = u // NF, u % NF
                if f == 0:
                    pe.wait_ge(o_free, NX * g + e + 1)
                pe.wait_ge(lo_done, 2 + U * g + u + 1)
                hh, hl = M.hh[u % 2], M.hl[u % 2]
                for t in range(TPB):
                    out = PS[:, 4 + e % OB, t * D:(t + 1) * D]
                    cols = slice(t * P, (t + 1) * P)
                    w = (e * NF + f) * D
                    pe.matmul(out, hh[:, cols], M.prh[:, w:w + D], start=(f == 0 and t == 0), stop=False,
                              skip_group_check=True)
                    pe.matmul(out, hh[:, cols], M.prl[:, w:w + D], start=False, stop=False, skip_group_check=True)
                    mm = pe.matmul(out, hl[:, cols], M.prh[:, w:w + D], start=False, stop=(f == NF - 1 and t == TPB - 1),
                                   skip_group_check=True)
                mm.then_inc(p_done, 1)

            with pe.Fori(0, B) as g:
                hidden(0, g)
                hidden(1, g)
                for u in range(U):
                    if u + 2 < U:
                        hidden(u + 2, g)
                    project(u, g)

        @block.scalar
        def _(act):
            act.sem_inc(h_free, HB)
            with act.Fori(0, B) as g:
                for u in range(U):
                    n = U * g + u
                    act.wait_ge(h_ready, n + 1)
                    act.wait_ge(sq_done, n + 1)
                    nc.scalar.activation(M.r[u % 2][:], PS[:, u % HB, :], ACT.Relu, scale=1.0 / WSCALE).then_inc(h_free, 1)
                    act.wait_ge(h_free, HB + n + 1)
                    act.wait_ge(p_done, n + 1)
                    nc.scalar.activation(M.hh[u % 2][:], M.r[u % 2][:], ACT.Square).then_inc(hi_done, 1)
                act.wait_ge(var, g + 1)
                nc.scalar.activation(M.std[:, 0:TPB], M.mv[:, 0:TPB, 1], ACT.Sqrt, bias=M.eps[:, 0:1]).then_inc(std, 1)

        @block.gpsimd
        def _(pool):
            pool.sem_inc(sq_done, 2)
            with pool.Fori(0, B) as g:
                for u in range(U):
                    n = U * g + u
                    pool.wait_ge(h_free, HB + n + 1)
                    pool.wait_ge(lo_done, n + 1)
                    nc.gpsimd.tensor_tensor(M.sq[u % 2][:], M.r[u % 2][:], M.r[u % 2][:], ALU.mult).then_inc(sq_done, 1)

        @block.vector
        def _(dve):
            dve.sem_inc(lo_done, 2)
            dve.sem_inc(o_free, OB)

            def combine(e, g):
                dve.wait_ge(p_done, 2 + U * g + NF * (e + 1))
                dve.wait_ge(o_free, OB + NX * g + e)
                for t in range(TPB):
                    prev = M.xg[:, t, :] if e == 0 else M.acc[:, t, :]
                    ins = nc.vector.scalar_tensor_tensor(out=M.acc[:, t, :], in0=PS[:, 4 + e % OB, t * D:(t + 1) * D],
                                                         scalar=M.cg[:, t, e:e + 1], in1=prev, op0=ALU.mult, op1=ALU.add)
                ins.then_inc(o_free, 1)

            with dve.Fori(0, B) as g:
                link = Links(dve, own, g * NL)
                nc.vector.tensor_copy(M.cg[:], M.comb[:, bass.ds(TPB * g, TPB), :])
                link(nc.vector.tensor_copy(M.xg[:], M.x[:, bass.ds(TPB * g, TPB), :]))
                for u in range(U):
                    n = U * g + u
                    dve.wait_ge(sq_done, 2 + n + 1)
                    dve.wait_ge(hi_done, n + 1)
                    dve.wait_ge(p_done, n + 1)
                    nc.vector.tensor_tensor(M.hl[u % 2][:], M.sq[u % 2][:], M.hh[u % 2][:], ALU.subtract).then_inc(lo_done, 1)
                    if u % NF == 1 and u > NF:
                        combine(u // NF - 1, g)
                combine(NX - 1, g)
                dve.wait_ge(o_free, OB + NX * (g + 1))
                for t in range(TPB):
                    ins = nc.vector.bn_stats(M.stats[:, t, :], M.acc[:, t, :])
                link(ins)
                dve.sem_inc(carried, 1)
                for t in range(TPB):
                    ins = nc.vector.bn_aggr(M.mv[:, t, :], M.stats[:, t, :])
                ins.then_inc(var, 1)
                dve.wait_ge(std, g + 1)
                link(nc.vector.reciprocal(M.rstd[:, 0:TPB], M.std[:, 0:TPB]))
                dve.wait_ge(y_out, 1 + 16 * g)
                for t in range(TPB):
                    ins = nc.vector.tensor_scalar(M.y[:, t, :], M.acc[:, t, :], M.mv[:, t, 0:1], M.rstd[:, t:t + 1],
                                                  ALU.subtract, ALU.mult)
                ins.then_inc(y_ready, 1)
                assert link.n == NL

        @block.sync
        def _(sp):
            sp.sem_inc(y_out, 1)
            with sp.Fori(0, B) as g:
                sp.wait_ge(y_ready, g + 1)
                sp.dma_start(M.out_dram[bass.ds(g, 1)].rearrange("b (t p) d -> p (b t) d", p=P), M.y[:]).then_inc(y_out, 16)
            sp.wait_ge(y_out, 1 + 16 * B)


class Memory:
    pass


def build(nc, I, out, debug=None):
    M = Memory()
    M.out_dram = out
    with ExitStack() as ctx:
        def sb(name, shape, dt=F32):
            return ctx.enter_context(nc.sbuf_tensor(name, shape, dt))

        def dram(name, shape, dt=F32):
            return nc.dram_tensor(name, shape, dt, kind="Internal").ap()

        M.PS = ctx.enter_context(nc.psum_tensor("PS", [P, 8, BANK], F32))
        M.sums_dram = dram("sums_scratch", [B, 8, 2, S])
        M.r_dram = dram("r_scratch", [B, 16 * S])
        M.qk0_dram = dram("qk0_scratch", [2, 4, 2 * P, S], F16)
        M.qk_dram = dram("qk_scratch", [4, P, S], F16)
        M.x_dram, M.xT_dram = I["x"], I["xT"]
        M.gamma0_dram, M.Wout_dram, M.blk_dram, M.spread_dram = I["gamma0"], I["Wout"], I["blk"], I["spread"]

        M.x = sb("x_tokens", [P, NT, D])
        M.xT = sb("x_transposed", [P, T])
        M.ident = sb("ident", [P, P])
        M.eps = sb("eps", [P, 1])
        M.stats = sb("stats", [P, TPB, 6])
        M.mv = sb("mv", [P, TPB, 2])
        M.std = sb("std", [P, TPB])
        M.rstd = sb("rstd", [P, TPB])
        M.xb = sb("xb", [P, S])
        M.Qs = sb("q_stack", [SROWS + 1, NQK, S], F16)
        M.Ks = sb("k_stack", [SROWS + 1, NQK, S], F16)
        M.Pr = sb("exp_ring", [P, PRING, S])
        M.qk = sb("qk_parts", [P, 2, 4, 2, S], F16)
        M.V = sb("V", [P, 4, 512])
        M.Vn = sb("V_next", [P, 4, 512])
        M.negm = sb("neg_max", [P, 2, 16])
        M.mrow = [sb(f"max_row{i}", [16, P], F16) for i in range(2)]
        M.ones = sb("ones", [P, 32])
        M.actsum = sb("actsum", [P, N_IN // P, B])

        M.ffn_in = ctx.enter_context(nc.semaphore("ffn_in"))
        M.piwT = M.qk[:].rearrange("p h a b c -> p (h a b c)").bitcast(F32).rearrange("p (n c) -> p n c", c=N_PROC)

        with ExitStack() as l0:
            def sb0(name, shape, dt=F32):
                return l0.enter_context(nc.sbuf_tensor(name, shape, dt))

            M.o = sb0("o0", [P, 2, H0 // 2, T])
            M.Wq = sb0("Wq", [P, 512])
            M.Wkv = sb0("Wkv", [P, 1024])
            M.sums = [sb0(f"sums{i}", [P, S]) for i in range(2)]

            M.esum = [sb0(f"exp_sums{i}", [P, 2, S]) for i in range(2)]
            M.csum, M.crec = sb0("csum", [P, 64]), sb0("crec", [P, 64])
            M.lam, M.lamp = sb0("lam", [P, 4, DH0]), sb0("lamp", [P, 2, DH0])
            M.lams, M.nlam, M.sign, M.gam0 = sb0("lams", [P, 8]), sb0("nlam", [P, 1]), sb0("sign", [P, 3]), sb0("gam0", [P, 1])
            M.rsum = [M.x[:].rearrange("p t d -> p (t d)").rearrange("p (h q) -> p h q", h=4),
                      M.xT[:].rearrange("p (h q) -> p h q", h=4)]

            def load_l0(sp, sem):
                pairs = [(M.Wq, I["Wq"]), (M.Wkv, I["Wkv"]), (M.ident, I["ident"]), (M.eps, I["eps"])]
                for dst, src in pairs:
                    sp.dma_start(dst[:], src).then_inc(sem, 16)
                sp.dma_start(M.lam[:], I["lam"].rearrange("(o k) d -> o k d", o=1).broadcast_to([P, 4, DH0])).then_inc(sem, 16)
                sp.dma_start(M.sign[:, 1:3], I["half"]).then_inc(sem, 16)
            M.n_l0, M.load_weights = 6, load_l0
            attention(nc, M, AttnPlan(0))

            M.Wout = M.Wq[:].rearrange("p (h n) -> p h n", n=D)
            M.blk, M.spread = M.Wkv[:, 0:32], M.Wkv[:, 512:1024]
            M.yT = [M.xb, M.sums[0]]
            ring = M.Pr[:].rearrange("p a b -> p (a b)")
            M.sqb = [ring[:, 2048 * i:2048 * (i + 1)].rearrange("p (h q) -> p h q", h=4) for i in range(2)]
            M.rmsb = [ring[:, 4096 + 512 * i:4096 + 512 * (i + 1)] for i in range(2)]
            M.junk = [ring[:, 5120 + 512 * i:5120 + 512 * (i + 1)] for i in range(2)]
            vn, vv = (v[:].rearrange("p a b -> p (a b)") for v in (M.Vn, M.V))
            M.patT, M.oiwT = vn[:, 0:N_IN], vn[:, N_IN:2 * N_IN]
            M.opat = vv[:, 0:1024].rearrange("p (n d) -> p n d", d=D)
            M.pv = vv[:, 1024:1280].rearrange("p (n d) -> p n d", d=D_PV)
            M.sel, M.gb1 = vv[0:B, 1280:1280 + B * P], vv[:, 1792:1794]

            def load_ffn(sp):
                pairs = [(M.patT, I["patT"]), (M.piwT, I["piwT"].rearrange("(n p) c -> p n c", p=P)),
                         (M.oiwT[0:D_PV, :], I["oiwT"]), (M.opat, I["opat"].rearrange("(n p) c -> p n c", p=P)),
                         (M.pv, I["pv"].rearrange("(n p) c -> p n c", p=P)), (M.sel, I["sel"]), (M.gb1, I["gb1"])]
                for dst, src in pairs:
                    sp.dma_start(dst, src).then_inc(M.ffn_in, 16)
            M.load_ffn, M.n_ffn = load_ffn, 7
            l0_output(nc, M)

        if debug == "x1":
            return M
        with ExitStack() as l1:
            def sb1(name, shape, dt=F32):
                return l1.enter_context(nc.sbuf_tensor(name, shape, dt))
            M.wh, M.wl = sb1("w_high", [P, 2 * NX, FF], F16), sb1("w_low", [P, 2 * NX, FF], F16)
            M.Wo1 = sb1("Wo1", [P, D])
            M.rT = sb1("routerT", [P, NE])
            M.tri = sb1("tri", [P, NE * NE])
            M.comb = sb1("comb", [P, NT, NX])
            M.Win = sb1("Win", [P, 3 * D])
            M.WinR = sb1("WinR", [P, 2 * D])
            M.cos, M.sin = sb1("cos", [P, S]), sb1("sin", [P, S])
            M.bqk, M.bv, M.bo = sb1("bqk", [P, 4]), sb1("bv", [P, D]), sb1("bo", [P, D])
            with ExitStack() as fc:
                def sbf(name, shape, dt=F32):
                    return fc.enter_context(nc.sbuf_tensor(name, shape, dt))
                M.rowa, M.rowb, M.rowc = (sbf(f"row{c}", [B, 1024]) for c in "abc")
                M.colb = sbf("colb", [P, 8 * B])
                M.tops = sbf("tops", [B, 16])
                M.aggT = sbf("aggT", [D_PV, B])
                M.res = sbf("res", [B, D])
                M.xn = [sbf(f"xn{i}", [P, TPB, D]) for i in range(2)]
                M.NSTAGE = 10
                M.wst, M.wtmp = sbf("w_stage", [P, M.NSTAGE, FF]), sbf("w_scaled", [P, 2, FF])
                M.wscale = sbf("w_scale", [P, 1])

                def load_l1(sp, sem):
                    pairs = [(M.Win, I["Win"]), (M.WinR, I["WinR"]), (M.cos, I["cos"]), (M.sin, I["sin"]), (M.bqk, I["bqk"]),
                             (M.Wo1, I["Wo1"]), (M.rT, I["rT"]), (M.tri, I["tri"])]
                    for dst, src in pairs:
                        sp.dma_start(dst[:], src).then_inc(sem, 16)
                    for dst, src in [(M.bv, I["bv"]), (M.bo, I["bo"])]:
                        sp.dma_start(dst[:], src.broadcast_to([P, D])).then_inc(sem, 16)
                M.load_l1, M.n_l1 = load_l1, 10

                def load_chunk(sp, c):
                    e, dst = c % NX, M.wst[:, c % M.NSTAGE, :]
                    if c < NX:
                        return sp.dma_start(dst, I["fcT"][e] if e < NE else I["sfcT"])
                    w = I["prT"][e] if e < NE else I["sprT"]
                    return sp.dma_start(dst.rearrange("p (f d) -> p f d", d=D), w.rearrange("(f p) d -> p f d", p=P))
                M.load_chunk = load_chunk
                ffn(nc, M)
            if debug == "x2":
                return M
            with ExitStack() as l1a:
                def sba(name, shape, dt=F32):
                    return l1a.enter_context(nc.sbuf_tensor(name, shape, dt))
                M.o = sba("o1", [P, 4, T])
                with ExitStack() as at:
                    def sbt(name, shape, dt=F32):
                        return at.enter_context(nc.sbuf_tensor(name, shape, dt))
                    M.raw = sbt("raw", [P, 5, S])
                    attention(nc, M, AttnPlan(1))
                    if debug == "o1":
                        return M
                NW = NX * FF
                wh, wl = (w[:].rearrange("p c n -> p (c n)") for w in (M.wh, M.wl))
                M.fch, M.prh, M.fcl, M.prl = wh[:, 0:NW], wh[:, NW:2 * NW], wl[:, 0:NW], wl[:, NW:2 * NW]
                with ExitStack() as po:
                    def sbp(name, shape, dt=F32):
                        return po.enter_context(nc.sbuf_tensor(name, shape, dt))
                    M.rden = sbp("rden", [P, 16])
                    M.cx = [sbp(f"cx{i}", [P, D]) for i in range(2)]
                    M.cxT = [sbp(f"cxT{i}", [P, P]) for i in range(2)]
                    M.rt, M.rt1 = sbp("rt", [P, 2, NT, NE]), sbp("rt1", [P, 3, NT])
                    vv = M.V[:].rearrange("p a b -> p (a b)")
                    M.gt = vv[:, 0:1024].rearrange("p (t e j) -> p t e j", e=NE, j=NE)
                    M.eq = vv[:, 1024:2048].rearrange("p (t e j) -> p t e j", e=NE, j=NE)
                    qkf = M.qk[:].rearrange("p h a b c -> p (h a b c)")
                    M.xTh, M.xTl = qkf[:, 0:T], qkf[:, T:2 * T]
                    l1_output(nc, M)
                    of = M.o[:].rearrange("p g t -> p (g t)")
                    oh = of.bitcast(F16)
                    M.r = [of[:, i * S:(i + 1) * S] for i in range(2)]
                    M.sq = [of[:, (2 + i) * S:(3 + i) * S] for i in range(2)]
                    M.hh = [oh[:, (8 + i) * S:(9 + i) * S] for i in range(2)]
                    M.hl = [oh[:, (10 + i) * S:(11 + i) * S] for i in range(2)]
                    vn = M.Vn[:].rearrange("p a b -> p (a b)")
                    M.acc, M.xg, M.y = (vn[:, 512 * i:512 * (i + 1)].rearrange("p (t d) -> p t d", d=D) for i in range(3))
                    M.cg = vn[:, 1536:1536 + TPB * NX].rearrange("p (t e) -> p t e", e=NX)
                    if debug == "x3":
                        return M
                    moe(nc, M)
    return M


def kernel(**inputs):
    import concourse.bacc as bacc
    from concourse.bass_utils import run_bass_kernel_spmd

    def row(name):
        return np.asarray(inputs[name])

    def laid(a):
        return np.ascontiguousarray(a)

    x = row("L0_attn_x").reshape(T, D)
    Win = row("L1_attn_W_in")
    within = np.arange(DH1)
    within[:RD] = within[:RD].reshape(-1, 2)[:, ::-1].reshape(-1)
    swap = (np.arange(D).reshape(-1, DH1)[:, within]).reshape(-1)
    b_in = row("L1_attn_b_in")
    t = np.arange(S, dtype=np.float32)
    inv_freq = (np.float32(1.0) / np.power(np.float32(10000.0), np.arange(0, RD, 2, dtype=np.float32) / np.float32(RD)))
    freqs = np.repeat(t[:, None] * inv_freq[None, :].astype(np.float32), 2, axis=-1)
    cos = np.ones((DH1, S), np.float32)
    sin = np.zeros((DH1, S), np.float32)
    cos[:RD] = np.cos(freqs).T
    sin[:RD] = np.sin(freqs).T * np.where(np.arange(RD) % 2 == 0, -1.0, 1.0)[:, None]
    blk = np.zeros((P, 32), np.float32)
    blk[:DV0, 0] = 1.0 / DV0
    blk[DV0:, 1] = 1.0 / DV0
    sel = np.zeros((B, B * P), np.float32)
    for b in range(B):
        sel[b, b * P:(b + 1) * P] = 1.0
    half = np.stack([1.0 - np.arange(P) // 16 % 2, np.arange(P) // 16 % 2], axis=1).astype(np.float32)
    spread_rows = np.zeros((P, 4, 2, DV0), np.float32)
    for h in range(4):
        for j in range(2):
            spread_rows[32 * h + j, h, j] = 1.0
    spread_rows = spread_rows.reshape(P, 4 * P)

    def by_half(w):
        return laid(w.reshape(D, 4, 2, 2, DH0).transpose(0, 1, 3, 2, 4).reshape(D, 512))

    arrays = {
        "x": laid(x), "xT": laid(x.T),
        "Wq": by_half(row("L0_attn_Wq")),
        "Wkv": laid(np.concatenate([by_half(row("L0_attn_Wkv")[:, :512]), row("L0_attn_Wkv")[:, 512:]], axis=1)),
        "half": half, "spread": spread_rows,
         "Wout": row("L0_attn_Wout"),
        "lam": laid(np.stack([row(f"L0_attn_lambda_{n}") for n in ("q1", "k1", "q2", "k2")])),
        "gamma0": laid(np.tile(row("L0_attn_gamma"), 2)[:, None]),
        "patT": laid(row("L0_ffn_input_patterns").T), "piwT": laid(row("L0_ffn_process_input_weights").T),
        "pv": row("L0_ffn_process_values"), "oiwT": laid(row("L0_ffn_output_input_weights").T),
        "opat": row("L0_ffn_output_patterns"),
        "Win": Win, "WinR": laid(np.concatenate([Win[:, :D][:, swap], Win[:, D:2 * D][:, swap]], axis=1)),
        "bqk": laid(np.stack([b_in[:D], b_in[D:2 * D], b_in[:D][swap], b_in[D:2 * D][swap]], axis=1)),
        "bv": laid(b_in[None, 2 * D:]), "bo": laid(row("L1_attn_b_out")[None]),
        "Wo1": row("L1_attn_W_out"),
        "gb1": laid(np.stack([row("L1_attn_gamma"), row("L1_attn_beta")], axis=1)),
        "rT": laid(row("L1_ffn_router_w").T),
        "fcT": laid(row("L1_ffn_w_fc").transpose(0, 2, 1)), "prT": laid(row("L1_ffn_w_proj").transpose(0, 2, 1)),
        "sfcT": laid(row("L1_ffn_shared_fc").T), "sprT": laid(row("L1_ffn_shared_proj").T),
        "ident": np.eye(P, dtype=np.float32), "eps": np.full((P, 1), EPS_LN, np.float32), "blk": blk, "sel": sel,
        "cos": laid(np.tile(cos, (D // DH1, 1))), "sin": laid(np.tile(sin, (D // DH1, 1))),
        "tri": laid(np.tile(np.tril(np.ones((NE, NE), np.float32), -1).reshape(1, -1), (P, 1))),
    }
    nc = bacc.Bacc("TRN2", target_bir_lowering=False, num_devices=1)
    maps, I = {}, {}
    for name, a in arrays.items():
        a = np.ascontiguousarray(a)
        maps[f"in_{name}"] = a
        I[name] = nc.dram_tensor(f"in_{name}", a.shape, mybir.dt.from_np(a.dtype), kind="ExternalInput").ap()
    out = nc.dram_tensor("out_0", (B, S, D), F32, kind="ExternalOutput").ap()
    build(nc, I, out)
    result = run_bass_kernel_spmd(nc, [maps], core_ids=[0])
    return result.results[0]["out_0"]
```

```python
from contextlib import ExitStack
import math

import numpy as np

import concourse.bass as bass
from concourse import mybir

F32 = mybir.dt.float32
F16 = mybir.dt.float16
ALU = mybir.AluOpType
ACT = mybir.ActivationFunctionType
AX = mybir.AxisListType

P = 128
D = 128
B = 4
S = 512
T = B * S
NT = T // P
TPB = S // P
BANK = 512
NQK = 16
H0, DH0, DV0 = 8, 32, 64
DH1 = 8
RD = DH1 // 2
LAMBDA_INIT = 0.8 - 0.6 * math.exp(-0.3)
SROWS = 96
PRING = 16
N_IN, N_PROC, N_OUT, D_PV = 1024, 512, 1024, 64
K_IN, K_PROC, K_OUT = N_IN // 8, N_PROC // 8, N_OUT // 8
NE, FF = 8, 512
NX = NE + 1
WSCALE = 64.0
MSHIFT = -3.0e38
EPS_LN, EPS_RMS = 1e-5, 1e-8


class Links:

    def __init__(self, eng, sem, base=0):
        self.eng, self.sem, self.base, self.n = eng, sem, base, 0

    def __call__(self, ins):
        self.n += 1
        ins.then_inc(self.sem, 1)
        self.eng.wait_ge(self.sem, self.base + self.n)


class AttnPlan:

    def __init__(self, layer):
        self.layer = layer
        self.J = 2 if layer == 0 else 4
        self.W = NQK // self.J
        self.dh = DH0 if layer == 0 else DH1
        self.scale = self.dh ** -0.5
        self.nd = 6
        self.ring_steps = PRING // self.J
        self.credit = self.ring_steps - 5 if layer == 0 else self.ring_steps
        if layer == 0:
            self.pieces = {(0, 2): "q0", (1, 2): "k0", (2, 2): "v0", (3, 2): "v1", (4, 2): "q1", (5, 2): "k1"}
            self.vcopies = {1: (3, 0), 6: (0, 16), 7: (2, 24)}
            self.vregions = {1: [3], 6: [0, 1], 7: [2]}
            self.bounces = {2: 0, 6: 1}
            self.last_v = 6
            self.banks = (6, 6)
        else:
            self.pieces = {}
            self.proj = {(0, 0, 0): 0, (0, 0, 1): 1, (0, 1, 0): 2, (0, 1, 1): 3, (0, 2, 1): 4}
            self.last_v = 3
            self.banks = (6, 7)
        self.NP = len(self.pieces)
        self.per_window = 2 * self.J + 1
        self.U0 = self.NP + 2 * self.per_window - 1
        self.UB = self.W * self.per_window + self.NP
        assert self.UB % 2 == 0

    @staticmethod
    def stack_rows(M):
        return [(M.Qs, 0, 0), (M.Qs, 1, 0), (M.Qs, 2, 1), (M.Ks, 0, 2), (M.Ks, 1, 3), (M.Ks, 2, 2)]

    def before(self, w, last):
        return w * self.per_window + (0 if last else sum(1 for p in self.pieces if p[0] < w))

    def use(self, w, s, kind, i=0, last=False):
        n = self.before(w, last)
        ahead = not (last and w >= self.W - 2)
        for step in range(4):
            for pair in range(self.J // 2 if ahead else 0):
                if kind == "sm" and (step, pair) == (s, i):
                    return n
                n += 1
            if step == 0:
                if kind == "tr":
                    return n
                n += 1
            if not last and (w, step) in self.pieces:
                if kind == "piece" and step == s:
                    return n
                n += 1

    @staticmethod
    def projection_bank(i, prologue):
        return i if prologue else 7

    def bank(self, base, local):
        return 2 * (((base if isinstance(base, int) else self.U0) + local) % 2)


def attention(nc, M, plan):
    A, L, J, W = plan, plan.layer, plan.J, plan.W
    PS = M.PS
    ctx = ExitStack()

    def sem(name, layer=plan.layer):
        return ctx.enter_context(nc.semaphore(f"l{L}_{name}")) if layer == L else None

    with ctx:
        weights_in = sem("weights_in", 0)
        wq_in = sem("wq_in", 0)
        xb_in = sem("xb_in")
        stack_in = [sem(f"stack_in{g}") for g in range(2 if L == 0 else W)]
        bounce_out = [sem(f"bounce_out{h}") for h in range(2 - L)]
        all_in = sem("all_in", 1)
        max_in = [sem(f"max_in{p}") for p in range(2)]
        sums_out = [sem(f"sums_out{p}", 0) for p in range(2)]
        sm_ready = sem("sm_ready")
        sm_free = sem("sm_free")
        st_ready = sem("st_ready")
        exp_done = sem("exp_done")
        added = sem("added", 0)
        pv_done = sem("pv_done")
        o_evac = sem("o_evac")
        sums_evac = sem("sums_evac", 0)
        hi_done = sem("hi_done", 0)
        v_copied = sem("v_copied")
        own = sem("own")
        pool_own = sem("pool_own")
        carried = sem("carried")
        pool_carried = sem("pool_carried")
        ready = sem("ready", 0)
        csum_in = sem("csum_in", 0)
        factors = sem("factors", 0)
        r_out = sem("r_out", 0)
        r_in = sem("r_in", 0)
        divided = sem("divided", 0)
        proj_ready = sem("proj_ready", 1)
        proj_out = sem("proj_out", 1)
        q_split = sem("q_split", 1)
        k_split = sem("k_split", 1)
        v_next = sem("v_next", 1)
        doubled = sem("doubled", 1)
        lam_e = sem("lam_e", 0)
        block = ctx.enter_context(nc.Block())

        piece_order = list(A.pieces.values())

        @block.sync
        def _(sp):
            def load_xb(b):
                if L == 0:
                    sp.dma_start(M.xb[:], M.xT_dram[:, bass.ds(b * S, S)]).then_inc(xb_in, 16)
                else:
                    sp.dma_start(M.xb[:], M.xT[:, bass.ds(b * S, S)]).then_inc(xb_in, 16)

            def wait(s, value):
                sp.wait_ge(s, value)
                if not isinstance(value, int):
                    sp.sem_inc(carried, 1)

            def bounce(h, n):
                if L == 0:
                    sp.dma_start(M.qk0_dram[h].rearrange("k (c p) t -> p (k c) t", p=P), M.qk[:, h].rearrange("p k c t -> p (k c) t"))\
                      .then_inc(bounce_out[h], 16)
                else:
                    sp.dma_start(M.qk_dram.rearrange("k p t -> p k t"), M.qk[:, 0, :, 0, :]).then_inc(bounce_out[h], 16)
                wait(bounce_out[h], 16 * (n + 1))

            def load_stack(g):
                for stack, blk, part in A.stack_rows(M):
                    if L == 0:
                        n, src = NQK // 2, M.qk0_dram[g, part]
                    else:
                        n, src = J, M.qk_dram[part, g * J * DH1:(g + 1) * J * DH1, :]
                    sp.dma_start(stack[A.dh * blk:A.dh * (blk + 1), g * n:(g + 1) * n, :],
                                 src.rearrange("(h p) t -> p h t", p=A.dh)).then_inc(stack_in[g], 16)

            def max_row(u, g, par):
                wait(sm_free, u + 1)
                sp.dma_start(M.Qs[SROWS:SROWS + 1, g * J:(g + 1) * J, :], M.mrow[par][0:4 * J, :])\
                  .then_inc(max_in[par], 16)

            if L == 0:
                load_xb(0)
                M.load_weights(sp, wq_in, weights_in)
                for par in range(2):
                    sp.sem_inc(sums_out[par], 1)
            if L == 0:
                for h in range(2):
                    sp.wait_ge(sm_free, (2, 6)[h])
                    bounce(h, 0)
                    load_stack(h)
            else:
                sp.wait_ge(q_split, 1)
                sp.wait_ge(k_split, 1)
                bounce(0, 0)
                for stack, blk, part in A.stack_rows(M):
                    sp.dma_start(stack[A.dh * blk:A.dh * (blk + 1), :, :],
                                 M.qk_dram[part].rearrange("(h p) t -> p h t", p=A.dh)).then_inc(all_in, 16)
                sp.wait_ge(all_in, 16 * A.nd)
                for g in range(W):
                    sp.sem_inc(stack_in[g], 16 * A.nd)
            max_row(A.NP + A.per_window - 1, 0, 0)

            def batch(b, first, last):
                base, stb = A.U0 + b * A.UB, 4 * J * W * b

                def store_sums(v):
                    wait(sums_evac, 1 + W * b + v + 1)
                    sp.dma_start(M.sums_dram[bass.ds(b, 1), v].rearrange("a t q -> (a t) q"),
                                 M.sums[v % 2][0:2 * 32:32, :]).then_inc(sums_out[v % 2], 16)

                if not last:
                    if L == 0:
                        wait(sm_free, base - 1)
                    else:
                        wait(proj_out, 5 * (b + 1))
                    load_xb(b + 1)
                for w in range(W):
                    if not (last and w == W - 1):
                        max_row(base + A.use(w, 0, "tr", last=last), (w + 1) % W, (w + 1) % 2)
                    if L == 0 and w:
                        store_sums(w - 1)
                    if L == 0 and w == 0 and not first:
                        wait(st_ready, stb)
                        load_stack(1)
                    if L == 0 and w == 4 and not last:
                        wait(st_ready, stb + 4 * J * 4)
                        load_stack(0)
                    if L == 0 and not first and w == 1:
                        for par in range(2):
                            wait(sums_out[par], 1 + 16 * (W // 2 * b))
                        sp.dma_start(M.csum[:], M.sums_dram[bass.ds(b - 1, 1)].rearrange("o g j (a c) -> (o g j a) c", c=64))\
                          .then_inc(csum_in, 16)
                    if L == 0 and not first and w == 2:
                        wait(factors, b)
                        sp.dma_start(M.r_dram[bass.ds(b - 1, 1)].rearrange("o (p c) -> (o p) c", c=64), M.crec[:])\
                          .then_inc(r_out, 16)
                        wait(r_out, 16 * b)
                        wait(divided, 1 + 12 * (b - 1))
                        for half in range(2):
                            for j in range(2):
                                src = M.r_dram[bass.ds(b - 1, 1)].rearrange("o (h s j q) -> o j s h q", h=4, s=2, j=2)
                                sp.dma_start(M.rsum[half][64 * j:64 * j + 64], src[:, j, half].broadcast_to([64, 4, S]))\
                                  .then_inc(r_in, 16)
                    if L == 0 and not last and w in A.bounces:
                        h = A.bounces[w]
                        wait(sm_free, base + A.use(1 + 4 * h, 2, "piece") + 1)
                        wait(stack_in[h], 16 * A.nd * (b + 1))
                        bounce(h, b + 1)
                    if L == 1 and not last:
                        if w == 0:
                            wait(q_split, b + 2)
                            wait(k_split, b + 2)
                            for g in range(W):
                                wait(stack_in[g], 16 * A.nd * (b + 1))
                            bounce(0, b + 1)
                        wait(st_ready, stb + 4 * J * (w + 1))
                        load_stack(w)
                if L == 0:
                    store_sums(W - 1)

            batch(0, True, False)
            with sp.Fori(1, B - 1) as b:
                batch(b, False, False)
            batch(B - 1, False, True)
            if L == 0:
                for par in range(2):
                    sp.wait_ge(sums_out[par], 1 + 16 * B * W // 2)

        @block.gpsimd
        def _(pool):
            def wait(s, value):
                pool.wait_ge(s, value)
                if not isinstance(value, int):
                    pool.sem_inc(pool_carried, 1)

            if L == 0:
                nc.gpsimd.memset(M.ones[:], 1.0).then_inc(pool_own, 1)
                wait(pool_own, 1)
                nc.gpsimd.memset(M.Ks[SROWS:SROWS + 1], 1.0).then_inc(ready, 1)

                def batch(b):
                    n = 0
                    steps = 4 * W * b
                    own0 = 1 + (2 * W - 1) * b
                    for w in range(W):
                        wait(pv_done, A.credit + steps + 4 * (w - 1) + 2)
                        wait(exp_done, J * (steps + 4 * w + 2))
                        for j in range(J):
                            a, c = ((4 * w + i) * J + j for i in range(2))
                            ins = nc.gpsimd.tensor_tensor(M.esum[w % 2][:, j, :], M.Pr[:, a % PRING, :],
                                                          M.Pr[:, c % PRING, :], ALU.add)
                        ins.then_inc(pool_own, 1)
                        for kt in (2,) if w == W - 1 else (2, 3):
                            n += 1
                            wait(pool_own, own0 + n)
                            wait(exp_done, J * (steps + 4 * w + kt + 1))
                            for j in range(J):
                                c = (4 * w + kt) * J + j
                                ins = nc.gpsimd.tensor_tensor(M.esum[w % 2][:, j, :], M.esum[w % 2][:, j, :],
                                                              M.Pr[:, c % PRING, :], ALU.add)
                            ins.then_inc(added if w == W - 1 or kt == 3 else pool_own, 1)

                with pool.Fori(0, B) as b:
                    batch(b)
            else:
                def turn_q(n):
                    raw = M.raw
                    wait(proj_out, 5 * n + 2)
                    nc.gpsimd.tensor_tensor(M.raw[:, 0, :], M.raw[:, 0, :], M.cos[:], ALU.mult)
                    nc.gpsimd.tensor_tensor(M.raw[:, 1, :], M.raw[:, 1, :], M.sin[:], ALU.mult).then_inc(pool_own, 1)
                    wait(pool_own, 3 * n + 1)
                    nc.gpsimd.tensor_tensor(M.raw[:, 0, :], M.raw[:, 0, :], M.raw[:, 1, :], ALU.add).then_inc(pool_own, 1)
                    wait(pool_own, 3 * n + 2)
                    if not (isinstance(n, int) and n == 0):
                        wait(bounce_out[0], 16 * n)
                    nc.gpsimd.tensor_copy(M.qk[:, 0, 0, 0, :], M.raw[:, 0, :]).then_inc(pool_own, 1)
                    wait(pool_own, 3 * n + 3)
                    nc.gpsimd.tensor_tensor(M.qk[:, 0, 1, 0, :], M.raw[:, 0, :], M.qk[:, 0, 0, 0, :], ALU.subtract)\
                      .then_inc(q_split, 1)

                def take_v(n):
                    wait(proj_out, 5 * n + 5)
                    if not (isinstance(n, int) and n == 0):
                        wait(v_copied, 4 * n)
                    nc.gpsimd.tensor_tensor(
                        M.Vn[:].rearrange("p k (h e) -> p k h e", e=32)[:, :, :, 0:DH1],
                        M.raw[:, 4, :].rearrange("p (k h e) -> p k h e", k=4, e=DH1),
                        M.bv[:].rearrange("p (k h e) -> p k h e", k=1, e=DH1).broadcast_to([P, 4, NQK, DH1]),
                        ALU.add).then_inc(v_next, 1)

                def copy_v(region):
                    cols = (slice(None), slice(None), slice(4 * region, 4 * region + 4), slice(0, DH1))
                    nc.gpsimd.tensor_copy(M.V[:].rearrange("p k (h e) -> p k h e", e=32)[cols],
                                          M.Vn[:].rearrange("p k (h e) -> p k h e", e=32)[cols]).then_inc(v_copied, 1)

                turn_q(0)
                wait(own, 7)
                take_v(0)
                wait(v_next, 1)
                for region in range(3):
                    copy_v(region)
                def batch(b, first, last):
                    wait(pv_done, A.credit + 4 * W * b)
                    copy_v(3)
                    if last:
                        return
                    turn_q(b + 1)
                    take_v(b + 1)
                    wait(v_next, b + 2)
                    wait(pv_done, A.credit + 4 * W * b + 12)
                    for region in range(3):
                        copy_v(region)

                with pool.Fori(0, B - 1) as b:
                    batch(b, False, False)
                batch(B - 1, False, True)
                nc.gpsimd.tensor_tensor(M.x[:], M.x[:], M.x[:], ALU.add).then_inc(doubled, 1)
                wait(doubled, 1)
                nc.gpsimd.tensor_tensor(M.x[:], M.x[:], M.bo[:].rearrange("p (o d) -> p o d", o=1).broadcast_to([P, NT, D]),
                                        ALU.add)

        @block.tensor
        def _(pe):
            pe.sem_inc(pv_done, A.credit)
            if L == 0:
                pe.wait_ge(wq_in, 16)

            def free(base, local):
                u = base + local
                if not (isinstance(u, int) and u < 2):
                    pe.wait_ge(sm_free, u - 1)
                return A.bank(base, local)

            def score_max(base, local, g, qt, pair):
                bank = free(base, local)
                for i in range(2):
                    slot = g * J + 2 * pair + i
                    mm = pe.matmul(PS[:, bank + i, :], M.Qs[0:SROWS, slot, qt * P:(qt + 1) * P],
                                   M.Ks[0:SROWS, slot, :], start=True, stop=True)
                mm.then_inc(sm_ready, 1)

            def turn_max(base, local, par, written):
                pe.wait_ge(sm_free, base + written)
                bank = free(base, local)
                pe.transpose(PS[0:4 * J, bank, 0:P], M.negm[:, par, 0:4 * J], M.ident[:]).then_inc(sm_ready, 1)

            def piece(base, local, name, nb):
                pe.wait_ge(xb_in, 16 * (nb + 1))
                bank = free(base, local)
                for i in range(2):
                    c = 2 * int(name[1]) + i
                    if name[0] == "v":
                        mm = pe.matmul(PS[:, bank + i, :], M.xb[:, c * P:(c + 1) * P], M.Wkv[:, 512:1024],
                                       start=True, stop=True)
                    else:
                        w_ = (M.Wq if name[0] == "q" else M.Wkv)[:, c * P:(c + 1) * P]
                        mm = pe.matmul(PS[:, bank + i, :], w_, M.xb[:], start=True, stop=True)
                mm.then_inc(sm_ready, 1)

            def project(i, nb):
                prologue = isinstance(nb, int) and nb == 0
                xb = M.xT[:, 0:S] if prologue else M.xb[:]
                if not prologue:
                    pe.wait_ge(xb_in, 16 * nb)
                if i == 0 and not prologue:
                    pe.wait_ge(o_evac, 2 + W * (nb - 1))
                if not prologue:
                    pe.wait_ge(proj_out, 5 * nb + i)
                bank = A.projection_bank(i, prologue)
                if i < 4:
                    w_ = (M.WinR if i % 2 else M.Win)[:, (i // 2) * D:(i // 2 + 1) * D]
                    mm = pe.matmul(PS[:, bank, :], w_, xb, start=True, stop=True)
                else:
                    for c in range(4):
                        mm = pe.matmul(PS[:, bank, c * D:(c + 1) * D], xb[:, c * P:(c + 1) * P], M.Win[:, 2 * D:3 * D],
                                       start=True, stop=True)
                mm.then_inc(proj_ready, 1)

            def score_t(k, b, j):
                w, kt = k // 4, k % 4
                n, slot = k * J + j, w * J + j
                nb = 4 * W * J * b + n
                if not (isinstance(nb, int) and nb < 2):
                    pe.wait_ge(exp_done, nb - 1)
                if j == 0 and kt == 0:
                    pe.wait_ge(max_in[w % 2], 16 * (W // 2 * b + w // 2 + 1))
                pe.matmul(PS[:, 4 + n % 2, :], M.Ks[0:SROWS + 1, slot, kt * P:(kt + 1) * P],
                          M.Qs[0:SROWS + 1, slot, :], start=True, stop=True).then_inc(st_ready, 1)

            def product(k, b, heads, last):
                w, kt = k // 4, k % 4
                bank = A.banks[w % 2]
                if kt == 0 and heads[0] == 0:
                    pe.wait_ge(o_evac, 1 + W * b + w)
                    if L == 1 and w == 1:
                        pe.wait_ge(proj_out, 5 * (b + (1 if last else 2)))
                    if w in (0, A.last_v):
                        pe.wait_ge(v_copied, 3 + 4 * b + (1 if w else 0))
                for j in heads:
                    slot = (k * J + j) % PRING
                    pe.wait_ge(exp_done, 4 * W * J * b + J * k + j + 1)
                    if L == 0:
                        hp = w // 2
                        mm = pe.matmul(PS[64 * j:64 * j + 64, bank, :],
                                       M.V[:, kt, hp * P + DV0 * j:hp * P + DV0 * (j + 1)], M.Pr[:, slot, :],
                                       start=(kt == 0), stop=(kt == 3), skip_group_check=True)
                    else:
                        h = w * J + j
                        mm = pe.matmul(PS[32 * j:32 * j + 32, bank, :], M.V[:, kt, 32 * h:32 * h + 32], M.Pr[:, slot, :],
                                       start=(kt == 0), stop=(kt == 3), skip_group_check=True)
                if L == 0 and (k == 4 * W - 1 or (kt == 1 and w)):
                    v = w if kt == 3 else w - 1
                    pe.wait_ge(sums_evac, 1 + W * b + v)
                    if kt == 3:
                        for j in range(J):
                            pe.matmul(PS[32 * j:32 * j + 32, 7, :], M.ones[:, 0:32], M.Pr[:, (k * J + j) % PRING, :],
                                      start=True, stop=False, skip_group_check=True)
                    pe.wait_ge(added, W * b + v + 1)
                    for j in range(J):
                        mm = pe.matmul(PS[32 * j:32 * j + 32, 7, :], M.ones[:, 0:32], M.esum[v % 2][:, j, :],
                                       start=(kt == 1), stop=True, skip_group_check=True)
                if heads[-1] == J - 1:
                    mm.then_inc(pv_done, 1)

            if L == 0:
                for i, name in enumerate(piece_order):
                    if i == 1:
                        pe.wait_ge(weights_in, 16 * M.n_l0)
                        pe.wait_ge(ready, 1)
                    piece(0, i, name, 0)
            else:
                for i in range(5):
                    project(i, 0)
                pe.wait_ge(proj_out, 5)
            for g in range(2):
                pe.wait_ge(stack_in[0 if L == 0 else g], 16 * A.nd)
                for qt in range(4):
                    for pair in range(J // 2):
                        score_max(0, A.NP + g * A.per_window + qt * (J // 2) + pair, g, qt, pair)
                if g == 0:
                    turn_max(0, A.NP + A.per_window - 1, 0, A.NP + A.per_window - 1)
            for j in range(J):
                score_t(0, 0, j)

            def batch(b, last):
                base = A.U0 + b * A.UB
                for k in range(4 * W):
                    w, s = k // 4, k % 4
                    ahead = not (last and w >= W - 2)
                    g = (w + 2) % W
                    nk, nb = (k + 1) % (4 * W), b if k < 4 * W - 1 else b + 1
                    if ahead and s == 0 and (L == 1 or g % 4 == 0):
                        pe.wait_ge(stack_in[g // 4 if L == 0 else g], 16 * A.nd * (b + (2 if w + 2 >= W else 1)))
                    scores_left = not (last and k == 4 * W - 1)
                    turn_due = s == 0 and not (last and w == W - 1)
                    turn = A.use(w, 0, "tr", last=last) if turn_due else None
                    written = turn - (J // 2 if ahead else 0) if turn_due else None
                    if L == 0:
                        if scores_left:
                            score_t(nk, nb, 0)
                        if ahead:
                            score_max(base, A.use(w, s, "sm", 0, last), g, s, 0)
                        if scores_left:
                            score_t(nk, nb, 1)
                        if not last and (w, s) in A.pieces:
                            piece(base, A.use(w, s, "piece"), A.pieces[(w, s)], b + 1)
                        product(k, b, (0, 1), last)
                    else:
                        for place in range(2):
                            if scores_left:
                                score_t(nk, nb, 2 * place)
                            late = s == 1 and place == 0
                            if ahead and not late:
                                score_max(base, A.use(w, s, "sm", place, last), g, s, place)
                            if scores_left:
                                score_t(nk, nb, 2 * place + 1)
                            product(k, b, (2 * place, 2 * place + 1), last)
                            if ahead and late:
                                score_max(base, A.use(w, s, "sm", place, last), g, s, place)
                            if not last and (w, s, place) in A.proj:
                                project(A.proj[(w, s, place)], b + 1)
                    if turn_due:
                        turn_max(base, turn, (w + 1) % 2, written)

            with pe.Fori(0, B - 1) as b:
                batch(b, False)
            batch(B - 1, True)

        @block.scalar
        def _(act):
            def exp(k, b, j):
                n = k * J + j
                act.wait_ge(st_ready, 4 * W * J * b + n + 1)
                if j == 0:
                    act.wait_ge(pv_done, 4 * W * b + k + 1)
                nc.scalar.activation(M.Pr[:, n % PRING, :], PS[:, 4 + n % 2, :], ACT.Exp, scale=A.scale)\
                  .then_inc(exp_done, 1)

            def high_parts(base, local, name):
                u = base + local
                bank = A.bank(base, local)
                act.wait_ge(sm_ready, u + 1)
                part = 0 if name[0] == "q" else 2
                nc.scalar.activation(M.qk[:, int(name[1]), part], PS[:, bank:bank + 2, :], ACT.Copy).then_inc(hi_done, 1)

            def take_output(w, b):
                act.wait_ge(pv_done, A.credit + 4 * W * b + 4 * (w + 1))
                nc.scalar.activation(M.o[:, w, bass.ds(b * S, S)], PS[:, A.banks[w % 2], :], ACT.Copy).then_inc(o_evac, 1)

            def take_projection(i, nb):
                act.wait_ge(proj_ready, 5 * nb + i + 1)
                if not (isinstance(nb, int) and nb == 0):
                    if i == 0:
                        act.wait_ge(q_split, nb)
                    elif i == 2:
                        act.wait_ge(k_split, nb)
                    elif i == 4:
                        act.wait_ge(v_next, nb)
                src = PS[:, A.projection_bank(i, isinstance(nb, int) and nb == 0), :]
                if i < 4:
                    bias = M.bqk[:, (0, 2, 1, 3)[i]:(0, 2, 1, 3)[i] + 1]
                    nc.scalar.activation(M.raw[:, i, :], src, ACT.Identity, bias=bias).then_inc(proj_out, 1)
                else:
                    nc.scalar.activation(M.raw[:, i, :], src, ACT.Copy).then_inc(proj_out, 1)

            if L == 0:
                for i, name in enumerate(piece_order):
                    if name[0] in "qk":
                        high_parts(0, i, name)
                act.wait_ge(own, 2)
                nc.scalar.activation(M.lams[:, 2:4], M.lams[:, 0:2], ACT.Exp).then_inc(lam_e, 1)
            else:
                for i in range(5):
                    take_projection(i, 0)
            for j in range(J):
                exp(0, 0, j)
            act.sem_inc(o_evac, 1 + L)
            if L == 0:
                act.sem_inc(sums_evac, 1)

            def batch(b, last):
                base = A.U0 + b * A.UB
                for k in range(4 * W):
                    w, s = k // 4, k % 4
                    for j in range(J):
                        if k < 4 * W - 1:
                            exp(k + 1, b, j)
                        elif not last:
                            exp(0, b + 1, j)
                        if L == 1 and s == 0 and w and j == 1:
                            take_output(w - 1, b)
                        if L == 1 and not last and j % 2 == 1 and (w, s, j // 2) in A.proj:
                            take_projection(A.proj[(w, s, j // 2)], b + 1)
                    if L == 0 and not last and (w, s) in A.pieces and A.pieces[(w, s)][0] in "qk":
                        name = A.pieces[(w, s)]
                        act.wait_ge(bounce_out[int(name[1])], 16 * (b + 1))
                        high_parts(base, A.use(w, s, "piece"), name)
                    if L == 1 and w == W - 1 and s == 3:
                        take_output(w, b)
                    if L == 0 and s == 3:
                        act.wait_ge(pv_done, A.credit + 4 * W * b + k + 1)
                        nc.scalar.activation(M.o[:, w % 2, w // 2, bass.ds(b * S, S)], PS[:, 6, :], ACT.Copy)\
                          .then_inc(o_evac, 1)
                    if L == 0 and (k == 4 * W - 1 or (w and s == 2)):
                        v = w if s == 3 else w - 1
                        act.wait_ge(pv_done, A.credit + 4 * W * b + (k + 1 if s == 3 else k))
                        act.wait_ge(sums_out[v % 2], 1 + 16 * (W // 2 * b + v // 2))
                        nc.scalar.activation(M.sums[v % 2][0:64, :], PS[0:64, 7, :], ACT.Copy).then_inc(sums_evac, 1)

            with act.Fori(0, B - 1) as b:
                batch(b, False)
            batch(B - 1, True)

        @block.vector
        def _(dve):
            def reduce(base, local, par, qt, pair):
                bank = A.bank(base, local)
                dve.wait_ge(sm_ready, base + local + 1)
                cols = M.negm[:, par, 8 * pair:8 * pair + 8].rearrange("p (j q) -> p j q", q=4)[:, :, qt]
                nc.vector.tensor_reduce(cols, PS[:, bank:bank + 2, :], AX.X, ALU.max, negate=True).then_inc(sm_free, 1)

            def take_row(base, local, par, count):
                bank = A.bank(base, local)
                dve.wait_ge(sm_ready, base + local + 1)
                if not (isinstance(count, int) and count == 0):
                    dve.wait_ge(max_in[par], 16 * count)
                nc.vector.tensor_copy(M.mrow[par][0:4 * J, :], PS[0:4 * J, bank, 0:P]).then_inc(sm_free, 1)

            def piece(base, local, name, hi_count):
                bank = A.bank(base, local)
                dve.wait_ge(sm_ready, base + local + 1)
                c = 2 * int(name[1])
                if name[0] == "v":
                    nc.vector.tensor_copy(M.Vn[:, c:c + 2, :], PS[:, bank:bank + 2, :]).then_inc(sm_free, 1)
                else:
                    part = 0 if name[0] == "q" else 2
                    dve.wait_ge(hi_done, hi_count)
                    nc.vector.tensor_tensor(M.qk[:, int(name[1]), part + 1], PS[:, bank:bank + 2, :],
                                            M.qk[:, int(name[1]), part], ALU.subtract).then_inc(sm_free, 1)

            def turn_k(i, n, own0):
                raw = M.raw
                if i == 0:
                    dve.wait_ge(proj_out, 5 * n + 3)
                    nc.vector.tensor_tensor(raw[:, 2, :], raw[:, 2, :], M.cos[:], ALU.mult).then_inc(own, 1)
                elif i == 1:
                    dve.wait_ge(proj_out, 5 * n + 4)
                    nc.vector.tensor_tensor(raw[:, 3, :], raw[:, 3, :], M.sin[:], ALU.mult).then_inc(own, 1)
                elif i == 2:
                    dve.wait_ge(own, own0 + 2)
                    nc.vector.tensor_tensor(raw[:, 2, :], raw[:, 2, :], raw[:, 3, :], ALU.add).then_inc(own, 1)
                elif i == 3:
                    dve.wait_ge(own, own0 + 3)
                    if not (isinstance(n, int) and n == 0):
                        dve.wait_ge(bounce_out[0], 16 * n)
                    nc.vector.tensor_copy(M.qk[:, 0, 2, 0, :], raw[:, 2, :]).then_inc(own, 1)
                else:
                    dve.wait_ge(own, own0 + 4)
                    nc.vector.tensor_tensor(M.qk[:, 0, 3, 0, :], raw[:, 2, :], M.qk[:, 0, 2, 0, :], ALU.subtract)\
                      .then_inc(k_split, 1)

            def divide(i, b):
                hp, kind = i // 3, i % 3
                o = [M.o[:, half, hp, bass.ds((b - 1) * S, S)] for half in range(2)]
                if i == 0:
                    dve.wait_ge(o_evac, 1 + W * b)
                    dve.wait_ge(r_in, 64 * b)
                if kind < 2:
                    ins = nc.vector.tensor_tensor(o[kind], o[kind], M.rsum[kind][:, hp, :], ALU.mult)
                else:
                    dve.wait_ge(divided, 1 + 12 * (b - 1) + i)
                    ins = nc.vector.tensor_tensor(o[0], o[0], o[1], ALU.add)
                ins.then_inc(divided, 1)

            def copy_v(region):
                cols = slice(region * P, (region + 1) * P)
                nc.vector.tensor_copy(M.V[:, :, cols], M.Vn[:, :, cols]).then_inc(v_copied, 1)

            hi0 = 4
            if L == 0:
                dve.sem_inc(divided, 1)
                hi = 0
                for i, name in enumerate(piece_order):
                    if name[0] in "qk":
                        hi += 1
                    piece(0, i, name, hi)
                dve.wait_ge(sm_free, 6)
                for region in range(3):
                    copy_v(region)
                link = Links(dve, own)
                dve.wait_ge(weights_in, 16 * M.n_l0)
                link(nc.vector.tensor_tensor(M.lamp[:], M.lam[:].rearrange("p (a b) d -> p a b d", b=2)[:, :, 0, :],
                                             M.lam[:].rearrange("p (a b) d -> p a b d", b=2)[:, :, 1, :], ALU.mult))
                link(nc.vector.tensor_reduce(M.lams[:, 0:2], M.lamp[:], AX.X, ALU.add))
                dve.wait_ge(lam_e, 1)
                link(nc.vector.tensor_tensor(M.lams[:, 4:5], M.lams[:, 3:4], M.lams[:, 2:3], ALU.subtract))
                link(nc.vector.tensor_scalar(M.nlam[:], M.lams[:, 4:5], -LAMBDA_INIT, None, ALU.add))
                link(nc.vector.scalar_tensor_tensor(out=M.sign[:, 0:1], in0=M.sign[:, 2:3], scalar=M.nlam[:, 0:1],
                                                    in1=M.sign[:, 1:2], op0=ALU.mult, op1=ALU.add))
            else:
                for i in range(5):
                    turn_k(i, 0, 0)
                nc.vector.memset(M.Vn[:], 0.0).then_inc(own, 1)
                dve.wait_ge(own, 5)
                nc.vector.memset(M.Vn[:].rearrange("p k (h e) -> p k h e", e=32)[:, :, :, DH1], 1.0).then_inc(own, 1)
                dve.wait_ge(own, 6)
                nc.vector.tensor_copy(M.V[:], M.Vn[:]).then_inc(own, 1)
            for g in range(2):
                for qt in range(4):
                    for pair in range(J // 2):
                        reduce(0, A.NP + g * A.per_window + qt * (J // 2) + pair, g, qt, pair)
                if g == 0:
                    take_row(0, A.NP + A.per_window - 1, 0, 0)

            def batch(b, first, last):
                base = A.U0 + b * A.UB
                hi = 0
                for w in range(W):
                    for s in range(4):
                        for pair in range(J // 2):
                            if not (last and w >= W - 2):
                                reduce(base, A.use(w, s, "sm", pair, last), w % 2, s, pair)
                            if L == 1 and not last:
                                place = 8 * w + 2 * s + pair
                                for i in {3: (0,), 4: (1,), 5: (2, 3), 6: (4,)}.get(place, ()):
                                    turn_k(i, b + 1, 3 + 4 * (b + 1))
                        if s == 0 and not (last and w == W - 1):
                            take_row(base, A.use(w, 0, "tr", last=last), (w + 1) % 2, W // 2 * b + (w + 1) // 2)
                        if L == 1:
                            continue
                        if s == 0 and w == 2 and not first:
                            dve.wait_ge(csum_in, 16 * b)
                            nc.vector.reciprocal(M.crec[:], M.csum[:]).then_inc(own, 1)
                            dve.wait_ge(own, 5 + b)
                            nc.vector.tensor_scalar(M.crec[:], M.crec[:], M.sign[:, 0:1], None, ALU.mult).then_inc(factors, 1)
                        if s and w >= 4 and not first:
                            divide(3 * (w - 4) + s - 1, b)
                        if s == 2 and w in A.vcopies and not (last and w > 1):
                            dve.wait_ge(pv_done, A.credit + 4 * W * b + A.vcopies[w][1])
                            if w > 1:
                                vl = max(p for p in A.pieces if A.pieces[p][0] == "v")
                                dve.wait_ge(sm_free, base + A.use(*vl, "piece") + 1)
                            for region in A.vregions[w]:
                                copy_v(region)
                        if not last and (w, s) in A.pieces:
                            name = A.pieces[(w, s)]
                            if name[0] in "qk":
                                hi += 1
                            piece(base, A.use(w, s, "piece"), name, hi0 + b * hi0 + hi)

            batch(0, True, False)
            with dve.Fori(1, B - 1) as b:
                batch(b, False, False)
            batch(B - 1, False, True)


def spread(ap, n):
    p, a = ap.shape
    return ap.rearrange("p (a o) -> p a o", o=1).broadcast_to([p, a, n])


def l0_output(nc, M):
    PS = M.PS
    HP = H0 // 2
    NTI = N_IN // P
    ctx = ExitStack()

    def sem(name):
        return ctx.enter_context(nc.semaphore(f"out0_{name}"))

    with ctx:
        w_in = sem("w_in")
        x_in = sem("x_in")
        csum_in = sem("csum_in")
        factors = sem("factors")
        r_out = sem("r_out")
        r_in = sem("r_in")
        own = sem("own")
        first_half = sem("first_half")
        second_half = sem("second_half")
        diff = sem("diff")
        sq = sem("sq")
        ms = sem("ms")
        rms = sem("rms")
        inv = sem("inv")
        spr = sem("spr")
        normed = sem("normed")
        yT = sem("yT")
        yT_c = sem("yT_c")
        y = sem("y")
        var = sem("var")
        std = sem("std")
        x1 = sem("x1")
        x1T = sem("x1T")
        x1T_c = sem("x1T_c")
        acts = sem("acts")
        gelu = sem("gelu")
        block = ctx.enter_context(nc.Block())

        @block.sync
        def _(sp):
            sp.dma_start(M.csum[:], M.sums_dram[B - 1].rearrange("g j (a c) -> (g j a) c", c=64)).then_inc(csum_in, 16)
            sp.dma_start(M.gam0[:], M.gamma0_dram).then_inc(w_in, 16)
            sp.dma_start(M.Wout[:], M.Wout_dram.rearrange("(h p) n -> p h n", p=P)).then_inc(w_in, 16)
            sp.dma_start(M.blk[:], M.blk_dram).then_inc(w_in, 16)
            sp.dma_start(M.spread[:], M.spread_dram).then_inc(w_in, 16)
            sp.wait_ge(factors, 1)
            sp.dma_start(M.r_dram[B - 1].rearrange("(p c) -> p c", c=64), M.crec[:]).then_inc(r_out, 16)
            sp.wait_ge(r_out, 16)
            for half in range(2):
                for j in range(2):
                    src = M.r_dram[B - 1:B].rearrange("o (h s j q) -> o j s h q", h=4, s=2, j=2)
                    sp.dma_start(M.rsum[half][64 * j:64 * j + 64], src[:, j, half].broadcast_to([64, 4, S])).then_inc(r_in, 16)
            M.load_ffn(sp)
            sp.wait_ge(first_half, 1)
            sp.dma_start(M.x[:], M.x_dram.rearrange("(t p) d -> p t d", p=P)).then_inc(x_in, 16)

        @block.vector
        def _(dve):
            link = Links(dve, own)
            dve.wait_ge(csum_in, 16)
            link(nc.vector.reciprocal(M.crec[:], M.csum[:]))
            nc.vector.tensor_scalar(M.crec[:], M.crec[:], M.sign[:, 0:1], None, ALU.mult).then_inc(factors, 1)
            dve.wait_ge(w_in, 16 * 4)
            for h in range(HP):
                ins = nc.vector.tensor_scalar(M.Wout[:, h, :], M.Wout[:, h, :], M.gam0[:, 0:1], 1.0 - LAMBDA_INIT,
                                              ALU.mult, ALU.mult)
            link(ins)

            def invert(b):
                dve.wait_ge(rms, b + 1)
                link(nc.vector.tensor_scalar(M.rmsb[b % 2], M.rmsb[b % 2], EPS_RMS, None, ALU.add))
                nc.vector.reciprocal(M.rmsb[b % 2], M.rmsb[b % 2]).then_inc(inv, 1)

            def norm(b):
                for h in range(HP):
                    o = M.o[:, 0, h, b * S:(b + 1) * S]
                    dve.wait_ge(spr, HP * b + h + 1)
                    nc.vector.tensor_tensor(o, o, PS[:, 2 + h % 2, :], ALU.mult).then_inc(normed, 1)

            def finish(b):
                x = M.x[:, TPB * b:TPB * (b + 1), :]
                dve.wait_ge(y, b + 1)
                link(nc.vector.tensor_tensor(x, x, PS[:, 5, :].rearrange("p (t d) -> p t d", d=D), ALU.add))
                layernorm(nc, dve, link, M, TPB * b, TPB, var, std, b + 1, done=x1)

            invert(0)
            norm(0)
            invert(1)
            o = M.o[:, :, :, (B - 1) * S:B * S]
            dve.wait_ge(r_in, 64)
            nc.vector.tensor_tensor(o[:, 0], o[:, 0], M.rsum[0][:], ALU.mult).then_inc(first_half, 1)
            for b in range(B):
                if b + 1 < B:
                    norm(b + 1)
                if b == 0:
                    dve.wait_ge(x_in, 16)
                finish(b)
                if b + 2 < B:
                    invert(b + 2)

        @block.gpsimd
        def _(pool):
            o = M.o[:, :, :, (B - 1) * S:B * S]
            pool.wait_ge(r_in, 64)
            nc.gpsimd.tensor_tensor(o[:, 1], o[:, 1], M.rsum[1][:], ALU.mult).then_inc(second_half, 1)
            pool.wait_ge(second_half, 1)
            pool.wait_ge(first_half, 1)
            nc.gpsimd.tensor_tensor(o[:, 0], o[:, 0], o[:, 1], ALU.add).then_inc(diff, 1)

        @block.scalar
        def _(act):
            def square(b):
                if b == B - 1:
                    act.wait_ge(diff, 1)
                if b >= 2:
                    act.wait_ge(ms, b - 1)
                nc.scalar.activation(M.sqb[b % 2], M.o[:, 0, :, b * S:(b + 1) * S], ACT.Square).then_inc(sq, 1)

            def root(b):
                act.wait_ge(ms, b + 1)
                if b >= 2:
                    act.wait_ge(spr, HP * (b - 1))
                nc.scalar.activation(M.rmsb[b % 2], PS[:, 4, :], ACT.Sqrt).then_inc(rms, 1)

            def take_yT(b):
                act.wait_ge(yT, b + 1)
                nc.scalar.activation(M.yT[b % 2][:], PS[:, 6, :], ACT.Copy).then_inc(yT_c, 1)

            square(0)
            root(0)
            square(1)
            root(1)
            take_yT(0)
            for b in range(B):
                if b + 2 < B:
                    square(b + 2)
                    root(b + 2)
                act.wait_ge(var, b + 1)
                nc.scalar.activation(M.std[:, 0:TPB], M.mv[:, 0:TPB, 1], ACT.Sqrt, bias=M.eps[:, 0:1]).then_inc(std, 1)
                if b + 1 < B:
                    take_yT(b + 1)
                act.wait_ge(x1T, b + 1)
                if b == 0:
                    act.wait_ge(second_half, 1)
                nc.scalar.activation(M.xT[:, b * S:(b + 1) * S], PS[:, 7, :], ACT.Copy).then_inc(x1T_c, 1)
                for n in range(NTI):
                    i = b * NTI + n
                    act.wait_ge(acts, i + 1)
                    if i >= 2:
                        act.wait_ge(gelu, i - 1)
                    nc.scalar.activation(M.junk[i % 2], PS[:, i % 2, :], ACT.Gelu, accum_out=M.actsum[:, n, b:b + 1])\
                      .then_inc(gelu, 1)

        @block.tensor
        def _(pe):
            pe.wait_ge(w_in, 16 * 4)

            def mean_squares(b):
                pe.wait_ge(sq, b + 1)
                if b >= 1:
                    pe.wait_ge(rms, b)
                for h in range(HP):
                    mm = pe.matmul(PS[32 * h:32 * h + 32, 4, :], M.blk[:], M.sqb[b % 2][:, h, :], start=True, stop=True,
                                   skip_group_check=True)
                mm.then_inc(ms, 1)

            def spread_factors(b):
                pe.wait_ge(inv, b + 1)
                for h in range(HP):
                    if HP * b + h >= 2:
                        pe.wait_ge(normed, HP * b + h - 1)
                    pe.matmul(PS[:, 2 + h % 2, :], M.spread[:, h * P:(h + 1) * P], M.rmsb[b % 2], start=True, stop=True)\
                      .then_inc(spr, 1)

            def project(b):
                pe.wait_ge(own, 2)
                if b >= 1:
                    pe.wait_ge(yT_c, b)
                for h in range(HP):
                    pe.wait_ge(normed, HP * b + h + 1)
                    mm = pe.matmul(PS[:, 6, :], M.Wout[:, h, :], M.o[:, 0, h, b * S:(b + 1) * S],
                                   start=(h == 0), stop=(h == HP - 1))
                mm.then_inc(yT, 1)

            def turn_y(b):
                pe.wait_ge(yT_c, b + 1)
                if b >= 1:
                    pe.wait_ge(x1, b)
                for t in range(TPB):
                    mm = pe.transpose(PS[:, 5, t * P:(t + 1) * P], M.yT[b % 2][:, t * P:(t + 1) * P], M.ident[:])
                mm.then_inc(y, 1)

            mean_squares(0)
            mean_squares(1)
            spread_factors(0)
            project(0)
            turn_y(0)
            for b in range(B):
                if b + 1 < B:
                    spread_factors(b + 1)
                if b + 2 < B:
                    mean_squares(b + 2)
                if b + 1 < B:
                    project(b + 1)
                pe.wait_ge(x1, b + 1)
                if b >= 1:
                    pe.wait_ge(x1T_c, b)
                for t in range(TPB):
                    mm = pe.transpose(PS[:, 7, t * P:(t + 1) * P], M.x[:, TPB * b + t, :], M.ident[:])
                mm.then_inc(x1T, 1)
                if b + 1 < B:
                    turn_y(b + 1)
                if b == 0:
                    pe.wait_ge(M.ffn_in, 16 * M.n_ffn)
                pe.wait_ge(x1T_c, b + 1)
                for n in range(NTI):
                    i = b * NTI + n
                    if i >= 2:
                        pe.wait_ge(gelu, i - 1)
                    pe.matmul(PS[:, i % 2, :], M.patT[:, n * P:(n + 1) * P], M.xT[:, b * S:(b + 1) * S],
                              start=True, stop=True).then_inc(acts, 1)


def layernorm(nc, dve, link, M, first, n, var, std, count, out=None, done=None):
    def src(t):
        return M.x[:, first + t, :]
    out = src if out is None else out
    for t in range(n):
        ins = nc.vector.bn_stats(M.stats[:, t, :], src(t))
    link(ins)
    for t in range(n):
        ins = nc.vector.bn_aggr(M.mv[:, t, :], M.stats[:, t, :])
    ins.then_inc(var, 1)
    dve.wait_ge(std, count)
    link(nc.vector.reciprocal(M.rstd[:, 0:n], M.std[:, 0:n]))
    for t in range(n):
        ins = nc.vector.tensor_scalar(out(t), src(t), M.mv[:, t, 0:1], M.rstd[:, t:t + 1], ALU.subtract, ALU.mult)
    if done is None:
        link(ins)
    else:
        ins.then_inc(done, 1)


def ffn(nc, M):
    PS = M.PS
    NTI, NTP, NTO = N_IN // P, N_PROC // P, N_OUT // P
    ctx = ExitStack()

    def sem(name):
        return ctx.enter_context(nc.semaphore(f"ffn_{name}"))

    with ctx:
        sT = sem("sT")
        own = sem("own")
        rep = sem("rep")
        repT = sem("repT")
        repT_c = sem("repT_c")
        lin = sem("lin")
        lin_g = sem("lin_g")
        pmax = sem("pmax")
        pexp = sem("pexp")
        agg = sem("agg")
        agg_c = sem("agg_c")
        res = sem("res")
        res_c = sem("res_c")
        spreadb = sem("spread")
        var = sem("var")
        std = sem("std")
        xn = sem("xn")
        xnT = sem("xnT")
        xnT_c = sem("xnT_c")
        w_in = [sem(f"w_in{i}") for i in range(M.NSTAGE)]
        w_hi = sem("w_hi")
        w_sc = sem("w_sc")
        w_lo = sem("w_lo")
        l1_in = sem("l1_in")
        block = ctx.enter_context(nc.Block())

        NC = 2 * NX

        @block.sync
        def _(sp):
            M.load_l1(sp, l1_in)
            for c in range(NC):
                if c >= M.NSTAGE:
                    sp.wait_ge(w_lo, c - M.NSTAGE + 1)
                M.load_chunk(sp, c).then_inc(w_in[c % M.NSTAGE], 16)
            sp.wait_ge(l1_in, 16 * M.n_l1)

        @block.gpsimd
        def _(pool):
            nc.gpsimd.memset(M.wscale[:], WSCALE).then_inc(w_sc, 1)
            pool.wait_ge(w_sc, 1)
            for c in range(NC):
                pool.wait_ge(w_in[c % M.NSTAGE], 16 * (c // M.NSTAGE + 1))
                if c >= 2:
                    pool.wait_ge(w_lo, c - 1)
                nc.gpsimd.tensor_tensor(M.wtmp[:, c % 2, :], M.wst[:, c % M.NSTAGE, :],
                                        M.wscale[:].broadcast_to([P, 512]), ALU.mult).then_inc(w_sc, 1)
                pool.wait_ge(w_sc, c + 2)
                pool.wait_ge(w_hi, c + 1)
                hi, lo = (M.wh[:, c, :], M.wl[:, c, :])
                nc.gpsimd.tensor_tensor(lo, M.wtmp[:, c % 2, :], hi, ALU.subtract).then_inc(w_lo, 1)
            nc.gpsimd.memset(M.Ks[0:SROWS], 0.0)

        @block.tensor
        def _(pe):
            for n in range(NTI):
                mm = pe.transpose(PS[0:B, 4 + n // 4, (n % 4) * P:(n % 4 + 1) * P], M.actsum[:, n, :], M.ident[:])
            mm.then_inc(sT, 1)

            def turn(nt, count):
                pe.wait_ge(rep, count)
                for n in range(nt):
                    mm = pe.transpose(PS[:, 6, n * B:(n + 1) * B], M.rowb[:, n * P:(n + 1) * P], M.ident[0:B, 0:B])
                mm.then_inc(repT, 1)
                pe.wait_ge(repT_c, count)

            turn(NTI, 1)
            for n in range(NTI):
                mm = pe.matmul(PS[0:B, 0, :], M.colb[:, n * B:(n + 1) * B], M.piwT[:, n, :],
                               start=(n == 0), stop=(n == NTI - 1))
            mm.then_inc(lin, 1)
            turn(NTP, 2)
            for n in range(NTP):
                mm = pe.matmul(PS[0:D_PV, 7, 0:B], M.pv[:, n, :], M.colb[:, n * B:(n + 1) * B],
                               start=(n == 0), stop=(n == NTP - 1))
            mm.then_inc(agg, 1)
            pe.wait_ge(agg_c, 1)
            for n in range(2):
                mm = pe.matmul(PS[0:B, 1 + n, :], M.aggT[:], M.oiwT[0:D_PV, n * 512:(n + 1) * 512], start=True, stop=True)
            mm.then_inc(lin, 1)
            turn(NTO, 3)
            for n in range(NTO):
                mm = pe.matmul(PS[0:B, 3, 0:D], M.colb[:, n * B:(n + 1) * B], M.opat[:, n, :],
                               start=(n == 0), stop=(n == NTO - 1))
            mm.then_inc(res, 1)
            pe.wait_ge(res_c, 1)
            for b in range(B):
                mm = pe.matmul(PS[:, 7, b * D:(b + 1) * D], M.sel[:, b * P:(b + 1) * P], M.res[:], start=True, stop=True)
            mm.then_inc(spreadb, 1)
            for b in range(B):
                pe.wait_ge(xn, b + 1)
                if b >= 2:
                    pe.wait_ge(xnT_c, b - 1)
                for t in range(TPB):
                    mm = pe.transpose(PS[:, 4 + b % 2, t * P:(t + 1) * P], M.xn[b % 2][:, t, :], M.ident[:])
                mm.then_inc(xnT, 1)

        @block.scalar
        def _(act):
            def take_cols(nt, count):
                act.wait_ge(repT, count)
                nc.scalar.activation(M.colb[:, 0:nt * B], PS[:, 6, 0:nt * B], ACT.Copy).then_inc(repT_c, 1)

            for c in range(NC):
                act.wait_ge(w_in[c % M.NSTAGE], 16 * (c // M.NSTAGE + 1))
                nc.scalar.activation(M.wh[:, c, :], M.wst[:, c % M.NSTAGE, :], ACT.Copy, scale=WSCALE).then_inc(w_hi, 1)
            take_cols(NTI, 1)
            act.wait_ge(lin, 1)
            nc.scalar.activation(M.rowa[:, 0:N_PROC], PS[0:B, 0, :], ACT.Gelu).then_inc(lin_g, 1)
            act.wait_ge(pmax, 1)
            nc.scalar.activation(M.rowb[:, 0:N_PROC], M.rowa[:, 0:N_PROC], ACT.Exp, bias=M.tops[:, 8:9]).then_inc(pexp, 1)
            take_cols(NTP, 2)
            act.wait_ge(agg, 1)
            nc.scalar.activation(M.aggT[:], PS[0:D_PV, 7, 0:B], ACT.Copy).then_inc(agg_c, 1)
            act.wait_ge(lin, 2)
            nc.scalar.activation(M.rowa[:], PS[0:B, 1:3, :].rearrange("p a b -> p (a b)"), ACT.Gelu).then_inc(lin_g, 1)
            take_cols(NTO, 3)
            act.wait_ge(res, 1)
            nc.scalar.activation(M.res[:], PS[0:B, 3, 0:D], ACT.Copy).then_inc(res_c, 1)
            for i in range(2):
                act.wait_ge(var, i + 1)
                nc.scalar.activation(M.std[:], M.mv[:, :, 1], ACT.Sqrt, bias=M.eps[:, 0:1]).then_inc(std, 1)
            for b in range(B):
                act.wait_ge(xnT, b + 1)
                nc.scalar.activation(M.xT[:, b * S:(b + 1) * S], PS[:, 4 + b % 2, :], ACT.Identity,
                                     scale=M.gb1[:, 0:1], bias=M.gb1[:, 1:2]).then_inc(xnT_c, 1)

        @block.vector
        def _(dve):
            link = Links(dve, own)

            def take_top(n, k, first=None):
                for r in range(k // 8):
                    m8, src = M.tops[:, 0:8], M.rowc if r else M.rowa
                    link(nc.vector.max(m8, src[:, 0:n]))
                    if r == 0 and first is not None:
                        first()
                    link(nc.vector.match_replace(out=M.rowc[:, 0:n], in_to_replace=m8, in_values=src[:, 0:n],
                                                 imm_value=MSHIFT))

            dve.wait_ge(sT, 1)
            link(nc.vector.tensor_scalar(M.rowa[:], PS[0:B, 4:6, :].rearrange("p a b -> p (a b)"), 1.0 / S, None, ALU.mult))
            take_top(N_IN, K_IN)
            nc.vector.scalar_tensor_tensor(out=M.rowb[:], in0=M.rowc[:], scalar=MSHIFT, in1=M.rowa[:],
                                           op0=ALU.is_equal, op1=ALU.mult).then_inc(rep, 1)
            dve.wait_ge(lin_g, 1)
            def negate_max():
                nc.vector.tensor_scalar(M.tops[:, 8:9], M.tops[:, 0:1], -1.0, None, ALU.mult).then_inc(pmax, 1)

            take_top(N_PROC, K_PROC, negate_max)
            dve.wait_ge(pexp, 1)
            link(nc.vector.scalar_tensor_tensor(out=M.rowb[:, 0:N_PROC], in0=M.rowc[:, 0:N_PROC], scalar=MSHIFT,
                                                in1=M.rowb[:, 0:N_PROC], op0=ALU.is_equal, op1=ALU.mult))
            link(nc.vector.tensor_reduce(M.tops[:, 9:10], M.rowb[:, 0:N_PROC], AX.X, ALU.add))
            link(nc.vector.reciprocal(M.tops[:, 10:11], M.tops[:, 9:10]))
            nc.vector.tensor_scalar(M.rowb[:, 0:N_PROC], M.rowb[:, 0:N_PROC], M.tops[:, 10:11], None,
                                    ALU.mult).then_inc(rep, 1)
            dve.wait_ge(lin_g, 2)
            take_top(N_OUT, K_OUT)
            nc.vector.scalar_tensor_tensor(out=M.rowb[:], in0=M.rowc[:], scalar=MSHIFT, in1=M.rowa[:],
                                           op0=ALU.is_equal, op1=ALU.mult).then_inc(rep, 1)
            dve.wait_ge(spreadb, 1)

            def statistics():
                for t in range(NT):
                    ins = nc.vector.bn_stats(M.stats[:, t, :], M.x[:, t, :])
                link(ins)
                for t in range(NT):
                    ins = nc.vector.bn_aggr(M.mv[:, t, :], M.stats[:, t, :])
                ins.then_inc(var, 1)

            def scale(t, out):
                return nc.vector.tensor_scalar(out, M.x[:, t, :], M.mv[:, t, 0:1], M.rstd[:, t:t + 1],
                                               ALU.subtract, ALU.mult)

            for b in range(B):
                x = M.x[:, TPB * b:TPB * (b + 1), :]
                row = PS[:, 7, b * D:(b + 1) * D].rearrange("p (o d) -> p o d", o=1).broadcast_to([P, TPB, D])
                ins = nc.vector.tensor_tensor(x, x, row, ALU.add)
            link(ins)
            statistics()
            dve.wait_ge(std, 1)
            link(nc.vector.reciprocal(M.rstd[:], M.std[:]))
            for t in range(NT):
                ins = scale(t, M.x[:, t, :])
            link(ins)
            statistics()
            dve.wait_ge(std, 2)
            link(nc.vector.reciprocal(M.rstd[:], M.std[:]))
            for b in range(B):
                if b >= 2:
                    dve.wait_ge(xnT, b - 1)
                for t in range(TPB):
                    ins = scale(TPB * b + t, M.xn[b % 2][:, t, :])
                ins.then_inc(xn, 1)


def l1_output(nc, M):
    PS = M.PS
    ctx = ExitStack()

    def sem(name):
        return ctx.enter_context(nc.semaphore(f"out1_{name}"))

    with ctx:
        oT = sem("oT")
        cx = sem("cx")
        cxT = sem("cxT")
        cxT_c = sem("cxT_c")
        y = sem("y")
        y_added = sem("y_added")
        own = sem("own")
        var = sem("var")
        std = sem("std")
        x3 = sem("x3")
        x3T = sem("x3T")
        x3T_c = sem("x3T_c")
        x3T_h = sem("x3T_h")
        lo = sem("lo")
        logit = sem("logit")
        lexp = sem("lexp")
        lsub = sem("lsub")
        block = ctx.enter_context(nc.Block())

        @block.tensor
        def _(pe):
            def turn_o(t):
                if t >= 2:
                    pe.wait_ge(cx, t - 1)
                for g in range(4):
                    mm = pe.transpose(PS[:, t % 2, g * P:(g + 1) * P], M.o[:, g, t * P:(t + 1) * P], M.ident[:])
                mm.then_inc(oT, 1)

            def turn_cx(t):
                pe.wait_ge(cx, t + 1)
                if t >= 2:
                    pe.wait_ge(cxT_c, t - 1)
                pe.transpose(PS[:, 2 + t % 2, 0:P], M.cx[t % 2][:], M.ident[:]).then_inc(cxT, 1)

            def project(t):
                pe.wait_ge(cxT_c, t + 1)
                if t >= 2:
                    pe.wait_ge(y_added, t - 1)
                pe.matmul(PS[:, 4 + t % 2, 0:D], M.cxT[t % 2][:], M.Wo1[:], start=True, stop=True).then_inc(y, 1)

            def turn_x3(b):
                pe.wait_ge(x3, b + 1)
                if b >= 1:
                    pe.wait_ge(lo, b)
                for t in range(TPB):
                    mm = pe.transpose(PS[:, 6, t * P:(t + 1) * P], M.x[:, TPB * b + t, :], M.ident[:])
                mm.then_inc(x3T, 1)

            def route(b):
                pe.wait_ge(x3T_c, b + 1)
                for t in range(TPB * b, TPB * (b + 1)):
                    mm = pe.matmul(PS[:, 7, t * NE:(t + 1) * NE], M.xT[:, t * P:(t + 1) * P], M.rT[:], start=True, stop=True)
                mm.then_inc(logit, 1)

            turn_o(0)
            for t in range(NT + 1):
                if t + 1 < NT:
                    turn_o(t + 1)
                if t:
                    project(t - 1)
                if t < NT:
                    turn_cx(t)
                if t % TPB == 2 and t > TPB:
                    turn_x3(t // TPB - 1)
                if t % TPB == 3 and t > TPB:
                    route(t // TPB - 1)
            turn_x3(B - 1)
            route(B - 1)

        @block.scalar
        def _(act):
            def root(b):
                act.wait_ge(var, b + 1)
                nc.scalar.activation(M.std[:, 0:TPB], M.mv[:, 0:TPB, 1], ACT.Sqrt, bias=M.eps[:, 0:1]).then_inc(std, 1)

            def take_x3T(b):
                act.wait_ge(x3T, b + 1)
                nc.scalar.activation(M.xT[:, b * S:(b + 1) * S], PS[:, 6, :], ACT.Copy).then_inc(x3T_c, 1)
                nc.scalar.activation(M.xTh[:, b * S:(b + 1) * S], PS[:, 6, :], ACT.Copy).then_inc(x3T_h, 1)

            for t in range(NT):
                act.wait_ge(cxT, t + 1)
                if t >= 2:
                    act.wait_ge(y, t - 1)
                nc.scalar.activation(M.cxT[t % 2][:], PS[:, 2 + t % 2, 0:P], ACT.Copy).then_inc(cxT_c, 1)
                if t % TPB == 0 and t:
                    root(t // TPB - 1)
                if t % TPB == 2 and t > TPB:
                    take_x3T(t // TPB - 1)
            root(B - 1)
            take_x3T(B - 1)
            act.wait_ge(lsub, 1)
            nc.scalar.activation(M.rt[:, 0], M.rt[:, 0], ACT.Exp).then_inc(lexp, 1)

        @block.vector
        def _(dve):
            link = Links(dve, own)

            def take_lo(b):
                dve.wait_ge(x3T_h, b + 1)
                nc.vector.tensor_tensor(M.xTl[:, b * S:(b + 1) * S], PS[:, 6, :], M.xTh[:, b * S:(b + 1) * S],
                                        ALU.subtract).then_inc(lo, 1)

            def divide(t):
                dve.wait_ge(oT, t + 1)
                if t >= 2:
                    dve.wait_ge(cxT, t - 1)
                heads = PS[:, t % 2, :].rearrange("p (h e) -> p h e", e=32)
                link(nc.vector.reciprocal(M.rden[:, t % 2, :], heads[:, :, DH1]))
                nc.vector.tensor_tensor(M.cx[t % 2][:].rearrange("p (h e) -> p h e", e=DH1), heads[:, :, 0:DH1],
                                        spread(M.rden[:, t % 2, :], DH1), ALU.mult).then_inc(cx, 1)

            divide(0)
            for t in range(NT):
                if t + 1 < NT:
                    divide(t + 1)
                dve.wait_ge(y, t + 1)
                nc.vector.tensor_tensor(M.x[:, t, :], M.x[:, t, :], PS[:, 4 + t % 2, 0:D], ALU.add).then_inc(y_added, 1)
                if t % TPB == TPB - 1:
                    b = t // TPB
                    dve.wait_ge(y_added, t + 1)
                    layernorm(nc, dve, link, M, TPB * b, TPB, var, std, b + 1, done=x3)
                    if b:
                        take_lo(b - 1)
            take_lo(B - 1)
            dve.wait_ge(logit, B)
            lg = PS[:, 7, 0:NT * NE].rearrange("p (t e) -> p t e", e=NE)
            prob, one, two, three = M.rt[:, 0], M.rt1[:, 0], M.rt1[:, 1], M.rt1[:, 2]
            link(nc.vector.tensor_reduce(one, lg, AX.X, ALU.max))
            nc.vector.tensor_tensor(prob, lg, spread(one, NE), ALU.subtract).then_inc(lsub, 1)
            dve.wait_ge(lexp, 1)
            link(nc.vector.tensor_reduce(two, prob, AX.X, ALU.add))
            link(nc.vector.reciprocal(three, two))
            link(nc.vector.tensor_tensor(prob, prob, spread(three, NE), ALU.mult))
            other = prob.rearrange("p t (o e) -> p t o e", o=1).broadcast_to([P, NT, NE, NE])
            mine = prob.rearrange("p t (e o) -> p t e o", o=1).broadcast_to([P, NT, NE, NE])
            tri = M.tri[:].rearrange("p (o e j) -> p o e j", o=1, e=NE).broadcast_to([P, NT, NE, NE])
            nc.vector.tensor_tensor(M.gt[:], other, mine, ALU.is_gt)
            link(nc.vector.tensor_tensor(M.eq[:], other, mine, ALU.is_equal))
            link(nc.vector.tensor_tensor(M.eq[:], M.eq[:], tri, ALU.mult))
            link(nc.vector.tensor_tensor(M.gt[:], M.gt[:], M.eq[:], ALU.add))
            link(nc.vector.tensor_reduce(M.rt[:, 1], M.gt[:], AX.X, ALU.add))
            link(nc.vector.scalar_tensor_tensor(out=M.rt[:, 1], in0=M.rt[:, 1], scalar=1.5, in1=prob,
                                                op0=ALU.is_lt, op1=ALU.mult))
            link(nc.vector.tensor_reduce(one, M.rt[:, 1], AX.X, ALU.add))
            link(nc.vector.tensor_scalar(one, one, 1e-9, None, ALU.max))
            link(nc.vector.reciprocal(two, one))
            link(nc.vector.tensor_scalar(two, two, 1.0 / WSCALE, None, ALU.mult))
            link(nc.vector.memset(M.comb[:], 1.0 / WSCALE))
            link(nc.vector.tensor_tensor(M.comb[:, :, 0:NE], M.rt[:, 1], spread(two, NE), ALU.mult))


def moe(nc, M):
    PS = M.PS
    NF = FF // P
    U = NX * NF
    HB, OB = 4, 3
    Q = 4
    ctx = ExitStack()

    def sem(name):
        return ctx.enter_context(nc.semaphore(f"moe_{name}"))

    with ctx:
        h_ready = sem("h_ready")
        h_free = sem("h_free")
        sq_done = sem("sq_done")
        hi_done = sem("hi_done")
        lo_done = sem("lo_done")
        p_done = sem("p_done")
        o_free = sem("o_free")
        own = sem("own")
        var = sem("var")
        std = sem("std")
        carried = sem("carried")
        y_ready = sem("y_ready")
        y_out = [sem(f"y_out{i}") for i in range(2)]
        block = ctx.enter_context(nc.Block())

        @block.tensor
        def _(pe):
            pe.sem_inc(p_done, Q)

            def hidden(u, g):
                e, f = u // NF, u % NF
                pe.wait_ge(h_free, U * g + u + 1)
                cols = slice(e * FF + f * P, e * FF + (f + 1) * P)
                xh, xl = M.xTh[:, bass.ds(g * S, S)], M.xTl[:, bass.ds(g * S, S)]
                out = PS[:, u % HB, :]
                pe.matmul(out, M.fch[:, cols], xh, start=True, stop=False)
                pe.matmul(out, M.fch[:, cols], xl, start=False, stop=False)
                pe.matmul(out, M.fcl[:, cols], xh, start=False, stop=True).then_inc(h_ready, 1)

            def project(u, g):
                e, f = u // NF, u % NF
                if f == 0:
                    pe.wait_ge(o_free, NX * g + e + 1)
                pe.wait_ge(lo_done, Q + U * g + u + 1)
                hh, hl = M.hh[u % Q], M.hl[u % Q]
                for t in range(TPB):
                    out = PS[:, 4 + e % OB, t * D:(t + 1) * D]
                    cols = slice(t * P, (t + 1) * P)
                    w = (e * NF + f) * D
                    pe.matmul(out, hh[:, cols], M.prh[:, w:w + D], start=(f == 0 and t == 0), stop=False,
                              skip_group_check=True)
                    pe.matmul(out, hh[:, cols], M.prl[:, w:w + D], start=False, stop=False, skip_group_check=True)
                    mm = pe.matmul(out, hl[:, cols], M.prh[:, w:w + D], start=False, stop=(f == NF - 1 and t == TPB - 1),
                                   skip_group_check=True)
                mm.then_inc(p_done, 1)

            with pe.Fori(0, B // 2) as i:
                for u in range(HB - 1):
                    hidden(u, 2 * i)
                for n in range(2 * U):
                    ahead = n + HB - 1
                    if ahead < 2 * U:
                        hidden(ahead % U, 2 * i + ahead // U)
                    project(n % U, 2 * i + n // U)

        @block.scalar
        def _(act):
            act.sem_inc(h_free, HB)
            def root(g):
                act.wait_ge(var, g + 1)
                nc.scalar.activation(M.std[:, 0:TPB], M.mv[:, 0:TPB, 1], ACT.Sqrt, bias=M.eps[:, 0:1]).then_inc(std, 1)

            with act.Fori(0, B // 2) as i:
                for k in range(2 * U):
                    g, u = 2 * i + k // U, k % U
                    n = U * g + u
                    if k == U + 8:
                        root(g - 1)
                    act.wait_ge(h_ready, n + 1)
                    act.wait_ge(sq_done, n + 1)
                    nc.scalar.activation(M.r[u % Q][:], PS[:, u % HB, :], ACT.Relu, scale=1.0 / WSCALE).then_inc(h_free, 1)
                    act.wait_ge(h_free, HB + n + 1)
                    act.wait_ge(p_done, n + 1)
                    nc.scalar.activation(M.hh[u % Q][:], M.r[u % Q][:], ACT.Square).then_inc(hi_done, 1)
                root(2 * i + 1)

        @block.gpsimd
        def _(pool):
            pool.sem_inc(sq_done, Q)
            with pool.Fori(0, B // 2) as i:
                for u in range(2 * U):
                    n = 2 * U * i + u
                    pool.wait_ge(h_free, HB + n + 1)
                    pool.wait_ge(lo_done, n + 1)
                    nc.gpsimd.tensor_tensor(M.sq[u % Q][:], M.r[u % Q][:], M.r[u % Q][:], ALU.mult).then_inc(sq_done, 1)

        @block.vector
        def _(dve):
            dve.sem_inc(lo_done, Q)
            dve.sem_inc(o_free, OB)

            def combine(e, g, half):
                dve.wait_ge(p_done, Q + U * g + NF * (e + 1))
                dve.wait_ge(o_free, OB + NX * g + e)
                for t in range(TPB):
                    prev = (M.xg if e == 0 else M.acc)[half][:, t, :]
                    ins = nc.vector.scalar_tensor_tensor(out=M.acc[half][:, t, :], in0=PS[:, 4 + e % OB, t * D:(t + 1) * D],
                                                         scalar=M.cg[half][:, t, e:e + 1], in1=prev, op0=ALU.mult, op1=ALU.add)
                ins.then_inc(o_free, 1)

            def statistics(g, half):
                dve.wait_ge(o_free, OB + NX * (g + 1))
                if not half:
                    dve.wait_ge(y_ready, 1 + g)
                for t in range(TPB):
                    ins = nc.vector.bn_stats(M.stats[:, t, :], M.acc[half][:, t, :])
                ins.then_inc(own, 1)
                dve.wait_ge(own, 3 * (g - half) + 3 + 2 * half)
                dve.sem_inc(carried, 1)
                for t in range(TPB):
                    ins = nc.vector.bn_aggr(M.mv[:, t, :], M.stats[:, t, :])
                ins.then_inc(var, 1)

            def scale(g, half):
                dve.wait_ge(std, g + 1)
                nc.vector.reciprocal(M.rstd[:, 0:TPB], M.std[:, 0:TPB]).then_inc(own, 1)
                dve.wait_ge(own, 3 * (g - half) + 4 + 2 * half)
                dve.wait_ge(y_out[half], 1 + 8 * (g - half))
                for t in range(TPB):
                    ins = nc.vector.tensor_scalar(M.y[half][:, t, :], M.acc[half][:, t, :], M.mv[:, t, 0:1],
                                                  M.rstd[:, t:t + 1], ALU.subtract, ALU.mult)
                ins.then_inc(y_ready, 1)

            dve.sem_inc(y_ready, 1)
            with dve.Fori(0, B // 2) as i:
                for k in range(2 * U):
                    half, u = k // U, k % U
                    g = 2 * i + half
                    if u == 0:
                        nc.vector.tensor_copy(M.cg[half], M.comb[:, bass.ds(TPB * g, TPB), :])
                        nc.vector.tensor_copy(M.xg[half], M.x[:, bass.ds(TPB * g, TPB), :]).then_inc(own, 1)
                        dve.wait_ge(own, 3 * (g - half) + 1 + half)
                    n = U * g + u
                    dve.wait_ge(sq_done, Q + n + 1)
                    dve.wait_ge(hi_done, n + 1)
                    dve.wait_ge(p_done, n + 1)
                    nc.vector.tensor_tensor(M.hl[u % Q][:], M.sq[u % Q][:], M.hh[u % Q][:], ALU.subtract).then_inc(lo_done, 1)
                    if u % NF == 2 and u > NF:
                        combine(u // NF - 1, g, half)
                    if k == U + 2:
                        combine(NX - 1, g - 1, 0)
                    if k == U + 4:
                        statistics(g - 1, 0)
                    if k == U + 10:
                        scale(g - 1, 0)
                combine(NX - 1, 2 * i + 1, 1)
                statistics(2 * i + 1, 1)
                scale(2 * i + 1, 1)

        @block.sync
        def _(sp):
            for half in range(2):
                sp.sem_inc(y_out[half], 1)
            with sp.Fori(0, B // 2) as i:
                for half in range(2):
                    g = 2 * i + half
                    sp.wait_ge(y_ready, 1 + g + 1)
                    sp.dma_start(M.out_dram[bass.ds(g, 1)].rearrange("b (t p) d -> p (b t) d", p=P), M.y[half])\
                      .then_inc(y_out[half], 16)
            for half in range(2):
                sp.wait_ge(y_out[half], 1 + 16 * (B // 2))


class Memory:
    pass


def build(nc, I, out, debug=None):
    M = Memory()
    M.out_dram = out
    with ExitStack() as ctx:
        def sb(name, shape, dt=F32):
            return ctx.enter_context(nc.sbuf_tensor(name, shape, dt))

        def dram(name, shape, dt=F32):
            return nc.dram_tensor(name, shape, dt, kind="Internal").ap()

        M.PS = ctx.enter_context(nc.psum_tensor("PS", [P, 8, BANK], F32))
        M.sums_dram = dram("sums_scratch", [B, 8, 2, S])
        M.r_dram = dram("r_scratch", [B, 16 * S])
        M.qk0_dram = dram("qk0_scratch", [2, 4, 2 * P, S], F16)
        M.qk_dram = dram("qk_scratch", [4, P, S], F16)
        M.x_dram, M.xT_dram = I["x"], I["xT"]
        M.gamma0_dram, M.Wout_dram, M.blk_dram, M.spread_dram = I["gamma0"], I["Wout"], I["blk"], I["spread"]

        M.x = sb("x_tokens", [P, NT, D])
        M.xT = sb("x_transposed", [P, T])
        M.ident = sb("ident", [P, P])
        M.eps = sb("eps", [P, 1])
        M.stats = sb("stats", [P, NT, 6])
        M.mv = sb("mv", [P, NT, 2])
        M.std = sb("std", [P, NT])
        M.rstd = sb("rstd", [P, NT])
        M.xb = sb("xb", [P, S])
        M.Qs = sb("q_stack", [SROWS + 1, NQK, S], F16)
        M.Ks = sb("k_stack", [SROWS + 1, NQK, S], F16)
        M.Pr = sb("exp_ring", [P, PRING, S])
        M.qk = sb("qk_parts", [P, 2, 4, 2, S], F16)
        M.V = sb("V", [P, 4, 512])
        M.Vn = sb("V_next", [P, 4, 512])
        M.negm = sb("neg_max", [P, 2, 16])
        M.mrow = [sb(f"max_row{i}", [16, P], F16) for i in range(2)]
        M.ones = sb("ones", [P, 32])
        M.actsum = sb("actsum", [P, N_IN // P, B])

        M.ffn_in = ctx.enter_context(nc.semaphore("ffn_in"))
        M.piwT = M.qk[:].rearrange("p h a b c -> p (h a b c)").bitcast(F32).rearrange("p (n c) -> p n c", c=N_PROC)

        with ExitStack() as l0:
            def sb0(name, shape, dt=F32):
                return l0.enter_context(nc.sbuf_tensor(name, shape, dt))

            M.o = sb0("o0", [P, 2, H0 // 2, T])
            M.Wq = sb0("Wq", [P, 512])
            M.Wkv = sb0("Wkv", [P, 1024])
            M.sums = [sb0(f"sums{i}", [P, S]) for i in range(2)]

            M.esum = [sb0(f"exp_sums{i}", [P, 2, S]) for i in range(2)]
            M.csum, M.crec = sb0("csum", [P, 64]), sb0("crec", [P, 64])
            M.lam, M.lamp = sb0("lam", [P, 4, DH0]), sb0("lamp", [P, 2, DH0])
            M.lams, M.nlam, M.sign, M.gam0 = sb0("lams", [P, 8]), sb0("nlam", [P, 1]), sb0("sign", [P, 3]), sb0("gam0", [P, 1])
            M.rsum = [M.x[:].rearrange("p t d -> p (t d)").rearrange("p (h q) -> p h q", h=4),
                      M.xT[:].rearrange("p (h q) -> p h q", h=4)]

            def load_l0(sp, wq_sem, sem):
                sp.dma_start(M.Wq[:], I["Wq"]).then_inc(wq_sem, 16)
                pairs = [(M.Wkv, I["Wkv"]), (M.ident, I["ident"]), (M.eps, I["eps"])]
                for dst, src in pairs:
                    sp.dma_start(dst[:], src).then_inc(sem, 16)
                sp.dma_start(M.lam[:], I["lam"].rearrange("(o k) d -> o k d", o=1).broadcast_to([P, 4, DH0])).then_inc(sem, 16)
                sp.dma_start(M.sign[:, 1:3], I["half"]).then_inc(sem, 16)
            M.n_l0, M.load_weights = 5, load_l0
            attention(nc, M, AttnPlan(0))

            M.Wout = M.Wq[:].rearrange("p (h n) -> p h n", n=D)
            M.blk, M.spread = M.Wkv[:, 0:32], M.Wkv[:, 512:1024]
            M.yT = [M.xb, M.sums[0]]
            ring = M.Pr[:].rearrange("p a b -> p (a b)")
            M.sqb = [ring[:, 2048 * i:2048 * (i + 1)].rearrange("p (h q) -> p h q", h=4) for i in range(2)]
            M.rmsb = [ring[:, 4096 + 512 * i:4096 + 512 * (i + 1)] for i in range(2)]
            M.junk = [ring[:, 5120 + 512 * i:5120 + 512 * (i + 1)] for i in range(2)]
            vn, vv = (v[:].rearrange("p a b -> p (a b)") for v in (M.Vn, M.V))
            M.patT, M.oiwT = vn[:, 0:N_IN], vn[:, N_IN:2 * N_IN]
            M.opat = vv[:, 0:1024].rearrange("p (n d) -> p n d", d=D)
            M.pv = vv[:, 1024:1280].rearrange("p (n d) -> p n d", d=D_PV)
            M.sel, M.gb1 = vv[0:B, 1280:1280 + B * P], vv[:, 1792:1794]

            def load_ffn(sp):
                pairs = [(M.patT, I["patT"]), (M.piwT, I["piwT"].rearrange("(n p) c -> p n c", p=P)),
                         (M.oiwT[0:D_PV, :], I["oiwT"]), (M.opat, I["opat"].rearrange("(n p) c -> p n c", p=P)),
                         (M.pv, I["pv"].rearrange("(n p) c -> p n c", p=P)), (M.sel, I["sel"]), (M.gb1, I["gb1"])]
                for dst, src in pairs:
                    sp.dma_start(dst, src).then_inc(M.ffn_in, 16)
            M.load_ffn, M.n_ffn = load_ffn, 7
            l0_output(nc, M)

        if debug == "x1":
            return M
        with ExitStack() as l1:
            def sb1(name, shape, dt=F32):
                return l1.enter_context(nc.sbuf_tensor(name, shape, dt))
            M.wh, M.wl = sb1("w_high", [P, 2 * NX, FF], F16), sb1("w_low", [P, 2 * NX, FF], F16)
            M.Wo1 = sb1("Wo1", [P, D])
            M.rT = sb1("routerT", [P, NE])
            M.tri = sb1("tri", [P, NE * NE])
            M.comb = sb1("comb", [P, NT, NX])
            M.Win = sb1("Win", [P, 3 * D])
            M.WinR = sb1("WinR", [P, 2 * D])
            M.cos, M.sin = sb1("cos", [P, S]), sb1("sin", [P, S])
            M.bqk, M.bv, M.bo = sb1("bqk", [P, 4]), sb1("bv", [P, D]), sb1("bo", [P, D])
            with ExitStack() as fc:
                def sbf(name, shape, dt=F32):
                    return fc.enter_context(nc.sbuf_tensor(name, shape, dt))
                M.rowa, M.rowb, M.rowc = (sbf(f"row{c}", [B, 1024]) for c in "abc")
                M.colb = sbf("colb", [P, 8 * B])
                M.tops = sbf("tops", [B, 16])
                M.aggT = sbf("aggT", [D_PV, B])
                M.res = sbf("res", [B, D])
                M.xn = [sbf(f"xn{i}", [P, TPB, D]) for i in range(2)]
                M.NSTAGE = 10
                M.wst, M.wtmp = sbf("w_stage", [P, M.NSTAGE, FF]), sbf("w_scaled", [P, 2, FF])
                M.wscale = sbf("w_scale", [P, 1])

                def load_l1(sp, sem):
                    pairs = [(M.Win, I["Win"]), (M.WinR, I["WinR"]), (M.cos, I["cos"]), (M.sin, I["sin"]), (M.bqk, I["bqk"]),
                             (M.Wo1, I["Wo1"]), (M.rT, I["rT"]), (M.tri, I["tri"])]
                    for dst, src in pairs:
                        sp.dma_start(dst[:], src).then_inc(sem, 16)
                    for dst, src in [(M.bv, I["bv"]), (M.bo, I["bo"])]:
                        sp.dma_start(dst[:], src.broadcast_to([P, D])).then_inc(sem, 16)
                M.load_l1, M.n_l1 = load_l1, 10

                def load_chunk(sp, c):
                    e, dst = c % NX, M.wst[:, c % M.NSTAGE, :]
                    if c < NX:
                        return sp.dma_start(dst, I["fcT"][e] if e < NE else I["sfcT"])
                    w = I["prT"][e] if e < NE else I["sprT"]
                    return sp.dma_start(dst.rearrange("p (f d) -> p f d", d=D), w.rearrange("(f p) d -> p f d", p=P))
                M.load_chunk = load_chunk
                ffn(nc, M)
            if debug == "x2":
                return M
            with ExitStack() as l1a:
                def sba(name, shape, dt=F32):
                    return l1a.enter_context(nc.sbuf_tensor(name, shape, dt))
                M.o = sba("o1", [P, 4, T])
                with ExitStack() as at:
                    def sbt(name, shape, dt=F32):
                        return at.enter_context(nc.sbuf_tensor(name, shape, dt))
                    M.raw = sbt("raw", [P, 5, S])
                    attention(nc, M, AttnPlan(1))
                    if debug == "o1":
                        return M
                NW = NX * FF
                wh, wl = (w[:].rearrange("p c n -> p (c n)") for w in (M.wh, M.wl))
                M.fch, M.prh, M.fcl, M.prl = wh[:, 0:NW], wh[:, NW:2 * NW], wl[:, 0:NW], wl[:, NW:2 * NW]
                with ExitStack() as po:
                    def sbp(name, shape, dt=F32):
                        return po.enter_context(nc.sbuf_tensor(name, shape, dt))
                    M.rden = sbp("rden", [P, 2, 16])
                    M.cx = [sbp(f"cx{i}", [P, D]) for i in range(2)]
                    M.cxT = [sbp(f"cxT{i}", [P, P]) for i in range(2)]
                    M.rt, M.rt1 = sbp("rt", [P, 2, NT, NE]), sbp("rt1", [P, 3, NT])
                    vv = M.V[:].rearrange("p a b -> p (a b)")
                    M.gt = vv[:, 0:1024].rearrange("p (t e j) -> p t e j", e=NE, j=NE)
                    M.eq = vv[:, 1024:2048].rearrange("p (t e j) -> p t e j", e=NE, j=NE)
                    qkf = M.qk[:].rearrange("p h a b c -> p (h a b c)")
                    M.xTh, M.xTl = qkf[:, 0:T], qkf[:, T:2 * T]
                    l1_output(nc, M)
                    of = M.o[:].rearrange("p g t -> p (g t)")
                    oh = of.bitcast(F16)
                    M.r = [of[:, i * S:(i + 1) * S] for i in range(4)]
                    M.sq = [of[:, (4 + i) * S:(5 + i) * S] for i in range(4)]
                    M.hh = [oh[:, (16 + i) * S:(17 + i) * S] for i in range(4)]
                    M.hl = [oh[:, (20 + i) * S:(21 + i) * S] for i in range(4)]
                    vn, vv = (v[:].rearrange("p a b -> p (a b)") for v in (M.Vn, M.V))
                    halves = [vn, vv]
                    M.acc, M.xg, M.y = ([v[:, 512 * i:512 * (i + 1)].rearrange("p (t d) -> p t d", d=D) for v in halves]
                                        for i in range(3))
                    M.cg = [v[:, 1536:1536 + TPB * NX].rearrange("p (t e) -> p t e", e=NX) for v in halves]
                    if debug == "x3":
                        return M
                    moe(nc, M)
    return M


def kernel(**inputs):
    import concourse.bacc as bacc
    from concourse.bass_utils import run_bass_kernel_spmd

    def row(name):
        return np.asarray(inputs[name])

    def laid(a):
        return np.ascontiguousarray(a)

    x = row("L0_attn_x").reshape(T, D)
    Win = row("L1_attn_W_in")
    within = np.arange(DH1)
    within[:RD] = within[:RD].reshape(-1, 2)[:, ::-1].reshape(-1)
    swap = (np.arange(D).reshape(-1, DH1)[:, within]).reshape(-1)
    b_in = row("L1_attn_b_in")
    t = np.arange(S, dtype=np.float32)
    inv_freq = (np.float32(1.0) / np.power(np.float32(10000.0), np.arange(0, RD, 2, dtype=np.float32) / np.float32(RD)))
    freqs = np.repeat(t[:, None] * inv_freq[None, :].astype(np.float32), 2, axis=-1)
    cos = np.ones((DH1, S), np.float32)
    sin = np.zeros((DH1, S), np.float32)
    cos[:RD] = np.cos(freqs).T
    sin[:RD] = np.sin(freqs).T * np.where(np.arange(RD) % 2 == 0, -1.0, 1.0)[:, None]
    blk = np.zeros((P, 32), np.float32)
    blk[:DV0, 0] = 1.0 / DV0
    blk[DV0:, 1] = 1.0 / DV0
    sel = np.zeros((B, B * P), np.float32)
    for b in range(B):
        sel[b, b * P:(b + 1) * P] = 1.0
    half = np.stack([1.0 - np.arange(P) // 16 % 2, np.arange(P) // 16 % 2], axis=1).astype(np.float32)
    spread_rows = np.zeros((P, 4, 2, DV0), np.float32)
    for h in range(4):
        for j in range(2):
            spread_rows[32 * h + j, h, j] = 1.0
    spread_rows = spread_rows.reshape(P, 4 * P)

    def by_half(w):
        return laid(w.reshape(D, 4, 2, 2, DH0).transpose(0, 1, 3, 2, 4).reshape(D, 512))

    arrays = {
        "x": laid(x), "xT": laid(x.T),
        "Wq": by_half(row("L0_attn_Wq")),
        "Wkv": laid(np.concatenate([by_half(row("L0_attn_Wkv")[:, :512]), row("L0_attn_Wkv")[:, 512:]], axis=1)),
        "half": half, "spread": spread_rows,
         "Wout": row("L0_attn_Wout"),
        "lam": laid(np.stack([row(f"L0_attn_lambda_{n}") for n in ("q1", "k1", "q2", "k2")])),
        "gamma0": laid(np.tile(row("L0_attn_gamma"), 2)[:, None]),
        "patT": laid(row("L0_ffn_input_patterns").T), "piwT": laid(row("L0_ffn_process_input_weights").T),
        "pv": row("L0_ffn_process_values"), "oiwT": laid(row("L0_ffn_output_input_weights").T),
        "opat": row("L0_ffn_output_patterns"),
        "Win": Win, "WinR": laid(np.concatenate([Win[:, :D][:, swap], Win[:, D:2 * D][:, swap]], axis=1)),
        "bqk": laid(np.stack([b_in[:D], b_in[D:2 * D], b_in[:D][swap], b_in[D:2 * D][swap]], axis=1)),
        "bv": laid(b_in[None, 2 * D:]), "bo": laid(row("L1_attn_b_out")[None]),
        "Wo1": row("L1_attn_W_out"),
        "gb1": laid(np.stack([row("L1_attn_gamma"), row("L1_attn_beta")], axis=1)),
        "rT": laid(row("L1_ffn_router_w").T),
        "fcT": laid(row("L1_ffn_w_fc").transpose(0, 2, 1)), "prT": laid(row("L1_ffn_w_proj").transpose(0, 2, 1)),
        "sfcT": laid(row("L1_ffn_shared_fc").T), "sprT": laid(row("L1_ffn_shared_proj").T),
        "ident": np.eye(P, dtype=np.float32), "eps": np.full((P, 1), EPS_LN, np.float32), "blk": blk, "sel": sel,
        "cos": laid(np.tile(cos, (D // DH1, 1))), "sin": laid(np.tile(sin, (D // DH1, 1))),
        "tri": laid(np.tile(np.tril(np.ones((NE, NE), np.float32), -1).reshape(1, -1), (P, 1))),
    }
    nc = bacc.Bacc("TRN2", target_bir_lowering=False, num_devices=1)
    maps, I = {}, {}
    for name, a in arrays.items():
        a = np.ascontiguousarray(a)
        maps[f"in_{name}"] = a
        I[name] = nc.dram_tensor(f"in_{name}", a.shape, mybir.dt.from_np(a.dtype), kind="ExternalInput").ap()
    out = nc.dram_tensor("out_0", (B, S, D), F32, kind="ExternalOutput").ap()
    build(nc, I, out)
    result = run_bass_kernel_spmd(nc, [maps], core_ids=[0])
    return result.results[0]["out_0"]
```
